# Optimizing a Trainium2 kernel written in Bass

```python
import numpy as np
import jax
import jax.numpy as jnp

def _softmax(x, axis=-1):
    return jax.nn.softmax(x, axis=axis)

def _gelu(x):
    return jax.nn.gelu(x, approximate=True)

def _silu(x):
    return jax.nn.silu(x)

def _sigmoid(x):
    return jax.nn.sigmoid(x)

def _layernorm(x, axis=-1, eps=1e-05):
    m = jnp.mean(x, axis=axis, keepdims=True)
    v = jnp.var(x, axis=axis, keepdims=True)
    return (x - m) / jnp.sqrt(v + eps)

def _scatter_add(tgt, idx, src, axis=0):
    return tgt.at[idx].add(src)

def _segment_sum(src, seg, n):
    return jax.ops.segment_sum(src, seg, n)
kernel_name = 'mk_vit_tower_d2_tok_img1024_r4_d8ce14'

def setup_inputs(seed: int=0):
    np.random.seed(seed)
    _w = jnp.asarray

    def _rec_inputs():
        import jax
        import jax.numpy as jnp
        _rk = jax.random.key(seed)
        x = -0.00016672 + 0.999947 * jax.random.normal(jax.random.fold_in(_rk, 1), (16, 3, 96, 96), jnp.float32)
        return x
    x = _rec_inputs()

    def _L0_tok_setup():
        import jax, jax.numpy as jnp
        import numpy as np
        B, C, H, W = (64, 3, 96, 96)
        P = 16
        HP, WP = (H // P, W // P)
        N = HP * WP
        F = C * P * P
        D = 256
        key = jax.random.key(seed)
        k1, k2, k3, k4, k5 = jax.random.split(key, 5)
        data = jax.random.normal(k1, (B, C, H, W), dtype=jnp.float32)
        lim = 1.0 / np.sqrt(F)
        W_lin = jax.random.uniform(k2, (D, F), minval=-lim, maxval=lim, dtype=jnp.float32)
        b_lin = jax.random.uniform(k3, (D,), minval=-lim, maxval=lim, dtype=jnp.float32)
        class_token = jax.random.normal(k4, (1, 1, D), dtype=jnp.float32)
        position_embeddings = jax.random.normal(k5, (1, N + 1, D), dtype=jnp.float32)
        return {'data': data, 'W_lin': W_lin, 'b_lin': b_lin, 'class_token': class_token, 'position_embeddings': position_embeddings}
    _L0_tok_all = _L0_tok_setup()
    _L0_tok_in = {k: v for k, v in _L0_tok_all.items() if k in ('W_lin', 'b_lin', 'class_token', 'position_embeddings')}
    del _L0_tok_all

    def _L0_attn_setup():
        import jax, jax.numpy as jnp
        import numpy as np
        import math
        D_MODEL = 256
        N_HEADS = 16
        D_KV = 64
        INNER = N_HEADS * D_KV
        NUM_BUCKETS = 32
        MAX_DISTANCE = 128

        def _relative_position_bucket(relative_position, bidirectional=True, num_buckets=NUM_BUCKETS, max_distance=MAX_DISTANCE):
            relative_buckets = jnp.zeros_like(relative_position)
            if bidirectional:
                num_buckets //= 2
                relative_buckets = relative_buckets + (relative_position > 0).astype(jnp.int32) * num_buckets
                relative_position = jnp.abs(relative_position)
            else:
                relative_position = -jnp.minimum(relative_position, jnp.zeros_like(relative_position))
            max_exact = num_buckets // 2
            is_small = relative_position < max_exact
            rp_large = max_exact + (jnp.log(relative_position.astype(jnp.float32) / max_exact) / math.log(max_distance / max_exact) * (num_buckets - max_exact)).astype(jnp.int32)
            rp_large = jnp.minimum(rp_large, num_buckets - 1)
            return relative_buckets + jnp.where(is_small, relative_position, rp_large)

        def compute_bias(rel_bias_table, q_len, k_len):
            context = jnp.arange(q_len, dtype=jnp.int32)[:, None]
            memory = jnp.arange(k_len, dtype=jnp.int32)[None, :]
            buckets = _relative_position_bucket(memory - context, bidirectional=True)
            values = rel_bias_table[buckets]
            return jnp.transpose(values, (2, 0, 1))[None]
        key = jax.random.key(seed)
        ks = jax.random.split(key, 6)
        B, S = (2, 512)
        scale = 0.02
        return {'hidden_states': jax.random.normal(ks[0], (B, S, D_MODEL), jnp.float32), 'w_q': jax.random.normal(ks[1], (D_MODEL, INNER), jnp.float32) * scale, 'w_k': jax.random.normal(ks[2], (D_MODEL, INNER), jnp.float32) * scale, 'w_v': jax.random.normal(ks[3], (D_MODEL, INNER), jnp.float32) * scale, 'w_o': jax.random.normal(ks[4], (INNER, D_MODEL), jnp.float32) * scale, 'rel_bias_table': jax.random.normal(ks[5], (NUM_BUCKETS, N_HEADS), jnp.float32) * scale}
    _L0_attn_all = _L0_attn_setup()
    _L0_attn_in = {k: v for k, v in _L0_attn_all.items() if k in ('w_q', 'w_k', 'w_v', 'w_o', 'rel_bias_table')}
    del _L0_attn_all

    def _L0_ffn_setup():
        import jax, jax.numpy as jnp
        import numpy as np
        D_MODEL = 256
        HIDDEN = 1024
        NUM_ROUTED = 7
        TOP_K = 2

        def _swiglu(x_flat, wg, wu, wd):
            g = jnp.einsum('nd,edh->enh', x_flat, wg)
            u = jnp.einsum('nd,edh->enh', x_flat, wu)
            h = jax.nn.silu(g) * u
            return jnp.einsum('enh,ehd->end', h, wd)
        key = jax.random.key(seed)
        ks = jax.random.split(key, 8)
        s = 0.02
        return {'x': jax.random.normal(ks[0], (4, 512, D_MODEL), jnp.float32), 'router_w': jax.random.normal(ks[1], (NUM_ROUTED, D_MODEL), jnp.float32) * s, 'w_gate': jax.random.normal(ks[2], (NUM_ROUTED, D_MODEL, HIDDEN), jnp.float32) * s, 'w_up': jax.random.normal(ks[3], (NUM_ROUTED, D_MODEL, HIDDEN), jnp.float32) * s, 'w_down': jax.random.normal(ks[4], (NUM_ROUTED, HIDDEN, D_MODEL), jnp.float32) * s, 'sw_gate': jax.random.normal(ks[5], (1, D_MODEL, HIDDEN), jnp.float32) * s, 'sw_up': jax.random.normal(ks[6], (1, D_MODEL, HIDDEN), jnp.float32) * s, 'sw_down': jax.random.normal(ks[7], (1, HIDDEN, D_MODEL), jnp.float32) * s}
    _L0_ffn_all = _L0_ffn_setup()
    _L0_ffn_in = {k: v for k, v in _L0_ffn_all.items() if k in ('router_w', 'w_gate', 'w_up', 'w_down', 'sw_gate', 'sw_up', 'sw_down')}
    del _L0_ffn_all

    def _L1_attn_setup():
        import jax, jax.numpy as jnp
        import numpy as np
        B, T, D = (8, 1024, 256)
        key = jax.random.key(seed)
        k1, k2, k3, k4, k5 = jax.random.split(key, 5)
        s = 1.0 / np.sqrt(D)
        return {'seq': jax.random.normal(k1, (B, T, D), dtype=jnp.float32), 'W_delta': jax.random.uniform(k2, (D, D), jnp.float32, -s, s), 'b_delta': jax.random.uniform(k3, (D,), jnp.float32, -s, s), 'W_value': jax.random.uniform(k4, (D, D), jnp.float32, -s, s), 'b_value': jax.random.uniform(k5, (D,), jnp.float32, -s, s)}
    _L1_attn_all = _L1_attn_setup()
    _L1_attn_in = {k: v for k, v in _L1_attn_all.items() if k in ('W_delta', 'b_delta', 'W_value', 'b_value')}
    del _L1_attn_all

    def _L1_ffn_setup():
        import jax, jax.numpy as jnp
        import numpy as np
        DIM = 256

        def _reference_tuple_inner(x, W_r, W_k, W_v, mu_r, mu_k):
            B, T, C = x.shape
            x_prev = jnp.concatenate([jnp.zeros((B, 1, C), x.dtype), x[:, :-1, :]], axis=1)
            xr = mu_r * x + (1.0 - mu_r) * x_prev
            xk = mu_k * x + (1.0 - mu_k) * x_prev
            r = jax.nn.sigmoid(jnp.einsum('btc,dc->btd', xr, W_r))
            k = jnp.einsum('btc,dc->btd', xk, W_k)
            k_act = jnp.square(jax.nn.relu(k))
            out = r * jnp.einsum('btc,dc->btd', k_act, W_v)
            new_state = x[:, -1, :]
            return (out, new_state)
        key = jax.random.key(seed)
        ks = jax.random.split(key, 6)
        B, T, C = (8, 512, DIM)
        x = jax.random.normal(ks[0], (B, T, C), dtype=jnp.float32)
        s = 1.0 / np.sqrt(C)
        W_r = jax.random.uniform(ks[1], (C, C), jnp.float32, -s, s)
        W_k = jax.random.uniform(ks[2], (C, C), jnp.float32, -s, s)
        W_v = jax.random.uniform(ks[3], (C, C), jnp.float32, -s, s)
        mu_r = jax.random.uniform(ks[4], (C,), jnp.float32)
        mu_k = jax.random.uniform(ks[5], (C,), jnp.float32)
        return {'x': x, 'W_r': W_r, 'W_k': W_k, 'W_v': W_v, 'mu_r': mu_r, 'mu_k': mu_k}
    _L1_ffn_all = _L1_ffn_setup()
    _L1_ffn_in = {k: v for k, v in _L1_ffn_all.items() if k in ('W_r', 'W_k', 'W_v', 'mu_r', 'mu_k')}
    del _L1_ffn_all
    return {'x': x, 'L0_tok_W_lin': _L0_tok_in['W_lin'], 'L0_tok_b_lin': _L0_tok_in['b_lin'], 'L0_tok_class_token': _L0_tok_in['class_token'], 'L0_tok_position_embeddings': _L0_tok_in['position_embeddings'], 'L0_attn_w_q': _L0_attn_in['w_q'], 'L0_attn_w_k': _L0_attn_in['w_k'], 'L0_attn_w_v': _L0_attn_in['w_v'], 'L0_attn_w_o': _L0_attn_in['w_o'], 'L0_attn_rel_bias_table': _L0_attn_in['rel_bias_table'], 'L0_ffn_router_w': _L0_ffn_in['router_w'], 'L0_ffn_w_gate': _L0_ffn_in['w_gate'], 'L0_ffn_w_up': _L0_ffn_in['w_up'], 'L0_ffn_w_down': _L0_ffn_in['w_down'], 'L0_ffn_sw_gate': _L0_ffn_in['sw_gate'], 'L0_ffn_sw_up': _L0_ffn_in['sw_up'], 'L0_ffn_sw_down': _L0_ffn_in['sw_down'], 'L1_attn_W_delta': _L1_attn_in['W_delta'], 'L1_attn_b_delta': _L1_attn_in['b_delta'], 'L1_attn_W_value': _L1_attn_in['W_value'], 'L1_attn_b_value': _L1_attn_in['b_value'], 'L1_ffn_W_r': _L1_ffn_in['W_r'], 'L1_ffn_W_k': _L1_ffn_in['W_k'], 'L1_ffn_W_v': _L1_ffn_in['W_v'], 'L1_ffn_mu_r': _L1_ffn_in['mu_r'], 'L1_ffn_mu_k': _L1_ffn_in['mu_k']}

def reference(x, L0_tok_W_lin, L0_tok_b_lin, L0_tok_class_token, L0_tok_position_embeddings, L0_attn_w_q, L0_attn_w_k, L0_attn_w_v, L0_attn_w_o, L0_attn_rel_bias_table, L0_ffn_router_w, L0_ffn_w_gate, L0_ffn_w_up, L0_ffn_w_down, L0_ffn_sw_gate, L0_ffn_sw_up, L0_ffn_sw_down, L1_attn_W_delta, L1_attn_b_delta, L1_attn_W_value, L1_attn_b_value, L1_ffn_W_r, L1_ffn_W_k, L1_ffn_W_v, L1_ffn_mu_r, L1_ffn_mu_k):
    import jax
    import jax.numpy as jnp

    def _L0_tok_ref(data, W_lin, b_lin, class_token, position_embeddings):
        import jax, jax.numpy as jnp
        import numpy as np
        B, C, H, W = (64, 3, 96, 96)
        P = 16
        HP, WP = (H // P, W // P)
        N = HP * WP
        F = C * P * P
        D = 256
        b = data.shape[0]
        x = data.reshape(b, C, HP, P, WP, P)
        x = x.transpose(0, 2, 4, 1, 3, 5).reshape(b, N, F)
        x = jnp.einsum('bnf,df->bnd', x, W_lin) + b_lin
        cls = jnp.broadcast_to(class_token, (b, 1, D))
        out = jnp.concatenate([cls, x], axis=1) + position_embeddings
        return out

    def _L0_attn_ref(hidden_states, w_q, w_k, w_v, w_o, rel_bias_table):
        import jax, jax.numpy as jnp
        import numpy as np
        import math
        D_MODEL = 256
        N_HEADS = 16
        D_KV = 64
        INNER = N_HEADS * D_KV
        NUM_BUCKETS = 32
        MAX_DISTANCE = 128

        def _relative_position_bucket(relative_position, bidirectional=True, num_buckets=NUM_BUCKETS, max_distance=MAX_DISTANCE):
            relative_buckets = jnp.zeros_like(relative_position)
            if bidirectional:
                num_buckets //= 2
                relative_buckets = relative_buckets + (relative_position > 0).astype(jnp.int32) * num_buckets
                relative_position = jnp.abs(relative_position)
            else:
                relative_position = -jnp.minimum(relative_position, jnp.zeros_like(relative_position))
            max_exact = num_buckets // 2
            is_small = relative_position < max_exact
            rp_large = max_exact + (jnp.log(relative_position.astype(jnp.float32) / max_exact) / math.log(max_distance / max_exact) * (num_buckets - max_exact)).astype(jnp.int32)
            rp_large = jnp.minimum(rp_large, num_buckets - 1)
            return relative_buckets + jnp.where(is_small, relative_position, rp_large)

        def compute_bias(rel_bias_table, q_len, k_len):
            context = jnp.arange(q_len, dtype=jnp.int32)[:, None]
            memory = jnp.arange(k_len, dtype=jnp.int32)[None, :]
            buckets = _relative_position_bucket(memory - context, bidirectional=True)
            values = rel_bias_table[buckets]
            return jnp.transpose(values, (2, 0, 1))[None]
        B, S, _ = hidden_states.shape

        def shape(x):
            return jnp.transpose(x.reshape(B, S, N_HEADS, D_KV), (0, 2, 1, 3))
        q = shape(hidden_states @ w_q)
        k = shape(hidden_states @ w_k)
        v = shape(hidden_states @ w_v)
        scores = jnp.einsum('bhqd,bhkd->bhqk', q, k)
        position_bias = compute_bias(rel_bias_table, S, S)
        scores = scores + position_bias
        attn = jax.nn.softmax(scores.astype(jnp.float32), axis=-1).astype(scores.dtype)
        ctx = jnp.einsum('bhqk,bhkd->bhqd', attn, v)
        ctx = jnp.transpose(ctx, (0, 2, 1, 3)).reshape(B, S, INNER)
        return ctx @ w_o

    def _L0_ffn_ref(x, router_w, w_gate, w_up, w_down, sw_gate, sw_up, sw_down):
        import jax, jax.numpy as jnp
        import numpy as np
        D_MODEL = 256
        HIDDEN = 1024
        NUM_ROUTED = 7
        TOP_K = 2

        def _swiglu(x_flat, wg, wu, wd):
            g = jnp.einsum('nd,edh->enh', x_flat, wg)
            u = jnp.einsum('nd,edh->enh', x_flat, wu)
            h = jax.nn.silu(g) * u
            return jnp.einsum('enh,ehd->end', h, wd)
        orig_shape = x.shape
        x_flat = x.reshape(-1, orig_shape[-1])
        N = x_flat.shape[0]
        logits = x_flat @ router_w.T
        top_vals, top_idx = jax.lax.top_k(logits, TOP_K)
        top_w = jax.nn.softmax(top_vals, axis=-1)
        combine = jnp.sum(jax.nn.one_hot(top_idx, NUM_ROUTED, dtype=x.dtype) * top_w[..., None], axis=1)
        routed_out = _swiglu(x_flat, w_gate, w_up, w_down)
        mixed = jnp.einsum('end,ne->nd', routed_out, combine)
        shared_out = _swiglu(x_flat, sw_gate, sw_up, sw_down)
        mixed = mixed + jnp.mean(shared_out, axis=0)
        return mixed.reshape(orig_shape)

    def _L1_attn_ref(seq, W_delta, b_delta, W_value, b_value):
        import jax, jax.numpy as jnp
        import numpy as np
        B, T, D = (8, 1024, 256)
        delta = jax.nn.sigmoid(jnp.einsum('btd,ed->bte', seq, W_delta) + b_delta)
        value = jnp.einsum('btd,ed->bte', seq, W_value) + b_value

        def step(state, dv):
            d, v = dv
            state = (1.0 - d) * state + d * v
            return (state, state)
        init = jnp.zeros((seq.shape[0], seq.shape[-1]), dtype=seq.dtype)
        _, out = jax.lax.scan(step, init, (delta.transpose(1, 0, 2), value.transpose(1, 0, 2)))
        return out.transpose(1, 0, 2)

    def _L1_ffn_ref(x, W_r, W_k, W_v, mu_r, mu_k):
        import jax, jax.numpy as jnp
        import numpy as np
        DIM = 256

        def _reference_tuple_inner(x, W_r, W_k, W_v, mu_r, mu_k):
            B, T, C = x.shape
            x_prev = jnp.concatenate([jnp.zeros((B, 1, C), x.dtype), x[:, :-1, :]], axis=1)
            xr = mu_r * x + (1.0 - mu_r) * x_prev
            xk = mu_k * x + (1.0 - mu_k) * x_prev
            r = jax.nn.sigmoid(jnp.einsum('btc,dc->btd', xr, W_r))
            k = jnp.einsum('btc,dc->btd', xk, W_k)
            k_act = jnp.square(jax.nn.relu(k))
            out = r * jnp.einsum('btc,dc->btd', k_act, W_v)
            new_state = x[:, -1, :]
            return (out, new_state)
        return _reference_tuple_inner(x, W_r, W_k, W_v, mu_r, mu_k)[0]
    h = _L0_tok_ref(x, L0_tok_W_lin, L0_tok_b_lin, L0_tok_class_token, L0_tok_position_embeddings)
    h = h + _L0_attn_ref(_layernorm(h, axis=-1), L0_attn_w_q, L0_attn_w_k, L0_attn_w_v, L0_attn_w_o, L0_attn_rel_bias_table)
    h = h + _L0_ffn_ref(_layernorm(h, axis=-1), L0_ffn_router_w, L0_ffn_w_gate, L0_ffn_w_up, L0_ffn_w_down, L0_ffn_sw_gate, L0_ffn_sw_up, L0_ffn_sw_down)
    h = h + _L1_attn_ref(_layernorm(h, axis=-1), L1_attn_W_delta, L1_attn_b_delta, L1_attn_W_value, L1_attn_b_value)
    h = h + _L1_ffn_ref(_layernorm(h, axis=-1), L1_ffn_W_r, L1_ffn_W_k, L1_ffn_W_v, L1_ffn_mu_r, L1_ffn_mu_k)
    return h

_drawn_inputs = setup_inputs


def setup_inputs(seed=0):
    import zlib

    import numpy as np

    out = dict(_drawn_inputs(seed))
    spreads = {}
    factors = {'L0_tok_b_lin': 2.791,
     'L0_attn_rel_bias_table': 8.0,
     'L0_ffn_router_w': 3.177,
     'L0_ffn_w_gate': 2.759,
     'L0_ffn_w_up': 2.741,
     'L0_ffn_w_down': 2.724,
     'L1_attn_b_delta': 8.0,
     'L1_ffn_W_r': 3.937,
     'L1_ffn_mu_r': 8.0}
    for name, (base, spread) in spreads.items():
        noise = np.random.default_rng([zlib.crc32(name.encode()), seed]).standard_normal(out[name].shape)
        drawn = base * np.exp(spread * noise) if base else spread * noise
        out[name] = jnp.asarray(drawn.astype(out[name].dtype))
    for name, factor in factors.items():
        out[name] = (out[name] * factor).astype(out[name].dtype)
    return out
```

```python
import math
from contextlib import ExitStack

import numpy as np

import concourse.bass as bass
from concourse import mybir

F32 = mybir.dt.float32
F32R = mybir.dt.float32r
ACT = mybir.ActivationFunctionType
ALU = mybir.AluOpType
AX = mybir.AxisListType

P = 128
B = 16
PATCH = 16
GRID = 96 // PATCH
NP = GRID * GRID
T = NP + 1
N = B * T
D = 256
KD = D // P
FP = 3 * PATCH * PATCH
KF = FP // P
HEADS = 16
DH = 64
INNER = HEADS * DH
HP = INNER // P
HID = 1024
KH = HID // P
E = 7
NX = E + 1
C = 2
NC = N // C
BC = B // C
NPC = BC * NP
PAIRS = B // 2
PPC = PAIRS // C
NT = 640
TT = NT // P
T2 = 2 * T
SC = 2 * PPC * T2
MASK = -1e30
W1 = KD * HID
BUCKETS = 32
EPS = 1e-5

MC = [(0, 0), (1, 0), (0, 1), (1, 1)]

PB_POS, PB_CLS, PB_BLIN, PB_BD, PB_BV, PB_MUR, PB_MUK, PB_WR = 0, 74, 76, 78, 80, 82, 84, 86
PB = PB_WR + KD * E
CB_ID, CB_TRI, CB_OH = 0, P, P + E * E
CB = CB_OH + 100


def pat(a, off, *dims):
    return bass.AP(a.tensor, a.offset + off, [list(a.ap[0])] + [list(d) for d in dims])


def vit_tower(nc, patches, w_lin, par, const, table, w_q, w_k, w_v, w_o, w_gate, w_up, w_down, w_l1, out):
    ctx = ExitStack()
    with ctx:
        def sb(name, cols, dt=F32):
            return ctx.enter_context(nc.sbuf_tensor(name, [P, cols], dt))

        def sem(name):
            return ctx.enter_context(nc.semaphore(name))

        ws = sb("w_stage", 3 * W1)
        vreg = sb("v_region", PAIRS * INNER)
        hT = sb("hT", KD * N)
        xnf = sb("xn_f32", KD * NT)
        xc = sb("x_centred", KD * N)
        sq = sb("x_squared", KD * N)
        rstd = sb("rstd", N)
        eps = sb("eps", 1)
        qb = sb("q_buf", 2 * NT)
        kb = sb("k_buf", 2 * N)
        sreg = sb("s_region", 3072)
        ptb = sb("probs_T", 2 * 592)
        bias = sb("bias_pair", HEADS * T2)
        stat = sb("softmax_stats", 3 * 3 * 8)
        pb = sb("params", PB)
        cb = sb("consts", CB)
        tb = sb("bias_table", HEADS)
        ones = sb("ones_over_d", P)
        zero = sb("zeros", P)
        small = sb("small", 24)
        wh = sb("w_hi", 3 * W1, F32R)
        wl = sb("w_lo", 3 * W1, F32R)
        cr = sb("c_region", 2 * HP * N, F32R)
        xh = sb("xn_hi", KD * NT, F32R)
        xl = sb("xn_lo", KD * NT, F32R)
        ps = ctx.enter_context(nc.psum_tensor("ps", [P, 8, 512], F32))

        PW = KF * NPC * C
        patch_s = vreg[:, 0:PW]
        wlin_s = vreg[:, PW:PW + KF * D]
        patch_h, patch_l = cr[:, 0:PW], cr[:, PW:2 * PW]
        v_all = vreg[:, :]
        ctx_h, ctx_l = cr[:, 0:HP * N], cr[:, HP * N:2 * HP * N]
        HR = 4 * NC
        hid_h, hid_l = cr[:, 0:HR], cr[:, HR:2 * HR]
        L1W = 5 * KD * D
        l1_h, l1_l = cr[:, 2 * HR:2 * HR + L1W], cr[:, 2 * HR + L1W:2 * HR + 2 * L1W]
        xk_h, xk_l = cr[:, 0:KD * N], cr[:, KD * N:2 * KD * N]
        l1_s = vreg[:, 0:L1W]
        cbc = vreg[:, L1W:L1W + NX * N - 0] if L1W + NX * N <= PAIRS * INNER else None
        tmp = [vreg[:, k * KD * N:(k + 1) * KD * N] for k in range(6)]
        silu_b, prod_b, wprod_b = (sreg[:, k * 2 * NC:(k + 1) * 2 * NC] for k in range(3))
        route = sreg[:, 1800:3072]
        bias_q = ptb[:, 0:HEADS * T]
        cbe = ptb[:, 0:N]
        ident = cb[:, CB_ID:CB_ID + P]

        s = {n: sem(n) for n in (
            "d_par d_const d_table d_wlin d_l1 d_out "
            "const_set pad_set mask_set bias_mm bias_ev d_bias tok_hi tok_lo tok_mm cls_set h_ready "
            "ln_mean ln_xc ln_sq ln_var ln_std ln_rs ln_xn ln_hi ln_lo "
            "v_mm v_ev_act v_ev_dve q_mm k_mm q_ev k_ev sc_mm sc_ev maxed shifted expd summed recip normed "
            "pt_mm pt_ev ctx_mm ctx_hi ctx_lo wo_mm "
            "rt_mm rt_shift rt_exp dve_chain comb_set cb_mm cb_ev seeded gu_mm silu_ok gate_mul "
            "weighted cbe_set hid_hi hid_lo dn_mm moe_mm l1_hi l1_lo ra_mm ra_sig scan_chain "
            "mix_ok mixk_ok mix_hi mix_lo rk_mm r_sig k_relu k_sq k_hi k_lo vv_mm out_ok").split()}
        d_patch = [sem(f"d_patch{i}") for i in range(3)]
        d_w = [sem(f"d_w{i}") for i in range(3)]
        w_hi = [sem(f"w_hi{i}") for i in range(3)]
        w_lo = [sem(f"w_lo{i}") for i in range(3)]
        WBASE = (1, 1, 2)

        def bank(k, cols=512, off=0):
            return ps[:, k, off:off + cols]

        def chunk(a, c, width=N):
            return pat(a, c * NC, [width, KD], [1, NC])

        block = ctx.enter_context(nc.Block())

        @block.sync
        def _(sp):
            sp.dma_start(wlin_s, w_lin).then_inc(s["d_wlin"], 16)
            for i in range(3):
                n = PW // 3
                sp.dma_start(patch_s[:, i * n:(i + 1) * n], patches[:, i * n:(i + 1) * n]).then_inc(d_patch[i], 16)
            sp.dma_start(cb[:], const).then_inc(s["d_const"], 16)
            sp.dma_start(tb[0:BUCKETS, :], table).then_inc(s["d_table"], 16)
            sp.dma_start(pb[:], par).then_inc(s["d_par"], 16)

            def part(p):
                return ws[:, p * W1:(p + 1) * W1]

            def rows(w, k):
                return w.rearrange("(k p) n -> p k n", p=P)

            sp.dma_start(part(2).rearrange("p (k n) -> p k n", k=KD), rows(w_v, KD)).then_inc(d_w[2], 16)
            sp.dma_start(part(0).rearrange("p (k n) -> p k n", k=KD), rows(w_q, KD)).then_inc(d_w[0], 16)
            sp.dma_start(part(1).rearrange("p (k n) -> p k n", k=KD), rows(w_k, KD)).then_inc(d_w[1], 16)
            sp.wait_ge(s["bias_ev"], 2)
            sp.wait_ge(s["mask_set"], 1)
            for b2 in range(2):
                sp.dma_start(pat(bias[b2 * T:(b2 + 1) * T, :], b2 * T, [T2, HEADS], [1, T]),
                             bias_q[0:T, :].rearrange("p (h k) -> p h k", h=HEADS)).then_inc(s["d_bias"], 16)
            sp.wait_ge(w_lo[2], 1)
            sp.dma_start(part(2).rearrange("p (k n) -> p k n", k=HP), rows(w_o, HP)).then_inc(d_w[2], 16)
            with sp.Fori(0, NX) as e:
                for p, w in ((0, w_gate), (1, w_up), (2, w_down)):
                    k = KD if p < 2 else KH
                    sp.wait_ge(w_lo[p], e + WBASE[p])
                    sp.dma_start(part(p).rearrange("p (k n) -> p k n", k=k),
                                 w[bass.ds(e, 1)].rearrange("o (k p) n -> p (o k) n", p=P)).then_inc(d_w[p], 16)
                    if p == 2:
                        pass
            sp.wait_ge(s["out_ok"], 4)
            sp.dma_start(out.rearrange("(m p) n -> p m n", p=P),
                         tmp[5].rearrange("p (m n) -> p m n", m=KD)).then_inc(s["d_out"], 16)
            sp.wait_ge(s["d_out"], 16)

        @block.gpsimd
        def _(pool):
            g = nc.gpsimd
            g.memset(ones[:], 1.0 / D).then_inc(s["const_set"], 1)
            g.memset(zero[:], 0.0).then_inc(s["const_set"], 1)
            g.memset(eps[:], EPS).then_inc(s["const_set"], 1)
            for a in (xnf, xh, xl):
                g.memset(pat(a[:], N, [NT, KD], [1, NT - N]).bitcast(F32), 0.0).then_inc(s["pad_set"], 1)
            g.memset(bias[0:T2, :], MASK).then_inc(s["mask_set"], 1)
            for t in range(2 * HP):
                pool.wait_ge(s["recip"], t + 1)
                sc = pat(sreg[0:T2, :], (t % 3) * SC, [T2, 8], [1, T2])
                g.tensor_tensor(sc, sc, pat(stat[0:T2, :], (t % 3) * 24 + 16, [1, 8], [0, T2]),
                                ALU.mult).then_inc(s["normed"], 1)
            pool.wait_ge(s["d_l1"], 16)
            pool.wait_ge(s["wo_mm"], 4)
            for i in range(5):
                r = slice(i * KD * D, (i + 1) * KD * D)
                g.tensor_copy(l1_h[:, r], l1_s[:, r]).then_inc(s["l1_hi"], 1)
                pool.wait_ge(s["l1_hi"], i + 1)
                g.tensor_tensor(l1_l[:, r], l1_s[:, r], l1_h[:, r].bitcast(F32), ALU.subtract).then_inc(s["l1_lo"], 1)
            for i in range(2):
                g.memset(wprod_b[:, i * NC:(i + 1) * NC], 0.0).then_inc(s["weighted"], 1)
                g.memset(small[:, 16 + i:17 + i], 0.0).then_inc(s["hid_lo"], 1)
            pool.wait_ge(s["cb_ev"], 2 * NX)
            with pool.Fori(0, NX) as e:
                def weigh(u):
                    pool.wait_ge(s["gate_mul"], e * 16 + (u + 3))
                    pool.wait_ge(s["hid_lo"], e * 16 + (u + 1))
                    g.tensor_tensor(wprod_b[:, (u % 2) * NC:(u % 2 + 1) * NC],
                                    prod_b[:, (u % 2) * NC:(u % 2 + 1) * NC],
                                    cbe[:, (u // 8) * NC:(u // 8 + 1) * NC], ALU.mult).then_inc(s["weighted"], 1)

                def low(u):
                    pool.wait_ge(s["hid_hi"], e * 16 + (u + 1))
                    g.tensor_tensor(hid_l[:, (u % 4) * NC:(u % 4 + 1) * NC],
                                    wprod_b[:, (u % 2) * NC:(u % 2 + 1) * NC],
                                    hid_h[:, (u % 4) * NC:(u % 4 + 1) * NC].bitcast(F32),
                                    ALU.subtract).then_inc(s["hid_lo"], 1)
                g.tensor_copy(cbe, cbc[:, bass.ds(e * N, N)]).then_inc(s["cbe_set"], 1)
                pool.wait_ge(s["cbe_set"], e + 1)
                weigh(0)
                for u in range(1, 16):
                    weigh(u)
                    low(u - 1)
                low(15)

        @block.scalar
        def _(act):
            a = nc.scalar

            def w_high(p, n):
                a.activation(wh[:, p * W1:p * W1 + n], ws[:, p * W1:p * W1 + n], ACT.Copy).then_inc(w_hi[p], 1)

            act.wait_ge(s["d_wlin"], 16)
            a.activation(wh[:, 0:KF * D], wlin_s, ACT.Copy).then_inc(s["tok_hi"], 1)
            for i in range(3):
                n = PW // 3
                act.wait_ge(d_patch[i], 16)
                a.activation(patch_h[:, i * n:(i + 1) * n], patch_s[:, i * n:(i + 1) * n],
                             ACT.Copy).then_inc(s["tok_hi"], 1)
            act.wait_ge(d_w[2], 16)
            w_high(2, W1)

            def norm(L, dst, width, dst_hi=True):
                for c in range(C):
                    act.wait_ge(s["ln_xc"], 2 * L + c + 1)
                    a.activation(chunk(sq[:], c), chunk(xc[:], c), ACT.Square).then_inc(s["ln_sq"], 1)
                for c in range(C):
                    act.wait_ge(s["ln_var"], 2 * L + c + 1)
                    a.activation(rstd[:, c * NC:(c + 1) * NC], bank(2 + c, NC), ACT.Sqrt,
                                 bias=eps[:, 0:1]).then_inc(s["ln_std"], 1)
                if dst_hi:
                    for c in range(C):
                        act.wait_ge(s["ln_xn"], 2 * L + c + 1)
                        a.activation(chunk(xh[:], c, NT), chunk(dst, c, NT), ACT.Copy).then_inc(s["ln_hi"], 1)

            act.wait_ge(s["const_set"], 3)
            act.wait_ge(s["pad_set"], 3)
            norm(0, xnf[:], NT)
            for i in range(0, 2 * PAIRS, 2):
                act.wait_ge(s["v_mm"], i + 1)
                a.activation(v_all[0:T2, i * 512:(i + 1) * 512], ps[0:T2, i % 4, :], ACT.Copy).then_inc(s["v_ev_act"], 1)
                if i in (0, 2):
                    act.wait_ge(d_w[i // 2], 16)
                    act.wait_ge(s["tok_mm"], 4)
                    w_high(i // 2, W1)
            act.wait_ge(d_w[2], 32)
            act.wait_ge(s["v_mm"], 2 * PAIRS)
            w_high(2, W1)

            def q_evac(n):
                hp, c = n // 2, n % 2
                act.wait_ge(s["q_mm"], n + 1)
                if hp >= 2:
                    act.wait_ge(s["sc_mm"], 2 * hp - 2)
                a.activation(qb[:, (hp % 2) * NT + c * NC:(hp % 2) * NT + (c + 1) * NC], bank(6, NC),
                             ACT.Copy).then_inc(s["q_ev"], 1)

            q_evac(0)
            q_evac(1)
            for t in range(2 * HP + 2):
                if t + 2 < 2 * HP:
                    q_evac(t + 2)
                if t < 2 * HP:
                    act.wait_ge(s["shifted"], t + 1)
                    sc = sreg[0:T2, (t % 3) * SC:(t % 3 + 1) * SC]
                    a.activation(sc, sc, ACT.Exp).then_inc(s["expd"], 1)
                if t >= 2:
                    v = t - 2
                    act.wait_ge(s["pt_mm"], v + 1)
                    if v >= 2:
                        act.wait_ge(s["ctx_mm"], v - 1)
                    a.activation(pat(ptb[0:T2, :], (v % 2) * SC, [SC // 2, 2], [1, SC // 2]),
                                 pat(ps[0:T2, 2, :], 0, [512, 2], [1, SC // 2]), ACT.Copy).then_inc(s["pt_ev"], 1)
                    act.wait_ge(s["ctx_mm"], v + 1)
                    hp, c = v // 2, v % 2
                    a.activation(ctx_h[:, hp * N + c * NC:hp * N + (c + 1) * NC], bank(4 + v % 2, NC),
                                 ACT.Copy).then_inc(s["ctx_hi"], 1)
            act.dma_start(l1_s, w_l1).then_inc(s["d_l1"], 16)
            norm(1, xnf[:], NT)
            act.wait_ge(s["rt_shift"], 1)
            a.activation(route[:, 80:115], route[:, 80:115], ACT.Exp).then_inc(s["rt_exp"], 1)
            with act.Fori(0, NX) as e:
                for p in range(3):
                    act.wait_ge(d_w[p], e * 16 + 16 * (WBASE[p] + 1))
                    if p < 2:
                        act.wait_ge(s["gate_mul"], e * 16 + 2)
                    else:
                        act.wait_ge(s["dn_mm"], e * 16 + 4)
                    w_high(p, W1)

                def silu(u):
                    act.wait_ge(s["gu_mm"], e * 16 + (u + 1))
                    act.wait_ge(s["gate_mul"], e * 16 + (u + 1))
                    a.activation(silu_b[:, (u % 2) * NC:(u % 2 + 1) * NC], bank(2 * (u % 2), NC),
                                 ACT.Silu).then_inc(s["silu_ok"], 1)

                def high(u):
                    act.wait_ge(s["weighted"], e * 16 + (u + 3))
                    act.wait_ge(s["dn_mm"], e * 16 + (u + 1))
                    a.activation(hid_h[:, (u % 4) * NC:(u % 4 + 1) * NC], wprod_b[:, (u % 2) * NC:(u % 2 + 1) * NC],
                                 ACT.Copy).then_inc(s["hid_hi"], 1)
                silu(0)
                for u in range(1, 16):
                    silu(u)
                    high(u - 1)
                high(15)
            norm(2, xnf[:], NT)
            for i, (m, c) in enumerate(MC):
                act.wait_ge(s["ra_mm"], 2 * i + 1)
                a.activation(tmp[0][:, m * N + c * NC:m * N + (c + 1) * NC], bank(4 + i, NC), ACT.Sigmoid,
                             bias=pb[:, PB_BD + m:PB_BD + m + 1]).then_inc(s["ra_sig"], 1)
            norm(3, xnf[:], NT, dst_hi=False)
            act.wait_ge(s["mix_ok"], 4)
            for k in range(2):
                dst = (xh[:, 0:KD * N], xk_h)[k]
                for c in range(C):
                    a.activation(chunk(dst, c), chunk(tmp[2 + k], c), ACT.Copy).then_inc(s["mix_hi"], 1)
            for i, (m, c) in enumerate(MC):
                r = slice(m * N + c * NC, m * N + (c + 1) * NC)
                act.wait_ge(s["rk_mm"], 2 * i + 1)
                a.activation(tmp[0][:, r], bank(4 + i, NC), ACT.Sigmoid).then_inc(s["r_sig"], 1)
                act.wait_ge(s["rk_mm"], 2 * i + 2)
                a.activation(tmp[1][:, r], bank(i, NC), ACT.Relu).then_inc(s["k_relu"], 1)
            act.wait_ge(s["rk_mm"], 8)
            for c in range(C):
                act.wait_ge(s["k_sq"], c + 1)
                a.activation(chunk(xh[:], c), chunk(tmp[4], c), ACT.Copy).then_inc(s["k_hi"], 1)

        @block.vector
        def _(dve):
            v = nc.vector
            chain = [0]

            def link(ins):
                chain[0] += 1
                ins.then_inc(s["dve_chain"], 1)
                dve.wait_ge(s["dve_chain"], chain[0])

            def sub(o, x, hi):
                return v.tensor_tensor(o, x, hi.bitcast(F32), ALU.subtract)

            def w_low(p, n):
                return sub(wl[:, p * W1:p * W1 + n], ws[:, p * W1:p * W1 + n],
                           wh[:, p * W1:p * W1 + n]).then_inc(w_lo[p], 1)

            dve.wait_ge(s["tok_hi"], 1)
            sub(wl[:, 0:KF * D], wlin_s, wh[:, 0:KF * D]).then_inc(s["tok_lo"], 1)
            for i in range(3):
                n = PW // 3
                dve.wait_ge(s["tok_hi"], i + 2)
                r = slice(i * n, (i + 1) * n)
                sub(patch_l[:, r], patch_s[:, r], patch_h[:, r]).then_inc(s["tok_lo"], 1)
            dve.wait_ge(s["bias_mm"], 1)
            v.tensor_copy(pat(bias_q[0:T, :], 0, [T, HEADS], [1, 32]),
                          pat(ps[0:T, 0, :], 0, [1, HEADS], [HEADS, 32])).then_inc(s["bias_ev"], 1)
            v.tensor_copy(pat(bias_q[0:T, :], 32, [T, HEADS], [1, T - 32]),
                          pat(ps[0:T, 1, :], 0, [1, HEADS], [HEADS, T - 32])).then_inc(s["bias_ev"], 1)
            dve.wait_ge(w_hi[2], 1)
            w_low(2, W1)
            dve.wait_ge(s["d_par"], 16)
            link(v.tensor_tensor(small[:, 0:KD], pb[:, PB_CLS:PB_CLS + KD],
                                 pat(pb[:], PB_POS, [T, KD]), ALU.add))
            v.tensor_copy(pat(hT[:], 0, [N, KD], [T, B]),
                          pat(small[:], 0, [1, KD], [0, B])).then_inc(s["cls_set"], 1)
            for i, (m, c) in enumerate(MC):
                dve.wait_ge(s["tok_mm"], i + 1)
                v.scalar_tensor_tensor(out=pat(hT[:], m * N + c * NC + 1, [T, BC], [1, NP]),
                                       in0=bank(4 + i, NPC).rearrange("p (b n) -> p b n", b=BC),
                                       scalar=pb[:, PB_BLIN + m:PB_BLIN + m + 1],
                                       in1=pat(pb[:], PB_POS + m * T + 1, [0, BC], [1, NP]),
                                       op0=ALU.add, op1=ALU.add).then_inc(s["h_ready"], 1)

            def norm(L, dst, lo=True):
                for c in range(C):
                    dve.wait_ge(s["ln_mean"], 2 * L + c + 1)
                    v.tensor_tensor(chunk(xc[:], c), chunk(hT[:], c), pat(bank(c), 0, [0, KD], [1, NC]),
                                    ALU.subtract).then_inc(s["ln_xc"], 1)
                for c in range(C):
                    dve.wait_ge(s["ln_std"], 2 * L + c + 1)
                    r = rstd[:, c * NC:(c + 1) * NC]
                    v.reciprocal(r, r).then_inc(s["ln_rs"], 1)
                    dve.wait_ge(s["ln_rs"], 2 * L + c + 1)
                    for o, i_, r_ in dst(c):
                        v.tensor_tensor(o, i_, r_, ALU.mult).then_inc(s["ln_xn"], 1)
                if lo:
                    for c in range(C):
                        dve.wait_ge(s["ln_hi"], 2 * L + c + 1)
                        sub(chunk(xl[:], c, NT), chunk(xnf[:], c, NT), chunk(xh[:], c, NT)).then_inc(s["ln_lo"], 1)

            def plain(c):
                return [(chunk(xnf[:], c, NT), chunk(xc[:], c), pat(rstd[:], c * NC, [0, KD], [1, NC]))]

            norm(0, plain)
            for i in range(1, 2 * PAIRS, 2):
                dve.wait_ge(s["v_mm"], i + 1)
                v.tensor_copy(v_all[0:T2, i * 512:(i + 1) * 512], ps[0:T2, i % 4, :]).then_inc(s["v_ev_dve"], 1)
                if i in (3, 5):
                    p = (i - 3) // 2
                    dve.wait_ge(w_hi[p], 1)
                    w_low(p, W1)
            dve.wait_ge(w_hi[2], 2)
            w_low(2, W1)

            def k_evac(n):
                hp, c = n // 2, n % 2
                dve.wait_ge(s["k_mm"], n + 1)
                if hp >= 2:
                    dve.wait_ge(s["sc_mm"], 2 * hp - 2)
                v.tensor_copy(kb[:, (hp % 2) * N + c * NC:(hp % 2) * N + (c + 1) * NC],
                              bank(7, NC)).then_inc(s["k_ev"], 1)

            k_evac(0)
            k_evac(1)
            dve.wait_ge(s["d_bias"], 32)
            for t in range(2 * HP + 2):
                if t < 2 * HP:
                    hp = t // 2
                    sc = sreg[0:T2, (t % 3) * SC:(t % 3 + 1) * SC]
                    sg = sc.rearrange("p (g k) -> p g k", g=8)
                    mx, sm, rc = (stat[0:T2, (t % 3) * 24 + 8 * k:(t % 3) * 24 + 8 * k + 8] for k in range(3))
                    dve.wait_ge(s["sc_mm"], t + 1)
                    if t >= 3:
                        dve.wait_ge(s["pt_mm"], t - 2)
                    v.tensor_tensor(pat(sc, 0, [PPC * T2, 2], [T2, PPC], [1, T2]),
                                    pat(ps[0:T2, 0, :], 0, [512, 2], [T2, PPC], [1, T2]),
                                    pat(bias[0:T2, :], 2 * hp * T2, [T2, 2], [0, PPC], [1, T2]),
                                    ALU.add).then_inc(s["sc_ev"], 1)
                    dve.wait_ge(s["sc_ev"], t + 1)
                    v.tensor_reduce(mx, sg, AX.X, ALU.max).then_inc(s["maxed"], 1)
                    dve.wait_ge(s["maxed"], t + 1)
                    v.tensor_tensor(sg, sg, pat(mx, 0, [1, 8], [0, T2]), ALU.subtract).then_inc(s["shifted"], 1)
                if t + 2 < 2 * HP:
                    k_evac(t + 2)
                if t < 2 * HP:
                    dve.wait_ge(s["expd"], t + 1)
                    v.tensor_reduce(sm, sg, AX.X, ALU.add).then_inc(s["summed"], 1)
                    dve.wait_ge(s["summed"], t + 1)
                    v.reciprocal(rc, sm).then_inc(s["recip"], 1)
                if t >= 2:
                    u = t - 2
                    hp, c = u // 2, u % 2
                    r = slice(hp * N + c * NC, hp * N + (c + 1) * NC)
                    dve.wait_ge(s["ctx_hi"], u + 1)
                    sub(ctx_l[:, r], bank(4 + u % 2, NC), ctx_h[:, r]).then_inc(s["ctx_lo"], 1)
            for i, (m, c) in enumerate(MC):
                r = slice(m * N + c * NC, m * N + (c + 1) * NC)
                dve.wait_ge(s["wo_mm"], i + 1)
                v.tensor_tensor(hT[:, r], hT[:, r], bank(4 + i, NC), ALU.add).then_inc(s["h_ready"], 1)
            norm(1, plain)
            lg, gt, eq = route[:, 0:40], route[:, 120:365], route[:, 365:610]
            rank, selm, mx5, sm5 = route[:, 610:645], route[:, 645:680], route[:, 680:685], route[:, 685:690]
            ex, comb = route[:, 80:115], route[:, 690:730]
            jj = ([8, TT], [0, E], [1, E])
            ee = ([8, TT], [1, E], [0, E])
            three = ([49, TT], [E, E], [1, E])
            dve.wait_ge(s["rt_mm"], 1)
            dve.wait_ge(s["d_const"], 16)
            link(v.tensor_copy(lg, bank(0, 40)))
            link(v.tensor_tensor(pat(gt, 0, *three), pat(lg, 0, *jj), pat(lg, 0, *ee), ALU.is_gt))
            link(v.tensor_tensor(pat(eq, 0, *three), pat(lg, 0, *jj), pat(lg, 0, *ee), ALU.is_equal))
            link(v.tensor_tensor(pat(eq, 0, *three), pat(eq, 0, *three),
                                 pat(cb[:], CB_TRI, [0, TT], [E, E], [1, E]), ALU.mult))
            link(v.tensor_tensor(gt, gt, eq, ALU.add))
            link(v.tensor_reduce(rank, pat(gt, 0, [E, TT * E], [1, E]), AX.X, ALU.add))
            link(v.tensor_scalar(selm, rank, 1.5, None, ALU.is_lt))
            link(v.tensor_reduce(mx5, pat(lg, 0, [8, TT], [1, E]), AX.X, ALU.max))
            v.tensor_tensor(pat(ex, 0, [E, TT], [1, E]), pat(lg, 0, [8, TT], [1, E]),
                            pat(mx5, 0, [1, TT], [0, E]), ALU.subtract).then_inc(s["rt_shift"], 1)
            dve.wait_ge(s["rt_exp"], 1)
            link(v.tensor_tensor(ex, ex, selm, ALU.mult))
            link(v.tensor_reduce(sm5, pat(ex, 0, [E, TT], [1, E]), AX.X, ALU.add))
            link(v.reciprocal(sm5, sm5))
            v.memset(pat(comb, E, [8, TT]), 1.0).then_inc(s["comb_set"], 1)
            v.tensor_tensor(pat(comb, 0, [8, TT], [1, E]), pat(ex, 0, [E, TT], [1, E]),
                            pat(sm5, 0, [1, TT], [0, E]), ALU.mult).then_inc(s["comb_set"], 1)
            dve.wait_ge(s["l1_lo"], 0 + 5)
            for e in range(NX):
                dve.wait_ge(s["cb_mm"], e + 1)
                b = 2 * (e % 2)
                v.tensor_copy(cbc[:, e * N:e * N + 512], bank(b)).then_inc(s["cb_ev"], 1)
                w2 = v.tensor_copy(cbc[:, e * N + 512:(e + 1) * N], bank(b + 1, N - 512))
                w2.then_inc(s["cb_ev"], 1)
            dve.wait_ge(s["cb_ev"], 2 * NX)
            for i in range(2):
                v.memset(prod_b[:, i * NC:(i + 1) * NC], 0.0).then_inc(s["gate_mul"], 1)
            with dve.Fori(0, NX) as e:
                for p in range(3):
                    dve.wait_ge(w_hi[p], e + WBASE[p] + 1)
                    w_low(p, W1)
                for u in range(16):
                    dve.wait_ge(s["silu_ok"], e * 16 + (u + 1))
                    dve.wait_ge(s["weighted"], e * 16 + (u + 1))
                    r = slice((u % 2) * NC, (u % 2 + 1) * NC)
                    v.tensor_tensor(prod_b[:, r], silu_b[:, r], bank(2 * (u % 2) + 1, NC),
                                    ALU.mult).then_inc(s["gate_mul"], 1)
            for i, (m, c) in enumerate(MC):
                dve.wait_ge(s["moe_mm"], i + 1)
                v.tensor_copy(hT[:, m * N + c * NC:m * N + (c + 1) * NC], bank(4 + i, NC)).then_inc(s["h_ready"], 1)
            norm(2, plain)
            for i, (m, c) in enumerate(MC):
                r = slice(m * N + c * NC, m * N + (c + 1) * NC)
                dve.wait_ge(s["ra_sig"], i + 1)
                dve.wait_ge(s["ra_mm"], 2 * i + 2)
                v.scalar_tensor_tensor(out=tmp[1][:, r], in0=bank(i, NC), scalar=pb[:, PB_BV + m:PB_BV + m + 1],
                                       in1=tmp[0][:, r], op0=ALU.add, op1=ALU.mult).then_inc(s["scan_chain"], 1)
                dve.wait_ge(s["scan_chain"], i + 1)
            link(v.tensor_scalar(tmp[2], tmp[0], -1.0, 1.0, ALU.mult, ALU.add))
            link(v.memset(pat(tmp[2], 0, [T, KD * B]), 0.0))
            for m in range(KD):
                r = slice(m * N, (m + 1) * N)
                link(v.tensor_tensor_scan(tmp[3][:, r], tmp[2][:, r], tmp[1][:, r], 0.0, ALU.mult, ALU.add))
            for i, (m, c) in enumerate(MC):
                r = slice(m * N + c * NC, m * N + (c + 1) * NC)
                v.tensor_tensor(hT[:, r], hT[:, r], tmp[3][:, r], ALU.add).then_inc(s["h_ready"], 1)

            XW = B * (T + 1)
            link(v.memset(pat(xnf[:], 0, [T + 1, KD * B]), 0.0))

            def spread(c):
                return [(pat(xnf[:], m * XW + c * BC * (T + 1) + 1, [T + 1, BC], [1, T]),
                         pat(xc[:], m * N + c * NC, [T, BC], [1, T]),
                         pat(rstd[:], c * NC, [T, BC], [1, T])) for m in range(KD)]

            norm(3, spread, lo=False)
            link(v.tensor_scalar(small[:, 4:8], pb[:, PB_MUR:PB_MUR + 4], -1.0, 1.0, ALU.mult, ALU.add))
            dve.wait_ge(s["ln_xn"], 10)
            for k in range(2):
                for m in range(KD):
                    x_t = pat(xnf[:], m * XW + 1, [T + 1, B], [1, T])
                    x_p = pat(xnf[:], m * XW, [T + 1, B], [1, T])
                    j = 2 * k + m
                    o1 = pat(tmp[4], m * N, [T, B], [1, T])
                    link(v.tensor_scalar(o1, x_p, small[:, 4 + j:5 + j], None, ALU.mult))
                    v.scalar_tensor_tensor(out=pat(tmp[2 + k], m * N, [T, B], [1, T]), in0=x_t,
                                           scalar=pb[:, PB_MUR + j:PB_MUR + j + 1], in1=o1,
                                           op0=ALU.mult, op1=ALU.add).then_inc(s["mix_ok"], 1)
                    dve.wait_ge(s["mix_ok"], j + 1)
            for k in range(2):
                dh = (xh[:, 0:KD * N], xk_h)[k]
                dl = (xl[:, 0:KD * N], xk_l)[k]
                for c in range(C):
                    dve.wait_ge(s["mix_hi"], 2 * k + c + 1)
                    sub(chunk(dl, c), chunk(tmp[2 + k], c), chunk(dh, c)).then_inc(s["mix_lo"], 1)
            for c in range(C):
                dve.wait_ge(s["k_relu"], 2 * c + 2)
                v.tensor_tensor(chunk(tmp[4], c), chunk(tmp[1], c), chunk(tmp[1], c), ALU.mult).then_inc(s["k_sq"], 1)
            for c in range(C):
                dve.wait_ge(s["k_hi"], c + 1)
                sub(chunk(xl[:], c), chunk(tmp[4], c), chunk(xh[:], c)).then_inc(s["k_lo"], 1)
            dve.wait_ge(s["r_sig"], 4)
            for i, (m, c) in enumerate(MC):
                r = slice(m * N + c * NC, m * N + (c + 1) * NC)
                dve.wait_ge(s["vv_mm"], i + 1)
                link(v.tensor_tensor(tmp[2][:, r], tmp[0][:, r], bank(4 + i, NC), ALU.mult))
                v.tensor_tensor(tmp[5][:, r], hT[:, r], tmp[2][:, r], ALU.add).then_inc(s["out_ok"], 1)

        @block.tensor
        def _(pe):
            mm = nc.tensor.matmul

            def three(o, a_h, a_l, b_h, b_l, start, stop):
                mm(o, a_h, b_h, start=start, stop=False)
                mm(o, a_h, b_l, start=False, stop=False)
                return mm(o, a_l, b_h, start=False, stop=stop)

            pe.wait_ge(s["d_const"], 16)
            pe.wait_ge(s["d_table"], 16)
            for k in range(T):
                lhs = cb[0:BUCKETS, CB_OH + T - 1 - k:CB_OH + 2 * T - 1 - k]
                w = mm(ps[0:T, k // 32, (k % 32) * HEADS:(k % 32 + 1) * HEADS], lhs, tb[0:BUCKETS, :],
                       start=True, stop=True)
            w.then_inc(s["bias_mm"], 1)
            for k in range(KF):
                pe.wait_ge(s["tok_lo"], k // 2 + 2)
                for i, (m, c) in enumerate(MC):
                    w_ = slice(k * D + m * P, k * D + (m + 1) * P)
                    x_ = slice(k * NP * B + c * NPC, k * NP * B + (c + 1) * NPC)
                    w = three(bank(4 + i, NPC), wh[:, w_], wl[:, w_], patch_h[:, x_], patch_l[:, x_],
                              k == 0, k == KF - 1)
                    if k == KF - 1:
                        w.then_inc(s["tok_mm"], 1)

            def norm(L):
                if L == 0:
                    pe.wait_ge(s["const_set"], 3)
                    pe.wait_ge(s["cls_set"], 1)
                    pe.wait_ge(s["bias_ev"], 2)
                for c in range(C):
                    pe.wait_ge(s["h_ready"], 4 * L + 2 * c + 2)
                    for k in range(KD):
                        w = mm(bank(c, NC), ones[:], hT[:, k * N + c * NC:k * N + (c + 1) * NC],
                               start=(k == 0), stop=(k == KD - 1))
                    w.then_inc(s["ln_mean"], 1)
                for c in range(C):
                    pe.wait_ge(s["ln_sq"], 2 * L + c + 1)
                    for k in range(KD):
                        w = mm(bank(2 + c, NC), ones[:], sq[:, k * N + c * NC:k * N + (c + 1) * NC],
                               start=(k == 0), stop=(k == KD - 1))
                    w.then_inc(s["ln_var"], 1)

            norm(0)
            pe.wait_ge(s["ln_lo"], 2)
            pe.wait_ge(w_lo[2], 1)
            for i in range(2 * PAIRS):
                pair, n = i // 2, i % 2
                if i >= 4:
                    pe.wait_ge(s["v_ev_act"] if i % 2 == 0 else s["v_ev_dve"], (i - 4) // 2 + 1)
                for k in range(KD):
                    x_h, x_l = (x[:, k * NT + pair * T2:k * NT + (pair + 1) * T2] for x in (xh, xl))
                    w_ = slice(2 * W1 + k * INNER + n * 512, 2 * W1 + k * INNER + (n + 1) * 512)
                    w = three(ps[0:T2, i % 4, :], x_h, x_l, wh[:, w_], wl[:, w_], k == 0, k == KD - 1)
                w.then_inc(s["v_mm"], 1)

            def project(hp, c, j):
                n = 2 * hp + c
                if n >= 1:
                    pe.wait_ge(s["q_ev"] if j == 0 else s["k_ev"], n)
                for k in range(KD):
                    w_ = slice(j * W1 + k * INNER + hp * P, j * W1 + k * INNER + (hp + 1) * P)
                    x_ = slice(k * NT + c * NC, k * NT + (c + 1) * NC)
                    w = three(bank(6 + j, NC), wh[:, w_], wl[:, w_], xh[:, x_], xl[:, x_], k == 0, k == KD - 1)
                w.then_inc(s["q_mm"] if j == 0 else s["k_mm"], 1)

            pe.wait_ge(w_lo[0], 1)
            pe.wait_ge(w_lo[1], 1)
            for c in range(C):
                for j in range(2):
                    project(0, c, j)
            pe.wait_ge(s["v_ev_act"], PAIRS)
            pe.wait_ge(s["v_ev_dve"], PAIRS)
            for t in range(2 * HP + 2):
                if t < 2 * HP:
                    hp, half = t // 2, t % 2
                    pe.wait_ge(s["q_ev"], 2 * hp + 2)
                    pe.wait_ge(s["k_ev"], 2 * hp + 2)
                    if t >= 1:
                        pe.wait_ge(s["sc_ev"], t)
                    for g in range(8):
                        pair, hd = PPC * half + g // 2, g % 2
                        r = slice(64 * hd, 64 * hd + 64)
                        w = mm(ps[0:T2, hd, (g // 2) * T2:(g // 2 + 1) * T2],
                               qb[r, (hp % 2) * NT + pair * T2:(hp % 2) * NT + (pair + 1) * T2],
                               kb[r, (hp % 2) * N + pair * T2:(hp % 2) * N + (pair + 1) * T2],
                               start=True, stop=True)
                    w.then_inc(s["sc_mm"], 1)
                    if hp + 1 < HP:
                        project(hp + 1, half, 0)
                        project(hp + 1, half, 1)
                if t >= 2:
                    u = t - 2
                    hp, half = u // 2, u % 2
                    pe.wait_ge(s["normed"], u + 1)
                    if u >= 1:
                        pe.wait_ge(s["pt_ev"], u)
                    for g in range(8):
                        o = (u % 3) * SC + g * T2
                        w = nc.tensor.transpose(ps[0:T2, 2 + g // 4, (g % 4) * T2:(g % 4 + 1) * T2],
                                                sreg[0:T2, o:o + T2], ident[0:T2, 0:T2])
                    w.then_inc(s["pt_mm"], 1)
                    pe.wait_ge(s["pt_ev"], u + 1)
                    if u >= 2:
                        pe.wait_ge(s["ctx_lo"], u - 1)
                    for g in range(8):
                        pair, hd = PPC * half + g % 4, g // 4
                        vo = pair * INNER + hp * P + hd * DH
                        po = (u % 2) * SC + g * T2
                        w = mm(ps[64 * hd:64 * hd + 64, 4 + u % 2, (g % 4) * T2:(g % 4 + 1) * T2],
                               v_all[0:T2, vo:vo + DH], ptb[0:T2, po:po + T2], start=True, stop=True)
                    w.then_inc(s["ctx_mm"], 1)
            pe.wait_ge(w_lo[2], 2)
            pe.wait_ge(s["ctx_lo"], 2 * HP)
            for i, (m, c) in enumerate(MC):
                for k in range(HP):
                    w_ = slice(2 * W1 + k * D + m * P, 2 * W1 + k * D + (m + 1) * P)
                    x_ = slice(k * N + c * NC, k * N + (c + 1) * NC)
                    w = three(bank(4 + i, NC), wh[:, w_], wl[:, w_], ctx_h[:, x_], ctx_l[:, x_], k == 0, k == HP - 1)
                w.then_inc(s["wo_mm"], 1)
            norm(1)
            pe.wait_ge(s["ln_lo"], 4)
            for t in range(TT):
                for k in range(KD):
                    w = mm(ps[:, 0, t * 8:t * 8 + E], xnf[:, k * NT + t * P:k * NT + (t + 1) * P],
                           pb[:, PB_WR + k * E:PB_WR + (k + 1) * E], start=(k == 0), stop=(k == KD - 1))
            w.then_inc(s["rt_mm"], 1)
            comb = route[:, 690:730]
            pe.wait_ge(s["comb_set"], 2)
            for e in range(NX):
                if e >= 2:
                    pe.wait_ge(s["cb_ev"], 2 * (e - 1))
                for t in range(TT):
                    w = mm(ps[:, 2 * (e % 2) + t // 4, (t % 4) * P:(t % 4 + 1) * P],
                           pat(comb, t * 8 + e, [0, P]), ident, start=True, stop=True)
                w.then_inc(s["cb_mm"], 1)
            for i, (m, c) in enumerate(MC):
                mm(bank(4 + i, NC), ident, hT[:, m * N + c * NC:m * N + (c + 1) * NC],
                   start=True, stop=False).then_inc(s["dn_mm"], 1)
            with pe.Fori(0, NX) as e:
                pe.wait_ge(w_lo[0], e + (WBASE[0] + 1))
                pe.wait_ge(w_lo[1], e + (WBASE[1] + 1))

                def gate_up(u):
                    c, j = u // KH, u % KH
                    pe.wait_ge(s["gate_mul"], e * 16 + (u + 1))
                    for q in range(2):
                        for k in range(KD):
                            w_ = slice(q * W1 + k * HID + j * P, q * W1 + k * HID + (j + 1) * P)
                            x_ = slice(k * NT + c * NC, k * NT + (c + 1) * NC)
                            w = three(bank(2 * (u % 2) + q, NC), wh[:, w_], wl[:, w_], xh[:, x_], xl[:, x_],
                                      k == 0, k == KD - 1)
                    w.then_inc(s["gu_mm"], 1)

                def down(u):
                    c, j = u // KH, u % KH
                    pe.wait_ge(s["hid_lo"], e * 16 + (u + 3))
                    x_ = slice((u % 4) * NC, (u % 4 + 1) * NC)
                    for m in range(KD):
                        w_ = slice(2 * W1 + j * D + m * P, 2 * W1 + j * D + (m + 1) * P)
                        w = three(bank(4 + 2 * c + m, NC), wh[:, w_], wl[:, w_], hid_h[:, x_], hid_l[:, x_],
                                  False, False)
                    w.then_inc(s["dn_mm"], 1)

                gate_up(0)
                gate_up(1)
                for u in range(2, 16):
                    gate_up(u)
                    if u == 2:
                        pe.wait_ge(w_lo[2], e + (WBASE[2] + 1))
                    down(u - 2)
                down(14)
                down(15)
            for i in range(4):
                mm(bank(4 + i, P), zero[:], ident, start=False, stop=True).then_inc(s["moe_mm"], 1)
            norm(2)

            def last(w, k, m):
                return slice((w * KD + k) * D + m * P, (w * KD + k) * D + (m + 1) * P)

            pe.wait_ge(s["ln_lo"], 6)
            pe.wait_ge(s["l1_lo"], 5)
            for i, (m, c) in enumerate(MC):
                for w_i, b in ((0, 4 + i), (1, i)):
                    for k in range(KD):
                        x_ = slice(k * NT + c * NC, k * NT + (c + 1) * NC)
                        w = three(bank(b, NC), l1_h[:, last(w_i, k, m)], l1_l[:, last(w_i, k, m)],
                                  xh[:, x_], xl[:, x_], k == 0, k == KD - 1)
                    w.then_inc(s["ra_mm"], 1)
            norm(3)
            pe.wait_ge(s["mix_lo"], 4)
            for i, (m, c) in enumerate(MC):
                for w_i, b, a_h, a_l in ((2, 4 + i, xh, xl), (3, i, xk_h, xk_l)):
                    for k in range(KD):
                        x_ = slice(k * N + c * NC, k * N + (c + 1) * NC)
                        w = three(bank(b, NC), l1_h[:, last(w_i, k, m)], l1_l[:, last(w_i, k, m)],
                                  a_h[:, x_], a_l[:, x_], k == 0, k == KD - 1)
                    w.then_inc(s["rk_mm"], 1)
            for i, (m, c) in enumerate(MC):
                pe.wait_ge(s["r_sig"], i + 1)
                pe.wait_ge(s["k_lo"], c + 1)
                for k in range(KD):
                    x_ = slice(k * N + c * NC, k * N + (c + 1) * NC)
                    w = three(bank(4 + i, NC), l1_h[:, last(4, k, m)], l1_l[:, last(4, k, m)],
                              xh[:, x_], xl[:, x_], k == 0, k == KD - 1)
                w.then_inc(s["vv_mm"], 1)


def bucket_onehot():
    rp = 36 - np.arange(100)
    half, exact = BUCKETS // 2, BUCKETS // 4
    a = np.abs(rp)
    far = exact + (np.log(np.maximum(a, 1).astype(np.float32) / np.float32(exact))
                   / np.float32(math.log(128 / exact)) * np.float32(half - exact)).astype(np.int32)
    bucket = (rp > 0) * half + np.where(a < exact, a, np.minimum(far, half - 1))
    oh = np.zeros((P, 100), np.float32)
    for j in range(73):
        oh[bucket[j], j] = 1.0
    return oh


def kernel(**inputs):
    import concourse.bacc as bacc
    from concourse.bass_utils import run_bass_kernel_spmd

    x = {k: np.asarray(v) for k, v in inputs.items()}

    def tiles(a):
        return np.ascontiguousarray(a.reshape(-1, P, a.shape[-1]).transpose(1, 0, 2).reshape(P, -1))

    im = x["x"].reshape(B, 3, GRID, PATCH, GRID, PATCH).transpose(1, 3, 5, 0, 2, 4).reshape(FP, B * NP)
    cols = np.concatenate([x["L0_tok_position_embeddings"][0].T, x["L0_tok_class_token"][0].T], axis=1)
    per = [tiles(cols[:, :T]), tiles(cols[:, T:])]
    for n in ("L0_tok_b_lin", "L1_attn_b_delta", "L1_attn_b_value", "L1_ffn_mu_r", "L1_ffn_mu_k"):
        per.append(tiles(x[n][:, None]))
    per.append(tiles(x["L0_ffn_router_w"].T))
    tri = np.tile((np.arange(E)[None, :] < np.arange(E)[:, None]).astype(np.float32).reshape(1, -1), (P, 1))
    last = [tiles(x[n].T) for n in ("L1_attn_W_delta", "L1_attn_W_value", "L1_ffn_W_r", "L1_ffn_W_k", "L1_ffn_W_v")]
    arrays = {
        "patches": tiles(im),
        "w_lin": tiles(x["L0_tok_W_lin"].T),
        "par": np.concatenate(per, axis=1),
        "const": np.concatenate([np.eye(P, dtype=np.float32), tri, bucket_onehot()], axis=1),
        "table": x["L0_attn_rel_bias_table"],
        "w_q": x["L0_attn_w_q"], "w_k": x["L0_attn_w_k"], "w_v": x["L0_attn_w_v"], "w_o": x["L0_attn_w_o"],
        "w_gate": np.concatenate([x["L0_ffn_w_gate"], x["L0_ffn_sw_gate"]]),
        "w_up": np.concatenate([x["L0_ffn_w_up"], x["L0_ffn_sw_up"]]),
        "w_down": np.concatenate([x["L0_ffn_w_down"], x["L0_ffn_sw_down"]]),
        "w_l1": np.concatenate(last, axis=1),
    }
    nc = bacc.Bacc("TRN2", target_bir_lowering=False, num_devices=1)
    feed, args = {}, []
    for name, a in arrays.items():
        a = np.ascontiguousarray(a)
        feed[f"in_{name}"] = a
        args.append(nc.dram_tensor(f"in_{name}", a.shape, mybir.dt.from_np(a.dtype), kind="ExternalInput").ap())
    o = nc.dram_tensor("out_h", (D, N), F32, kind="ExternalOutput").ap()
    vit_tower(nc, *args, o)
    r = run_bass_kernel_spmd(nc, [feed], core_ids=[0])
    return np.ascontiguousarray(r.results[0]["out_h"].reshape(D, B, T).transpose(1, 2, 0))
```

```python
import math
from contextlib import ExitStack

import numpy as np

import concourse.bass as bass
from concourse import mybir

F32 = mybir.dt.float32
F32R = mybir.dt.float32r
ACT = mybir.ActivationFunctionType
ALU = mybir.AluOpType
AX = mybir.AxisListType

P = 128
B = 16
PATCH = 16
GRID = 96 // PATCH
NP = GRID * GRID
T = NP + 1
N = B * T
D = 256
KD = D // P
FP = 3 * PATCH * PATCH
KF = FP // P
HEADS = 16
DH = 64
INNER = HEADS * DH
HP = INNER // P
HID = 1024
KH = HID // P
E = 7
NX = E + 1
C = 2
NC = N // C
BC = B // C
NPC = BC * NP
PAIRS = B // 2
PPC = PAIRS // C
NT = 640
TT = NT // P
T2 = 2 * T
SC = 2 * PPC * T2
MASK = -1e30
SLOTS = 256
ST = SLOTS // P
W1 = KD * HID
BUCKETS = 32
EPS = 1e-5

MC = [(0, 0), (1, 0), (0, 1), (1, 1)]

PB_POS, PB_CLS, PB_BLIN, PB_BD, PB_BV, PB_MUR, PB_MUK, PB_WR = 0, 74, 76, 78, 80, 82, 84, 86
PB = PB_WR + KD * E
CB_ID, CB_TRI, CB_OH = 0, P, P + E * E
CB = CB_OH + 100
RB_IOTA, RB_PART, RB_TRI, RB_ONES = 0, SLOTS, SLOTS + ST, SLOTS + ST + P
RB_REAL = RB_ONES + P
RB = RB_REAL + TT


def pat(a, off, *dims):
    return bass.AP(a.tensor, a.offset + off, [list(a.ap[0])] + [list(d) for d in dims])


def vit_tower(nc, patches, w_lin, par, const, table, w_q, w_k, w_v, w_o, w_gate, w_up, w_down, w_l1, rconst, out):
    ctx = ExitStack()
    with ctx:
        def sb(name, cols, dt=F32):
            return ctx.enter_context(nc.sbuf_tensor(name, [P, cols], dt))

        def sem(name):
            return ctx.enter_context(nc.semaphore(name))

        ws = sb("w_stage", 3 * W1)
        vreg = sb("v_region", PAIRS * INNER)
        hT = sb("hT", KD * N)
        xnf = sb("xn_f32", KD * NT)
        xc = sb("x_centred", KD * N)
        sq = sb("x_squared", KD * N)
        rstd = sb("rstd", N)
        eps = sb("eps", 1)
        qb = sb("q_buf", 2 * NT)
        kb = sb("k_buf", 2 * N)
        sreg = sb("s_region", 3072)
        ptb = sb("probs_T", 2 * 592)
        bias = sb("bias_pair", HEADS * T2)
        stat = sb("softmax_stats", 3 * 3 * 8)
        pb = sb("params", PB)
        cb = sb("consts", CB)
        tb = sb("bias_table", HEADS)
        ones = sb("ones_over_d", P)
        zero = sb("zeros", P)
        small = sb("small", 24)
        wh = sb("w_hi", 3 * W1, F32R)
        wl = sb("w_lo", 3 * W1, F32R)
        cr = sb("c_region", 2 * HP * N, F32R)
        xh = sb("xn_hi", KD * NT, F32R)
        xl = sb("xn_lo", KD * NT, F32R)
        ps = ctx.enter_context(nc.psum_tensor("ps", [P, 8, 512], F32))

        PW = KF * NPC * C
        patch_s = vreg[:, 0:PW]
        wlin_s = vreg[:, PW:PW + KF * D]
        patch_h, patch_l = cr[:, 0:PW], cr[:, PW:2 * PW]
        v_all = vreg[:, :]
        ctx_h, ctx_l = cr[:, 0:HP * N], cr[:, HP * N:2 * HP * N]
        HR = 4 * NC
        hid_h, hid_l = cr[:, 0:HR], cr[:, HR:2 * HR]
        xk_h, xk_l = cr[:, 0:KD * N], cr[:, KD * N:2 * KD * N]
        gh_h, gh_l = cr[:, 0:KH * SLOTS], cr[:, KH * SLOTS:2 * KH * SLOTS]
        r0 = 2 * KH * SLOTS
        xt_h, xt_l = cr[:, r0:r0 + TT * D], cr[:, r0 + TT * D:r0 + 2 * TT * D]
        r0 += 2 * TT * D
        pg = cr[:, r0:r0 + TT * SLOTS]
        r0 += TT * SLOTS
        pt = cr[:, r0:r0 + ST * N]
        r0 += ST * N
        slot_r, cw_r, ident_r = cr[:, r0:r0 + 8], cr[:, r0 + 8:r0 + 24], cr[:, r0 + 24:r0 + 24 + P]
        G = KD * SLOTS
        xg_h, xg_l = xh[:, 0:G], xl[:, 0:G]
        y_h, y_l = xh[:, G:G + ST * D], xl[:, G:G + ST * D]
        silu_g, prod_g = sreg[:, 0:2 * G], sreg[:, 2 * G:4 * G]
        L1W = 5 * KD * D
        l1_s = vreg[:, 0:L1W]
        l1_h, l1_l = wh[:, 0:L1W], wl[:, 0:L1W]
        cbc = vreg[:, L1W:L1W + E * N]
        rc0 = L1W + 4 * KD * N
        rcb = vreg[:, rc0:rc0 + RB]
        r1 = rc0 + RB
        comb, slot = vreg[:, r1:r1 + 40], vreg[:, r1 + 40:r1 + 80]
        slot_c, comb_c = vreg[:, r1 + 80:r1 + 88], vreg[:, r1 + 88:r1 + 96]
        cw_slot, count = vreg[:, r1 + 96:r1 + 98], vreg[:, r1 + 98:r1 + 99]
        tmp = [vreg[:, o:o + KD * N] for o in [L1W + k * KD * N for k in range(4)] + [0, KD * N]]
        silu_b, prod_b, wprod_b = (sreg[:, k * 2 * NC:(k + 1) * 2 * NC] for k in range(3))
        route = sreg[:, 1800:3072]
        bias_q = ptb[:, 0:HEADS * T]
        cbe = ptb[:, 0:N]
        ident = cb[:, CB_ID:CB_ID + P]

        count_i = ctx.enter_context(nc.sbuf_tensor("count_i", [P, 1], mybir.dt.int32))
        s = {n: sem(n) for n in (
            "d_par d_const d_table d_wlin d_l1 d_out "
            "const_set pad_set mask_set bias_mm bias_ev d_bias tok_hi tok_lo tok_mm cls_set h_ready "
            "ln_mean ln_xc ln_sq ln_var ln_std ln_rs ln_xn ln_hi ln_lo "
            "v_mm v_ev_act v_ev_dve q_mm k_mm q_ev k_ev sc_mm sc_ev maxed shifted expd summed recip normed "
            "pt_mm pt_ev ctx_mm ctx_hi ctx_lo wo_mm "
            "d_rc xt_mm xt_hi xt_lo sel_set pos_mm count_set "
            "g_mm g_silu g_mul g_hi g_lo g_scat g_row g_pt g_pg g_gath g_xh g_xl g_y g_yh g_yl g_chain "
            "rt_mm rt_shift rt_exp dve_chain comb_set cb_mm cb_ev seeded gu_mm silu_ok gate_mul "
            "weighted cbe_set hid_hi hid_lo dn_mm moe_mm l1_hi l1_lo ra_mm ra_sig scan_chain "
            "mix_ok mixk_ok mix_hi mix_lo rk_mm r_sig k_relu k_sq k_hi k_lo vv_mm out_ok").split()}
        d_patch = [sem(f"d_patch{i}") for i in range(3)]
        d_w = [sem(f"d_w{i}") for i in range(3)]
        w_hi = [sem(f"w_hi{i}") for i in range(3)]
        w_lo = [sem(f"w_lo{i}") for i in range(3)]
        WBASE = (1, 1, 2)

        def bank(k, cols=512, off=0):
            return ps[:, k, off:off + cols]

        def chunk(a, c, width=N):
            return pat(a, c * NC, [width, KD], [1, NC])

        block = ctx.enter_context(nc.Block())

        @block.sync
        def _(sp):
            sp.dma_start(wlin_s, w_lin).then_inc(s["d_wlin"], 16)
            for i in range(3):
                n = PW // 3
                sp.dma_start(patch_s[:, i * n:(i + 1) * n], patches[:, i * n:(i + 1) * n]).then_inc(d_patch[i], 16)
            sp.dma_start(cb[:], const).then_inc(s["d_const"], 16)
            sp.dma_start(tb[0:BUCKETS, :], table).then_inc(s["d_table"], 16)
            sp.dma_start(pb[:], par).then_inc(s["d_par"], 16)

            def part(p):
                return ws[:, p * W1:(p + 1) * W1]

            def rows(w, k):
                return w.rearrange("(k p) n -> p k n", p=P)

            sp.dma_start(part(2).rearrange("p (k n) -> p k n", k=KD), rows(w_v, KD)).then_inc(d_w[2], 16)
            sp.dma_start(part(0).rearrange("p (k n) -> p k n", k=KD), rows(w_q, KD)).then_inc(d_w[0], 16)
            sp.dma_start(part(1).rearrange("p (k n) -> p k n", k=KD), rows(w_k, KD)).then_inc(d_w[1], 16)
            sp.wait_ge(s["bias_ev"], 2)
            sp.wait_ge(s["mask_set"], 1)
            for b2 in range(2):
                sp.dma_start(pat(bias[b2 * T:(b2 + 1) * T, :], b2 * T, [T2, HEADS], [1, T]),
                             bias_q[0:T, :].rearrange("p (h k) -> p h k", h=HEADS)).then_inc(s["d_bias"], 16)
            sp.wait_ge(w_lo[2], 1)
            sp.dma_start(part(2).rearrange("p (k n) -> p k n", k=HP), rows(w_o, HP)).then_inc(d_w[2], 16)
            with sp.Fori(0, NX) as e:
                for p, w in ((0, w_gate), (1, w_up), (2, w_down)):
                    k = KD if p < 2 else KH
                    sp.wait_ge(w_lo[p], e + WBASE[p])
                    sp.dma_start(part(p).rearrange("p (k n) -> p k n", k=k),
                                 w[bass.ds(e, 1)].rearrange("o (k p) n -> p (o k) n", p=P)).then_inc(d_w[p], 16)
            sp.wait_ge(s["out_ok"], 4)
            sp.dma_start(out.rearrange("(m p) n -> p m n", p=P),
                         tmp[5].rearrange("p (m n) -> p m n", m=KD)).then_inc(s["d_out"], 16)
            sp.wait_ge(s["d_out"], 16)

        @block.gpsimd
        def _(pool):
            g = nc.gpsimd
            g.memset(ones[:], 1.0 / D).then_inc(s["const_set"], 1)
            g.memset(zero[:], 0.0).then_inc(s["const_set"], 1)
            g.memset(eps[:], EPS).then_inc(s["const_set"], 1)
            for a in (xnf, xh, xl):
                g.memset(pat(a[:], N, [NT, KD], [1, NT - N]).bitcast(F32), 0.0).then_inc(s["pad_set"], 1)
            g.memset(bias[0:T2, :], MASK).then_inc(s["mask_set"], 1)
            for t in range(2 * HP + 1):
                if t < 2 * HP:
                    pool.wait_ge(s["maxed"], t + 1)
                    sc = pat(sreg[0:T2, :], (t % 3) * SC, [T2, 8], [1, T2])
                    g.tensor_tensor(sc, sc, pat(stat[0:T2, :], (t % 3) * 24, [1, 8], [0, T2]),
                                    ALU.subtract).then_inc(s["shifted"], 1)
                if t >= 1:
                    u = t - 1
                    pool.wait_ge(s["recip"], u + 1)
                    sc = pat(sreg[0:T2, :], (u % 3) * SC, [T2, 8], [1, T2])
                    g.tensor_tensor(sc, sc, pat(stat[0:T2, :], (u % 3) * 24 + 16, [1, 8], [0, T2]),
                                    ALU.mult).then_inc(s["normed"], 1)
            pool.wait_ge(s["pt_mm"], 2 * HP)
            pool.wait_ge(s["ctx_mm"], 2 * HP)
            g.memset(cbe, 1.0).then_inc(s["cbe_set"], 1)
            for i in range(2):
                g.memset(wprod_b[:, i * NC:(i + 1) * NC], 0.0).then_inc(s["weighted"], 1)
                g.memset(small[:, 16 + i:17 + i], 0.0).then_inc(s["hid_lo"], 1)

            def dense_expert(e):
                pool.wait_ge(s["cbe_set"], e + 1)

                def weigh(u):
                    pool.wait_ge(s["gate_mul"], e * 16 + (u + 3))
                    pool.wait_ge(s["hid_lo"], e * 16 + (u + 1))
                    g.tensor_tensor(wprod_b[:, (u % 2) * NC:(u % 2 + 1) * NC],
                                    prod_b[:, (u % 2) * NC:(u % 2 + 1) * NC],
                                    cbe[:, (u // 8) * NC:(u // 8 + 1) * NC], ALU.mult).then_inc(s["weighted"], 1)

                def low(u):
                    pool.wait_ge(s["hid_hi"], e * 16 + (u + 1))
                    g.tensor_tensor(hid_l[:, (u % 4) * NC:(u % 4 + 1) * NC],
                                    wprod_b[:, (u % 2) * NC:(u % 2 + 1) * NC],
                                    hid_h[:, (u % 4) * NC:(u % 4 + 1) * NC].bitcast(F32),
                                    ALU.subtract).then_inc(s["hid_lo"], 1)
                weigh(0)
                for u in range(1, 16):
                    weigh(u)
                    low(u - 1)
                low(15)

            dense_expert(0)
            pool.wait_ge(s["count_set"], 1)
            with pool.If(pool.value_load(count_i[0:1, 0:1]) <= SLOTS):
                def down_low(e):
                    r = slice(2 * W1, 3 * W1)
                    pool.wait_ge(w_hi[2], e + (WBASE[2] + 1))
                    g.tensor_tensor(wl[:, r], ws[:, r], wh[:, r].bitcast(F32), ALU.subtract).then_inc(w_lo[2], 1)
                down_low(1)
                with pool.Fori(1, E) as e:
                    down_low(e + 1)
            with pool.Else():
                pool.wait_ge(s["cb_ev"], 2 * E)
                with pool.Fori(1, NX) as e:
                    g.tensor_copy(cbe, cbc[:, bass.ds((e - 1) * N, N)]).then_inc(s["cbe_set"], 1)
                    dense_expert(e)
            for i in range(2, 5):
                r = slice(i * KD * D, (i + 1) * KD * D)
                pool.wait_ge(s["l1_hi"], i + 1)
                g.tensor_tensor(l1_l[:, r], l1_s[:, r], l1_h[:, r].bitcast(F32), ALU.subtract).then_inc(s["l1_lo"], 1)

        @block.scalar
        def _(act):
            a = nc.scalar

            def w_high(p, n):
                a.activation(wh[:, p * W1:p * W1 + n], ws[:, p * W1:p * W1 + n], ACT.Copy).then_inc(w_hi[p], 1)

            act.wait_ge(s["d_wlin"], 16)
            a.activation(wh[:, 0:KF * D], wlin_s, ACT.Copy).then_inc(s["tok_hi"], 1)
            for i in range(3):
                n = PW // 3
                act.wait_ge(d_patch[i], 16)
                a.activation(patch_h[:, i * n:(i + 1) * n], patch_s[:, i * n:(i + 1) * n],
                             ACT.Copy).then_inc(s["tok_hi"], 1)
            act.wait_ge(d_w[2], 16)
            w_high(2, W1)

            def norm(L, dst, width, dst_hi=True):
                for c in range(C):
                    act.wait_ge(s["ln_xc"], 2 * L + c + 1)
                    a.activation(chunk(sq[:], c), chunk(xc[:], c), ACT.Square).then_inc(s["ln_sq"], 1)
                for c in range(C):
                    act.wait_ge(s["ln_var"], 2 * L + c + 1)
                    a.activation(rstd[:, c * NC:(c + 1) * NC], bank(2 + c, NC), ACT.Sqrt,
                                 bias=eps[:, 0:1]).then_inc(s["ln_std"], 1)
                if dst_hi:
                    for c in range(C):
                        act.wait_ge(s["ln_xn"], 2 * L + c + 1)
                        a.activation(chunk(xh[:], c, NT), chunk(dst, c, NT), ACT.Copy).then_inc(s["ln_hi"], 1)

            act.wait_ge(s["const_set"], 3)
            act.wait_ge(s["pad_set"], 3)
            norm(0, xnf[:], NT)
            for i in range(0, 2 * PAIRS, 2):
                act.wait_ge(s["v_mm"], i + 1)
                a.activation(v_all[0:T2, i * 512:(i + 1) * 512], ps[0:T2, i % 4, :], ACT.Copy).then_inc(s["v_ev_act"], 1)
                if i in (0, 2):
                    act.wait_ge(d_w[i // 2], 16)
                    act.wait_ge(s["tok_mm"], 4)
                    w_high(i // 2, W1)
            act.wait_ge(d_w[2], 32)
            act.wait_ge(s["v_mm"], 2 * PAIRS)
            w_high(2, W1)

            def q_evac(n):
                hp, c = n // 2, n % 2
                act.wait_ge(s["q_mm"], n + 1)
                if hp >= 2:
                    act.wait_ge(s["sc_mm"], 2 * hp - 2)
                a.activation(qb[:, (hp % 2) * NT + c * NC:(hp % 2) * NT + (c + 1) * NC], bank(6, NC),
                             ACT.Copy).then_inc(s["q_ev"], 1)

            def k_evac(n):
                hp, c = n // 2, n % 2
                act.wait_ge(s["k_mm"], n + 1)
                if hp >= 2:
                    act.wait_ge(s["sc_mm"], 2 * hp - 2)
                a.activation(kb[:, (hp % 2) * N + c * NC:(hp % 2) * N + (c + 1) * NC], bank(7, NC),
                             ACT.Copy).then_inc(s["k_ev"], 1)

            for n in range(2):
                q_evac(n)
                k_evac(n)
            for t in range(2 * HP + 2):
                if t >= 2:
                    v = t - 2
                    act.wait_ge(s["pt_mm"], v + 1)
                    if v >= 2:
                        act.wait_ge(s["ctx_mm"], v - 1)
                    a.activation(pat(ptb[0:T2, :], (v % 2) * SC, [SC // 2, 2], [1, SC // 2]),
                                 pat(ps[0:T2, 2, :], 0, [512, 2], [1, SC // 2]), ACT.Copy).then_inc(s["pt_ev"], 1)
                if t + 2 < 2 * HP:
                    q_evac(t + 2)
                    k_evac(t + 2)
                if t < 2 * HP:
                    act.wait_ge(s["shifted"], t + 1)
                    sc = sreg[0:T2, (t % 3) * SC:(t % 3 + 1) * SC]
                    a.activation(sc, sc, ACT.Exp).then_inc(s["expd"], 1)
                if t >= 2:
                    act.wait_ge(s["ctx_mm"], v + 1)
                    hp, c = v // 2, v % 2
                    a.activation(ctx_h[:, hp * N + c * NC:hp * N + (c + 1) * NC], bank(4 + v % 2, NC),
                                 ACT.Copy).then_inc(s["ctx_hi"], 1)
            act.dma_start(rcb, rconst).then_inc(s["d_rc"], 16)
            act.dma_start(l1_s, w_l1).then_inc(s["d_l1"], 16)

            def expert_high(p, e):
                act.wait_ge(d_w[p], e * 16 + 16 * (WBASE[p] + 1))
                w_high(p, W1)

            expert_high(0, 0)
            expert_high(1, 0)
            norm(1, xnf[:], NT)
            a.activation(ident_r, ident, ACT.Copy).then_inc(s["xt_hi"], 1)
            act.wait_ge(s["xt_mm"], 1)
            a.activation(xt_h, pat(bank(1), 0, [1, TT * D]), ACT.Copy).then_inc(s["xt_hi"], 1)
            act.wait_ge(s["rt_shift"], 1)
            a.activation(route[:, 80:115], route[:, 80:115], ACT.Exp).then_inc(s["rt_exp"], 1)
            act.wait_ge(s["wo_mm"], 4)
            expert_high(2, 0)

            def dense_expert(e):
                def silu(u):
                    act.wait_ge(s["gu_mm"], e * 16 + (u + 1))
                    act.wait_ge(s["gate_mul"], e * 16 + (u + 1))
                    a.activation(silu_b[:, (u % 2) * NC:(u % 2 + 1) * NC], bank(2 * (u % 2), NC),
                                 ACT.Silu).then_inc(s["silu_ok"], 1)

                def high(u):
                    act.wait_ge(s["weighted"], e * 16 + (u + 3))
                    act.wait_ge(s["dn_mm"], e * 16 + (u + 1))
                    a.activation(hid_h[:, (u % 4) * NC:(u % 4 + 1) * NC], wprod_b[:, (u % 2) * NC:(u % 2 + 1) * NC],
                                 ACT.Copy).then_inc(s["hid_hi"], 1)
                silu(0)
                for u in range(1, 16):
                    silu(u)
                    high(u - 1)
                high(15)

            dense_expert(0)
            act.wait_ge(s["gu_mm"], 16)
            expert_high(0, 1)
            expert_high(1, 1)
            act.wait_ge(s["dn_mm"], 4 + 16)
            expert_high(2, 1)
            act.wait_ge(s["count_set"], 1)
            with act.If(act.value_load(count_i[0:1, 0:1]) <= SLOTS):
                act.wait_ge(s["g_gath"], 1)
                a.activation(xg_h, bank(0), ACT.Copy).then_inc(s["g_xh"], 1)

                def gathered_expert(e, final):
                    x = e - 1

                    def silu(i):
                        act.wait_ge(s["g_mm"], x * 4 + (i + 1))
                        b = 2 if i == 2 else 0
                        a.activation(pat(silu_g, (i % 2) * G, [SLOTS, 2], [1, SLOTS]),
                                     pat(bank(b), 0, [512, 2], [1, SLOTS]), ACT.Silu).then_inc(s["g_silu"], 1)

                    def high(i):
                        act.wait_ge(s["g_mul"], x * 4 + (i + 1))
                        a.activation(gh_h[:, i * G:(i + 1) * G], prod_g[:, (i % 2) * G:(i % 2 + 1) * G],
                                     ACT.Copy).then_inc(s["g_hi"], 1)

                    for i in range(3):
                        silu(i)
                        high(i)
                    silu(3)
                    if not final:
                        expert_high(0, e + 1)
                    high(3)
                    if not final:
                        expert_high(1, e + 1)
                        act.wait_ge(s["g_gath"], x + 2)
                        a.activation(xg_h, bank(0), ACT.Copy).then_inc(s["g_xh"], 1)
                    act.wait_ge(s["g_y"], x + 1)
                    act.wait_ge(s["g_pt"], x + 2)
                    for st in range(ST):
                        a.activation(y_h[:, st * D:(st + 1) * D], bank(2 + st, D), ACT.Copy,
                                     scale=cw_slot[:, st:st + 1]).then_inc(s["g_yh"], 1)
                    if not final:
                        expert_high(2, e + 1)

                with act.Fori(1, E) as e:
                    gathered_expert(e, False)
                gathered_expert(E, True)
            with act.Else():
                dense_expert(1)
                with act.Fori(2, NX) as e:
                    act.wait_ge(s["gate_mul"], e * 16 + 2)
                    expert_high(0, e)
                    expert_high(1, e)
                    act.wait_ge(s["dn_mm"], e * 16 + 4)
                    expert_high(2, e)
                    dense_expert(e)
            act.wait_ge(s["d_l1"], 16)
            act.wait_ge(s["moe_mm"], 1)
            for i in range(5):
                r = slice(i * KD * D, (i + 1) * KD * D)
                a.activation(l1_h[:, r], l1_s[:, r], ACT.Copy).then_inc(s["l1_hi"], 1)
            norm(2, xnf[:], NT)
            for i, (m, c) in enumerate(MC):
                act.wait_ge(s["ra_mm"], 2 * i + 1)
                a.activation(tmp[0][:, m * N + c * NC:m * N + (c + 1) * NC], bank(4 + i, NC), ACT.Sigmoid,
                             bias=pb[:, PB_BD + m:PB_BD + m + 1]).then_inc(s["ra_sig"], 1)
            norm(3, xnf[:], NT, dst_hi=False)
            act.wait_ge(s["mix_ok"], 4)
            for k in range(2):
                dst = (xh[:, 0:KD * N], xk_h)[k]
                for c in range(C):
                    a.activation(chunk(dst, c), chunk(tmp[2 + k], c), ACT.Copy).then_inc(s["mix_hi"], 1)
            for i, (m, c) in enumerate(MC):
                r = slice(m * N + c * NC, m * N + (c + 1) * NC)
                act.wait_ge(s["rk_mm"], 2 * i + 1)
                a.activation(tmp[0][:, r], bank(4 + i, NC), ACT.Sigmoid).then_inc(s["r_sig"], 1)
                act.wait_ge(s["rk_mm"], 2 * i + 2)
                a.activation(tmp[1][:, r], bank(i, NC), ACT.Relu).then_inc(s["k_relu"], 1)
            act.wait_ge(s["rk_mm"], 8)
            for c in range(C):
                act.wait_ge(s["k_sq"], c + 1)
                a.activation(chunk(xh[:], c), chunk(tmp[4], c), ACT.Copy).then_inc(s["k_hi"], 1)

        @block.vector
        def _(dve):
            v = nc.vector
            chain = [0]

            def link(ins):
                chain[0] += 1
                ins.then_inc(s["dve_chain"], 1)
                dve.wait_ge(s["dve_chain"], chain[0])

            def sub(o, x, hi):
                return v.tensor_tensor(o, x, hi.bitcast(F32), ALU.subtract)

            def w_low(p, n):
                return sub(wl[:, p * W1:p * W1 + n], ws[:, p * W1:p * W1 + n],
                           wh[:, p * W1:p * W1 + n]).then_inc(w_lo[p], 1)

            dve.wait_ge(s["tok_hi"], 1)
            sub(wl[:, 0:KF * D], wlin_s, wh[:, 0:KF * D]).then_inc(s["tok_lo"], 1)
            for i in range(3):
                n = PW // 3
                dve.wait_ge(s["tok_hi"], i + 2)
                r = slice(i * n, (i + 1) * n)
                sub(patch_l[:, r], patch_s[:, r], patch_h[:, r]).then_inc(s["tok_lo"], 1)
            dve.wait_ge(s["bias_mm"], 1)
            v.tensor_copy(pat(bias_q[0:T, :], 0, [T, HEADS], [1, 32]),
                          pat(ps[0:T, 0, :], 0, [1, HEADS], [HEADS, 32])).then_inc(s["bias_ev"], 1)
            v.tensor_copy(pat(bias_q[0:T, :], 32, [T, HEADS], [1, T - 32]),
                          pat(ps[0:T, 1, :], 0, [1, HEADS], [HEADS, T - 32])).then_inc(s["bias_ev"], 1)
            dve.wait_ge(w_hi[2], 1)
            w_low(2, W1)
            dve.wait_ge(s["d_par"], 16)
            link(v.tensor_tensor(small[:, 0:KD], pb[:, PB_CLS:PB_CLS + KD],
                                 pat(pb[:], PB_POS, [T, KD]), ALU.add))
            v.tensor_copy(pat(hT[:], 0, [N, KD], [T, B]),
                          pat(small[:], 0, [1, KD], [0, B])).then_inc(s["cls_set"], 1)
            for i, (m, c) in enumerate(MC):
                dve.wait_ge(s["tok_mm"], i + 1)
                v.scalar_tensor_tensor(out=pat(hT[:], m * N + c * NC + 1, [T, BC], [1, NP]),
                                       in0=bank(4 + i, NPC).rearrange("p (b n) -> p b n", b=BC),
                                       scalar=pb[:, PB_BLIN + m:PB_BLIN + m + 1],
                                       in1=pat(pb[:], PB_POS + m * T + 1, [0, BC], [1, NP]),
                                       op0=ALU.add, op1=ALU.add).then_inc(s["h_ready"], 1)

            def norm(L, dst, lo=True):
                for c in range(C):
                    dve.wait_ge(s["ln_mean"], 2 * L + c + 1)
                    v.tensor_tensor(chunk(xc[:], c), chunk(hT[:], c), pat(bank(c), 0, [0, KD], [1, NC]),
                                    ALU.subtract).then_inc(s["ln_xc"], 1)
                for c in range(C):
                    dve.wait_ge(s["ln_std"], 2 * L + c + 1)
                    r = rstd[:, c * NC:(c + 1) * NC]
                    v.reciprocal(r, r).then_inc(s["ln_rs"], 1)
                    dve.wait_ge(s["ln_rs"], 2 * L + c + 1)
                    for o, i_, r_ in dst(c):
                        v.tensor_tensor(o, i_, r_, ALU.mult).then_inc(s["ln_xn"], 1)
                if lo:
                    for c in range(C):
                        dve.wait_ge(s["ln_hi"], 2 * L + c + 1)
                        sub(chunk(xl[:], c, NT), chunk(xnf[:], c, NT), chunk(xh[:], c, NT)).then_inc(s["ln_lo"], 1)

            def plain(c):
                return [(chunk(xnf[:], c, NT), chunk(xc[:], c), pat(rstd[:], c * NC, [0, KD], [1, NC]))]

            norm(0, plain)
            for i in range(1, 2 * PAIRS, 2):
                dve.wait_ge(s["v_mm"], i + 1)
                v.tensor_copy(v_all[0:T2, i * 512:(i + 1) * 512], ps[0:T2, i % 4, :]).then_inc(s["v_ev_dve"], 1)
                if i in (3, 5):
                    p = (i - 3) // 2
                    dve.wait_ge(w_hi[p], 1)
                    w_low(p, W1)
            dve.wait_ge(w_hi[2], 2)
            w_low(2, W1)

            dve.wait_ge(s["d_bias"], 32)
            for t in range(2 * HP + 3):
                if t < 2 * HP:
                    hp = t // 2
                    sc = sreg[0:T2, (t % 3) * SC:(t % 3 + 1) * SC]
                    dve.wait_ge(s["sc_mm"], t + 1)
                    if t >= 3:
                        dve.wait_ge(s["pt_mm"], t - 2)
                    v.tensor_tensor(pat(sc, 0, [PPC * T2, 2], [T2, PPC], [1, T2]),
                                    pat(ps[0:T2, 0, :], 0, [512, 2], [T2, PPC], [1, T2]),
                                    pat(bias[0:T2, :], 2 * hp * T2, [T2, 2], [0, PPC], [1, T2]),
                                    ALU.add).then_inc(s["sc_ev"], 1)
                    dve.wait_ge(s["sc_ev"], t + 1)
                    v.tensor_reduce(stat[0:T2, (t % 3) * 24:(t % 3) * 24 + 8], sc.rearrange("p (g k) -> p g k", g=8),
                                    AX.X, ALU.max).then_inc(s["maxed"], 1)
                if 1 <= t <= 2 * HP:
                    u = t - 1
                    sm, rc = (stat[0:T2, (u % 3) * 24 + 8 * k:(u % 3) * 24 + 8 * k + 8] for k in (1, 2))
                    dve.wait_ge(s["expd"], u + 1)
                    v.tensor_reduce(sm, pat(sreg[0:T2, :], (u % 3) * SC, [T2, 8], [1, T2]),
                                    AX.X, ALU.add).then_inc(s["summed"], 1)
                    dve.wait_ge(s["summed"], u + 1)
                    v.reciprocal(rc, sm).then_inc(s["recip"], 1)
                if t >= 3:
                    u = t - 3
                    hp, c = u // 2, u % 2
                    r = slice(hp * N + c * NC, hp * N + (c + 1) * NC)
                    dve.wait_ge(s["ctx_hi"], u + 1)
                    sub(ctx_l[:, r], bank(4 + u % 2, NC), ctx_h[:, r]).then_inc(s["ctx_lo"], 1)

            def expert_low(p, e):
                dve.wait_ge(w_hi[p], e + (WBASE[p] + 1))
                w_low(p, W1)

            expert_low(0, 0)
            expert_low(1, 0)
            for i, (m, c) in enumerate(MC):
                r = slice(m * N + c * NC, m * N + (c + 1) * NC)
                dve.wait_ge(s["wo_mm"], i + 1)
                v.tensor_tensor(hT[:, r], hT[:, r], bank(4 + i, NC), ALU.add).then_inc(s["h_ready"], 1)
            norm(1, plain)
            lg, gt, eq = route[:, 0:40], route[:, 120:365], route[:, 365:610]
            rank, selm, mx5, sm5 = route[:, 610:645], route[:, 645:680], route[:, 680:685], route[:, 685:690]
            ex, selr = route[:, 80:115], route[:, 690:725]
            jj = ([8, TT], [0, E], [1, E])
            ee = ([8, TT], [1, E], [0, E])
            three = ([49, TT], [E, E], [1, E])
            dve.wait_ge(s["rt_mm"], 1)
            dve.wait_ge(s["d_const"], 16)
            link(v.tensor_copy(lg, bank(0, 40)))
            link(v.tensor_tensor(pat(gt, 0, *three), pat(lg, 0, *jj), pat(lg, 0, *ee), ALU.is_gt))
            link(v.tensor_tensor(pat(eq, 0, *three), pat(lg, 0, *jj), pat(lg, 0, *ee), ALU.is_equal))
            link(v.tensor_tensor(pat(eq, 0, *three), pat(eq, 0, *three),
                                 pat(cb[:], CB_TRI, [0, TT], [E, E], [1, E]), ALU.mult))
            link(v.tensor_tensor(gt, gt, eq, ALU.add))
            link(v.tensor_reduce(rank, pat(gt, 0, [E, TT * E], [1, E]), AX.X, ALU.add))
            link(v.tensor_scalar(selm, rank, 1.5, None, ALU.is_lt))
            dve.wait_ge(s["d_rc"], 16)
            v.tensor_tensor(pat(selr, 0, [E, TT], [1, E]), pat(selm, 0, [E, TT], [1, E]),
                            pat(rcb, RB_REAL, [1, TT], [0, E]), ALU.mult).then_inc(s["sel_set"], 1)
            link(v.tensor_reduce(mx5, pat(lg, 0, [8, TT], [1, E]), AX.X, ALU.max))
            v.tensor_tensor(pat(ex, 0, [E, TT], [1, E]), pat(lg, 0, [8, TT], [1, E]),
                            pat(mx5, 0, [1, TT], [0, E]), ALU.subtract).then_inc(s["rt_shift"], 1)
            dve.wait_ge(s["rt_exp"], 1)
            link(v.tensor_tensor(ex, ex, selm, ALU.mult))
            link(v.tensor_reduce(sm5, pat(ex, 0, [E, TT], [1, E]), AX.X, ALU.add))
            link(v.reciprocal(sm5, sm5))
            v.memset(pat(comb, E, [8, TT]), 1.0).then_inc(s["comb_set"], 1)
            v.tensor_tensor(pat(comb, 0, [8, TT], [1, E]), pat(ex, 0, [E, TT], [1, E]),
                            pat(sm5, 0, [1, TT], [0, E]), ALU.mult).then_inc(s["comb_set"], 1)
            dve.wait_ge(s["comb_set"], 2)
            dve.wait_ge(s["pos_mm"], 1)
            link(v.memset(slot, -1.0))
            link(v.scalar_tensor_tensor(out=pat(slot, 0, [8, TT], [1, E]), in0=pat(bank(0), 64, [8, TT], [1, E]),
                                        scalar=1.0, in1=pat(selr, 0, [E, TT], [1, E]), op0=ALU.add, op1=ALU.mult))
            link(v.tensor_scalar(pat(slot, 0, [8, TT], [1, E]), pat(slot, 0, [8, TT], [1, E]),
                                 -1.0, None, ALU.add))
            link(v.tensor_reduce(count, bank(0, E, 128), AX.X, ALU.max))
            v.tensor_copy(count_i[:], count).then_inc(s["count_set"], 1)
            dve.wait_ge(s["xt_hi"], 2)
            sub(xt_l, pat(bank(1), 0, [1, TT * D]), xt_h).then_inc(s["xt_lo"], 1)
            for i in range(2):
                v.memset(prod_b[:, i * NC:(i + 1) * NC], 0.0).then_inc(s["gate_mul"], 1)
            expert_low(2, 0)

            def dense_expert(e):
                for u in range(16):
                    dve.wait_ge(s["silu_ok"], e * 16 + (u + 1))
                    dve.wait_ge(s["weighted"], e * 16 + (u + 1))
                    r = slice((u % 2) * NC, (u % 2 + 1) * NC)
                    v.tensor_tensor(prod_b[:, r], silu_b[:, r], bank(2 * (u % 2) + 1, NC),
                                    ALU.mult).then_inc(s["gate_mul"], 1)

            dense_expert(0)
            expert_low(0, 1)
            expert_low(1, 1)
            dve.wait_ge(s["count_set"], 1)
            with dve.If(dve.value_load(count_i[0:1, 0:1]) <= SLOTS):
                LINKS = 3

                def columns(x, n):
                    def glink(ins, j):
                        ins.then_inc(s["g_chain"], 1)
                        dve.wait_ge(s["g_chain"], n + j)
                    v.tensor_copy(slot_c[:, 0:TT].unsqueeze(2), slot_at(x))
                    glink(v.tensor_copy(comb_c[:, 0:TT].unsqueeze(2), comb_at(x)), 1)
                    v.tensor_copy(slot_r[:, 0:TT], slot_c[:, 0:TT])
                    glink(v.tensor_copy(pat(cw_r, 0, [2, TT]), comb_c[:, 0:TT]), 2)
                    glink(v.tensor_tensor(pat(cw_r, 1, [2, TT]), comb_c[:, 0:TT],
                                          pat(cw_r, 0, [2, TT]).bitcast(F32), ALU.subtract), 3)
                    for t in range(TT):
                        w = v.tensor_scalar(pg[:, t * SLOTS:(t + 1) * SLOTS], rcb[:, RB_IOTA:RB_IOTA + SLOTS],
                                            slot_c[:, t:t + 1], None, ALU.is_equal)
                    w.then_inc(s["g_pg"], 1)

                def slot_at(x):
                    return slot.rearrange("p (t e) -> p t e", e=8)[:, :, bass.ds(x, 1)]

                def comb_at(x):
                    return comb.rearrange("p (t e) -> p t e", e=8)[:, :, bass.ds(x, 1)]

                columns(0, 0)
                v.memset(pt.bitcast(F32), 0.0).then_inc(s["g_pt"], 1)
                dve.wait_ge(s["gu_mm"], 16)
                v.memset(y_h.bitcast(F32), 0.0).then_inc(s["g_yh"], 1)
                v.memset(y_l.bitcast(F32), 0.0).then_inc(s["g_yl"], 1)
                dve.wait_ge(s["g_gath"], 1)
                v.tensor_copy(xg_l, bank(1)).then_inc(s["g_xl"], 1)

                def gathered_expert(e, final):
                    x = e - 1

                    def gate(i):
                        dve.wait_ge(s["g_silu"], x * 4 + (i + 1))
                        b = 2 if i == 2 else 0
                        v.tensor_tensor(pat(prod_g, (i % 2) * G, [SLOTS, 2], [1, SLOTS]),
                                        pat(silu_g, (i % 2) * G, [SLOTS, 2], [1, SLOTS]),
                                        pat(bank(b), SLOTS, [512, 2], [1, SLOTS]), ALU.mult).then_inc(s["g_mul"], 1)

                    def low(i):
                        dve.wait_ge(s["g_hi"], x * 4 + (i + 1))
                        sub(gh_l[:, i * G:(i + 1) * G], prod_g[:, (i % 2) * G:(i % 2 + 1) * G],
                            gh_h[:, i * G:(i + 1) * G]).then_inc(s["g_lo"], 1)

                    gate(0)
                    low(0)
                    dve.wait_ge(s["g_row"], x + 1)
                    v.tensor_reduce(cw_slot, pat(bank(3), 256, [2, ST], [1, 2]), AX.X, ALU.add)
                    for st in range(ST):
                        w = v.tensor_scalar(pt[:, st * N:(st + 1) * N], pat(bank(2), 0, [1, N]),
                                            rcb[:, RB_PART + st:RB_PART + st + 1], None, ALU.is_equal)
                    w.then_inc(s["g_pt"], 1)
                    gate(1)
                    if not final:
                        columns(e, LINKS * e)
                    low(1)
                    gate(2)
                    low(2)
                    gate(3)
                    if not final:
                        expert_low(0, e + 1)
                    low(3)
                    if not final:
                        expert_low(1, e + 1)
                        dve.wait_ge(s["g_gath"], x + 2)
                        v.tensor_copy(xg_l, bank(1)).then_inc(s["g_xl"], 1)
                    dve.wait_ge(s["g_pt"], x + 2)
                    for st in range(ST):
                        r = slice(st * D, (st + 1) * D)
                        dve.wait_ge(s["g_yh"], x * ST + (st + 2))
                        v.scalar_tensor_tensor(out=y_l[:, r], in0=bank(2 + st, D), scalar=cw_slot[:, st:st + 1],
                                               in1=y_h[:, r].bitcast(F32), op0=ALU.mult,
                                               op1=ALU.subtract).then_inc(s["g_yl"], 1)

                with dve.Fori(1, E) as e:
                    gathered_expert(e, False)
                gathered_expert(E, True)
            with dve.Else():
                expert_low(2, 1)
                for e in range(E):
                    dve.wait_ge(s["cb_mm"], e + 1)
                    b = 2 * (e % 2)
                    v.tensor_copy(cbc[:, e * N:e * N + 512], bank(b)).then_inc(s["cb_ev"], 1)
                    v.tensor_copy(cbc[:, e * N + 512:(e + 1) * N], bank(b + 1, N - 512)).then_inc(s["cb_ev"], 1)
                dense_expert(1)
                with dve.Fori(2, NX) as e:
                    for p in range(3):
                        expert_low(p, e)
                    dense_expert(e)
            for i in range(2):
                r = slice(i * KD * D, (i + 1) * KD * D)
                dve.wait_ge(s["l1_hi"], i + 1)
                sub(l1_l[:, r], l1_s[:, r], l1_h[:, r]).then_inc(s["l1_lo"], 1)
            for i, (m, c) in enumerate(MC):
                dve.wait_ge(s["moe_mm"], i + 1)
                v.tensor_copy(hT[:, m * N + c * NC:m * N + (c + 1) * NC], bank(4 + i, NC)).then_inc(s["h_ready"], 1)
            norm(2, plain)
            for i, (m, c) in enumerate(MC):
                r = slice(m * N + c * NC, m * N + (c + 1) * NC)
                dve.wait_ge(s["ra_sig"], i + 1)
                dve.wait_ge(s["ra_mm"], 2 * i + 2)
                v.scalar_tensor_tensor(out=tmp[1][:, r], in0=bank(i, NC), scalar=pb[:, PB_BV + m:PB_BV + m + 1],
                                       in1=tmp[0][:, r], op0=ALU.add, op1=ALU.mult).then_inc(s["scan_chain"], 1)
                dve.wait_ge(s["scan_chain"], i + 1)
            link(v.tensor_scalar(tmp[2], tmp[0], -1.0, 1.0, ALU.mult, ALU.add))
            link(v.memset(pat(tmp[2], 0, [T, KD * B]), 0.0))
            for m in range(KD):
                r = slice(m * N, (m + 1) * N)
                link(v.tensor_tensor_scan(tmp[3][:, r], tmp[2][:, r], tmp[1][:, r], 0.0, ALU.mult, ALU.add))
            for i, (m, c) in enumerate(MC):
                r = slice(m * N + c * NC, m * N + (c + 1) * NC)
                v.tensor_tensor(hT[:, r], hT[:, r], tmp[3][:, r], ALU.add).then_inc(s["h_ready"], 1)

            XW = B * (T + 1)
            link(v.memset(pat(xnf[:], 0, [T + 1, KD * B]), 0.0))

            def spread(c):
                return [(pat(xnf[:], m * XW + c * BC * (T + 1) + 1, [T + 1, BC], [1, T]),
                         pat(xc[:], m * N + c * NC, [T, BC], [1, T]),
                         pat(rstd[:], c * NC, [T, BC], [1, T])) for m in range(KD)]

            norm(3, spread, lo=False)
            dve.wait_ge(s["l1_lo"], 5)
            link(v.tensor_scalar(small[:, 4:8], pb[:, PB_MUR:PB_MUR + 4], -1.0, 1.0, ALU.mult, ALU.add))
            dve.wait_ge(s["ln_xn"], 10)
            for k in range(2):
                for m in range(KD):
                    x_t = pat(xnf[:], m * XW + 1, [T + 1, B], [1, T])
                    x_p = pat(xnf[:], m * XW, [T + 1, B], [1, T])
                    j = 2 * k + m
                    o1 = pat(tmp[4], m * N, [T, B], [1, T])
                    link(v.tensor_scalar(o1, x_p, small[:, 4 + j:5 + j], None, ALU.mult))
                    v.scalar_tensor_tensor(out=pat(tmp[2 + k], m * N, [T, B], [1, T]), in0=x_t,
                                           scalar=pb[:, PB_MUR + j:PB_MUR + j + 1], in1=o1,
                                           op0=ALU.mult, op1=ALU.add).then_inc(s["mix_ok"], 1)
                    dve.wait_ge(s["mix_ok"], j + 1)
            for k in range(2):
                dh = (xh[:, 0:KD * N], xk_h)[k]
                dl = (xl[:, 0:KD * N], xk_l)[k]
                for c in range(C):
                    dve.wait_ge(s["mix_hi"], 2 * k + c + 1)
                    sub(chunk(dl, c), chunk(tmp[2 + k], c), chunk(dh, c)).then_inc(s["mix_lo"], 1)
            for c in range(C):
                dve.wait_ge(s["k_relu"], 2 * c + 2)
                v.tensor_tensor(chunk(tmp[4], c), chunk(tmp[1], c), chunk(tmp[1], c), ALU.mult).then_inc(s["k_sq"], 1)
            for c in range(C):
                dve.wait_ge(s["k_hi"], c + 1)
                sub(chunk(xl[:], c), chunk(tmp[4], c), chunk(xh[:], c)).then_inc(s["k_lo"], 1)
            dve.wait_ge(s["r_sig"], 4)
            for i, (m, c) in enumerate(MC):
                r = slice(m * N + c * NC, m * N + (c + 1) * NC)
                dve.wait_ge(s["vv_mm"], i + 1)
                link(v.tensor_tensor(tmp[2][:, r], tmp[0][:, r], bank(4 + i, NC), ALU.mult))
                v.tensor_tensor(tmp[5][:, r], hT[:, r], tmp[2][:, r], ALU.add).then_inc(s["out_ok"], 1)

        @block.tensor
        def _(pe):
            mm = nc.tensor.matmul

            def three(o, a_h, a_l, b_h, b_l, start, stop):
                mm(o, a_h, b_h, start=start, stop=False)
                mm(o, a_h, b_l, start=False, stop=False)
                return mm(o, a_l, b_h, start=False, stop=stop)

            pe.wait_ge(s["d_const"], 16)
            pe.wait_ge(s["d_table"], 16)
            for k in range(T):
                lhs = cb[0:BUCKETS, CB_OH + T - 1 - k:CB_OH + 2 * T - 1 - k]
                w = mm(ps[0:T, k // 32, (k % 32) * HEADS:(k % 32 + 1) * HEADS], lhs, tb[0:BUCKETS, :],
                       start=True, stop=True)
            w.then_inc(s["bias_mm"], 1)
            for k in range(KF):
                pe.wait_ge(s["tok_lo"], k // 2 + 2)
                for i, (m, c) in enumerate(MC):
                    w_ = slice(k * D + m * P, k * D + (m + 1) * P)
                    x_ = slice(k * NP * B + c * NPC, k * NP * B + (c + 1) * NPC)
                    w = three(bank(4 + i, NPC), wh[:, w_], wl[:, w_], patch_h[:, x_], patch_l[:, x_],
                              k == 0, k == KF - 1)
                    if k == KF - 1:
                        w.then_inc(s["tok_mm"], 1)

            def norm(L):
                if L == 0:
                    pe.wait_ge(s["const_set"], 3)
                    pe.wait_ge(s["cls_set"], 1)
                    pe.wait_ge(s["bias_ev"], 2)
                for c in range(C):
                    pe.wait_ge(s["h_ready"], 4 * L + 2 * c + 2)
                    for k in range(KD):
                        w = mm(bank(c, NC), ones[:], hT[:, k * N + c * NC:k * N + (c + 1) * NC],
                               start=(k == 0), stop=(k == KD - 1))
                    w.then_inc(s["ln_mean"], 1)
                for c in range(C):
                    pe.wait_ge(s["ln_sq"], 2 * L + c + 1)
                    for k in range(KD):
                        w = mm(bank(2 + c, NC), ones[:], sq[:, k * N + c * NC:k * N + (c + 1) * NC],
                               start=(k == 0), stop=(k == KD - 1))
                    w.then_inc(s["ln_var"], 1)

            norm(0)
            pe.wait_ge(s["ln_lo"], 2)
            pe.wait_ge(w_lo[2], 1)
            for i in range(2 * PAIRS):
                pair, n = i // 2, i % 2
                if i >= 4:
                    pe.wait_ge(s["v_ev_act"] if i % 2 == 0 else s["v_ev_dve"], (i - 4) // 2 + 1)
                for k in range(KD):
                    x_h, x_l = (x[:, k * NT + pair * T2:k * NT + (pair + 1) * T2] for x in (xh, xl))
                    w_ = slice(2 * W1 + k * INNER + n * 512, 2 * W1 + k * INNER + (n + 1) * 512)
                    w = three(ps[0:T2, i % 4, :], x_h, x_l, wh[:, w_], wl[:, w_], k == 0, k == KD - 1)
                w.then_inc(s["v_mm"], 1)

            def project(hp, c, j):
                n = 2 * hp + c
                if n >= 1:
                    pe.wait_ge(s["q_ev"] if j == 0 else s["k_ev"], n)
                for k in range(KD):
                    w_ = slice(j * W1 + k * INNER + hp * P, j * W1 + k * INNER + (hp + 1) * P)
                    x_ = slice(k * NT + c * NC, k * NT + (c + 1) * NC)
                    w = three(bank(6 + j, NC), wh[:, w_], wl[:, w_], xh[:, x_], xl[:, x_], k == 0, k == KD - 1)
                w.then_inc(s["q_mm"] if j == 0 else s["k_mm"], 1)

            pe.wait_ge(w_lo[0], 1)
            pe.wait_ge(w_lo[1], 1)
            for c in range(C):
                for j in range(2):
                    project(0, c, j)
            pe.wait_ge(s["v_ev_act"], PAIRS)
            pe.wait_ge(s["v_ev_dve"], PAIRS)
            for t in range(2 * HP + 2):
                if t < 2 * HP:
                    hp, half = t // 2, t % 2
                    pe.wait_ge(s["q_ev"], 2 * hp + 2)
                    pe.wait_ge(s["k_ev"], 2 * hp + 2)
                    if t >= 1:
                        pe.wait_ge(s["sc_ev"], t)
                    for g in range(8):
                        pair, hd = PPC * half + g // 2, g % 2
                        r = slice(64 * hd, 64 * hd + 64)
                        w = mm(ps[0:T2, hd, (g // 2) * T2:(g // 2 + 1) * T2],
                               qb[r, (hp % 2) * NT + pair * T2:(hp % 2) * NT + (pair + 1) * T2],
                               kb[r, (hp % 2) * N + pair * T2:(hp % 2) * N + (pair + 1) * T2],
                               start=True, stop=True)
                    w.then_inc(s["sc_mm"], 1)
                if t >= 2:
                    u = t - 2
                    pe.wait_ge(s["normed"], u + 1)
                    if u >= 1:
                        pe.wait_ge(s["pt_ev"], u)
                    for g in range(8):
                        o = (u % 3) * SC + g * T2
                        w = nc.tensor.transpose(ps[0:T2, 2 + g // 4, (g % 4) * T2:(g % 4 + 1) * T2],
                                                sreg[0:T2, o:o + T2], ident[0:T2, 0:T2])
                    w.then_inc(s["pt_mm"], 1)
                if t + 2 < 2 * HP:
                    project(t // 2 + 1, t % 2, 0)
                    project(t // 2 + 1, t % 2, 1)
                if t >= 2:
                    hp, half = u // 2, u % 2
                    pe.wait_ge(s["pt_ev"], u + 1)
                    if u >= 2:
                        pe.wait_ge(s["ctx_lo"], u - 1)
                    for g in range(8):
                        pair, hd = PPC * half + g % 4, g // 4
                        vo = pair * INNER + hp * P + hd * DH
                        po = (u % 2) * SC + g * T2
                        w = mm(ps[64 * hd:64 * hd + 64, 4 + u % 2, (g % 4) * T2:(g % 4 + 1) * T2],
                               v_all[0:T2, vo:vo + DH], ptb[0:T2, po:po + T2], start=True, stop=True)
                    w.then_inc(s["ctx_mm"], 1)
            pe.wait_ge(w_lo[2], 2)
            pe.wait_ge(s["ctx_lo"], 2 * HP)
            for i, (m, c) in enumerate(MC):
                for k in range(HP):
                    w_ = slice(2 * W1 + k * D + m * P, 2 * W1 + k * D + (m + 1) * P)
                    x_ = slice(k * N + c * NC, k * N + (c + 1) * NC)
                    w = three(bank(4 + i, NC), wh[:, w_], wl[:, w_], ctx_h[:, x_], ctx_l[:, x_], k == 0, k == HP - 1)
                w.then_inc(s["wo_mm"], 1)
            norm(1)
            pe.wait_ge(s["ln_lo"], 4)
            for t in range(TT):
                for k in range(KD):
                    w = mm(ps[:, 0, t * 8:t * 8 + E], xnf[:, k * NT + t * P:k * NT + (t + 1) * P],
                           pb[:, PB_WR + k * E:PB_WR + (k + 1) * E], start=(k == 0), stop=(k == KD - 1))
            w.then_inc(s["rt_mm"], 1)
            for t in range(TT):
                for k in range(KD):
                    o = (t * KD + k) * P
                    w = nc.tensor.transpose(ps[:, 1 + o // 512, o % 512:o % 512 + P],
                                            xnf[:, k * NT + t * P:k * NT + (t + 1) * P], ident)
            w.then_inc(s["xt_mm"], 1)
            pe.wait_ge(s["sel_set"], 1)
            pe.wait_ge(s["d_rc"], 16)
            selr = route[:, 690:725]
            tri, one = rcb[:, RB_TRI:RB_TRI + P], rcb[:, RB_ONES:RB_ONES + P]
            for t in range(TT + 1):
                for j in range(min(t + 1, TT)):
                    w = mm(ps[:, 0, 64 + t * 8:64 + t * 8 + E] if t < TT else bank(0, E, 128), tri if j == t else one,
                       selr[:, j * E:(j + 1) * E], start=(j == 0),
                           stop=(j == min(t, TT - 1)))
            w.then_inc(s["pos_mm"], 1)
            for i, (m, c) in enumerate(MC):
                mm(bank(4 + i, NC), ident, hT[:, m * N + c * NC:m * N + (c + 1) * NC],
                   start=True, stop=False).then_inc(s["dn_mm"], 1)
            def dense_expert(e):
                pe.wait_ge(w_lo[0], e + (WBASE[0] + 1))
                pe.wait_ge(w_lo[1], e + (WBASE[1] + 1))

                def gate_up(u):
                    c, j = u // KH, u % KH
                    pe.wait_ge(s["gate_mul"], e * 16 + (u + 1))
                    for q in range(2):
                        for k in range(KD):
                            w_ = slice(q * W1 + k * HID + j * P, q * W1 + k * HID + (j + 1) * P)
                            x_ = slice(k * NT + c * NC, k * NT + (c + 1) * NC)
                            w = three(bank(2 * (u % 2) + q, NC), wh[:, w_], wl[:, w_], xh[:, x_], xl[:, x_],
                                      k == 0, k == KD - 1)
                    w.then_inc(s["gu_mm"], 1)

                def down(u):
                    c, j = u // KH, u % KH
                    pe.wait_ge(s["hid_lo"], e * 16 + (u + 3))
                    x_ = slice((u % 4) * NC, (u % 4 + 1) * NC)
                    for m in range(KD):
                        w_ = slice(2 * W1 + j * D + m * P, 2 * W1 + j * D + (m + 1) * P)
                        w = three(bank(4 + 2 * c + m, NC), wh[:, w_], wl[:, w_], hid_h[:, x_], hid_l[:, x_],
                                  False, False)
                    w.then_inc(s["dn_mm"], 1)

                gate_up(0)
                gate_up(1)
                for u in range(2, 16):
                    gate_up(u)
                    if u == 2:
                        pe.wait_ge(w_lo[2], e + (WBASE[2] + 1))
                    down(u - 2)
                down(14)
                down(15)

            dense_expert(0)
            pe.wait_ge(s["count_set"], 1)
            with pe.If(pe.value_load(count_i[0:1, 0:1]) <= SLOTS):
                def gather(n):
                    pe.wait_ge(s["g_pg"], n)
                    for part, src in ((0, xt_h), (1, xt_l)):
                        for m in range(KD):
                            for t in range(TT):
                                w = mm(ps[:, part, m * SLOTS:(m + 1) * SLOTS],
                                       src[:, t * D + m * P:t * D + (m + 1) * P],
                                       pg[:, t * SLOTS:(t + 1) * SLOTS], start=(t == 0), stop=(t == TT - 1))
                    w.then_inc(s["g_gath"], 1)

                def scatter(x):
                    pe.wait_ge(s["g_yl"], x * ST + 1)
                    pe.wait_ge(s["g_yh"], x * ST + 1)
                    pe.wait_ge(s["g_pt"], x + 1)
                    for i, (m, c) in enumerate(MC):
                        for st in range(ST):
                            for y in (y_h, y_l):
                                w = mm(bank(4 + i, NC), y[:, st * D + m * P:st * D + (m + 1) * P],
                                       pt[:, st * N + c * NC:st * N + (c + 1) * NC], start=False, stop=False)
                    w.then_inc(s["g_scat"], 1)

                def gathered_expert(e, final):
                    x = e - 1

                    def gate_up(i):
                        b = 2 if i == 2 else 0
                        for jj in range(2):
                            j = 2 * i + jj
                            for q in range(2):
                                for k in range(KD):
                                    w_ = slice(q * W1 + k * HID + j * P, q * W1 + k * HID + (j + 1) * P)
                                    x_ = slice(k * SLOTS, (k + 1) * SLOTS)
                                    w = three(ps[:, b + jj, q * SLOTS:(q + 1) * SLOTS], wh[:, w_], wl[:, w_],
                                              xg_h[:, x_], xg_l[:, x_], k == 0, k == KD - 1)
                        w.then_inc(s["g_mm"], 1)

                    def down(i):
                        pe.wait_ge(s["g_lo"], x * 4 + (i + 1))
                        for j in (2 * i, 2 * i + 1):
                            w_ = slice(2 * W1 + j * D, 2 * W1 + (j + 1) * D)
                            for st in range(ST):
                                h_ = slice(j * SLOTS + st * P, j * SLOTS + (st + 1) * P)
                                w = three(bank(2 + st, D), gh_h[:, h_], gh_l[:, h_], wh[:, w_], wl[:, w_],
                                          j == 0, j == KH - 1)
                        return w

                    pe.wait_ge(w_lo[0], e + (WBASE[0] + 1))
                    pe.wait_ge(w_lo[1], e + (WBASE[1] + 1))
                    pe.wait_ge(s["g_xh"], x + 1)
                    pe.wait_ge(s["g_xl"], x + 1)
                    gate_up(0)
                    scatter(x)
                    for t in range(TT):
                        mm(ps[:, 2 + t // 4, (t % 4) * P:(t % 4 + 1) * P], pat(slot_r, t, [0, P]), ident_r,
                           start=True, stop=True)
                    for st in range(ST):
                        for t in range(TT):
                            w = mm(bank(3, 2, 256 + 2 * st), pg[:, t * SLOTS + st * P:t * SLOTS + (st + 1) * P],
                                   cw_r[:, 2 * t:2 * t + 2], start=(t == 0), stop=(t == TT - 1))
                    w.then_inc(s["g_row"], 1)
                    pe.wait_ge(s["g_mul"], x * 4 + 1)
                    gate_up(1)
                    pe.wait_ge(s["g_pt"], x + 2)
                    gate_up(2)
                    pe.wait_ge(s["g_mul"], x * 4 + 2)
                    gate_up(3)
                    pe.wait_ge(s["g_mul"], x * 4 + 3)
                    pe.wait_ge(w_lo[2], e + (WBASE[2] + 1))
                    for i in range(3):
                        down(i)
                    if not final:
                        pe.wait_ge(s["g_mul"], x * 4 + 4)
                        gather(x + 2)
                    down(3).then_inc(s["g_y"], 1)

                pe.wait_ge(s["xt_lo"], 1)
                pe.wait_ge(s["gate_mul"], 2 + 16)
                gather(1)
                with pe.Fori(1, E) as e:
                    gathered_expert(e, False)
                gathered_expert(E, True)
                scatter(E)
            with pe.Else():
                pe.wait_ge(s["gate_mul"], 2 + 16)
                pe.wait_ge(s["comb_set"], 2)
                for e in range(E):
                    if e >= 2:
                        pe.wait_ge(s["cb_ev"], 2 * (e - 1))
                    for t in range(TT):
                        w = mm(ps[:, 2 * (e % 2) + t // 4, (t % 4) * P:(t % 4 + 1) * P],
                               pat(comb, t * 8 + e, [0, P]), ident, start=True, stop=True)
                    w.then_inc(s["cb_mm"], 1)
                pe.wait_ge(s["cb_ev"], 2 * E)
                with pe.Fori(1, NX) as e:
                    dense_expert(e)
            for i in range(4):
                mm(bank(4 + i, P), zero[:], ident, start=False, stop=True).then_inc(s["moe_mm"], 1)
            norm(2)

            def last(w, k, m):
                return slice((w * KD + k) * D + m * P, (w * KD + k) * D + (m + 1) * P)

            pe.wait_ge(s["ln_lo"], 6)
            pe.wait_ge(s["l1_lo"], 5)
            for i, (m, c) in enumerate(MC):
                for w_i, b in ((0, 4 + i), (1, i)):
                    for k in range(KD):
                        x_ = slice(k * NT + c * NC, k * NT + (c + 1) * NC)
                        w = three(bank(b, NC), l1_h[:, last(w_i, k, m)], l1_l[:, last(w_i, k, m)],
                                  xh[:, x_], xl[:, x_], k == 0, k == KD - 1)
                    w.then_inc(s["ra_mm"], 1)
            norm(3)
            pe.wait_ge(s["mix_lo"], 4)
            for i, (m, c) in enumerate(MC):
                for w_i, b, a_h, a_l in ((2, 4 + i, xh, xl), (3, i, xk_h, xk_l)):
                    for k in range(KD):
                        x_ = slice(k * N + c * NC, k * N + (c + 1) * NC)
                        w = three(bank(b, NC), l1_h[:, last(w_i, k, m)], l1_l[:, last(w_i, k, m)],
                                  a_h[:, x_], a_l[:, x_], k == 0, k == KD - 1)
                    w.then_inc(s["rk_mm"], 1)
            for i, (m, c) in enumerate(MC):
                pe.wait_ge(s["r_sig"], i + 1)
                pe.wait_ge(s["k_lo"], c + 1)
                for k in range(KD):
                    x_ = slice(k * N + c * NC, k * N + (c + 1) * NC)
                    w = three(bank(4 + i, NC), l1_h[:, last(4, k, m)], l1_l[:, last(4, k, m)],
                              xh[:, x_], xl[:, x_], k == 0, k == KD - 1)
                w.then_inc(s["vv_mm"], 1)


def bucket_onehot():
    rp = 36 - np.arange(100)
    half, exact = BUCKETS // 2, BUCKETS // 4
    a = np.abs(rp)
    far = exact + (np.log(np.maximum(a, 1).astype(np.float32) / np.float32(exact))
                   / np.float32(math.log(128 / exact)) * np.float32(half - exact)).astype(np.int32)
    bucket = (rp > 0) * half + np.where(a < exact, a, np.minimum(far, half - 1))
    oh = np.zeros((P, 100), np.float32)
    for j in range(73):
        oh[bucket[j], j] = 1.0
    return oh


def routing_constants():
    p, f = np.arange(P), np.float32
    return np.concatenate([
        np.tile(np.arange(SLOTS), (P, 1)).astype(f),
        (p[:, None] + P * np.arange(ST)[None, :]).astype(f),
        (p[:, None] < p[None, :]).astype(f),
        np.ones((P, P), f),
        (p[:, None] + P * np.arange(TT)[None, :] < N).astype(f)], axis=1)


def kernel(**inputs):
    import concourse.bacc as bacc
    from concourse.bass_utils import run_bass_kernel_spmd

    x = {k: np.asarray(v) for k, v in inputs.items()}

    def tiles(a):
        return np.ascontiguousarray(a.reshape(-1, P, a.shape[-1]).transpose(1, 0, 2).reshape(P, -1))

    im = x["x"].reshape(B, 3, GRID, PATCH, GRID, PATCH).transpose(1, 3, 5, 0, 2, 4).reshape(FP, B * NP)
    cols = np.concatenate([x["L0_tok_position_embeddings"][0].T, x["L0_tok_class_token"][0].T], axis=1)
    per = [tiles(cols[:, :T]), tiles(cols[:, T:])]
    for n in ("L0_tok_b_lin", "L1_attn_b_delta", "L1_attn_b_value", "L1_ffn_mu_r", "L1_ffn_mu_k"):
        per.append(tiles(x[n][:, None]))
    per.append(tiles(x["L0_ffn_router_w"].T))
    tri = np.tile((np.arange(E)[None, :] < np.arange(E)[:, None]).astype(np.float32).reshape(1, -1), (P, 1))
    last = [tiles(x[n].T) for n in ("L1_attn_W_delta", "L1_attn_W_value", "L1_ffn_W_r", "L1_ffn_W_k", "L1_ffn_W_v")]
    arrays = {
        "patches": tiles(im),
        "w_lin": tiles(x["L0_tok_W_lin"].T),
        "par": np.concatenate(per, axis=1),
        "const": np.concatenate([np.eye(P, dtype=np.float32), tri, bucket_onehot()], axis=1),
        "table": x["L0_attn_rel_bias_table"],
        "w_q": x["L0_attn_w_q"], "w_k": x["L0_attn_w_k"], "w_v": x["L0_attn_w_v"], "w_o": x["L0_attn_w_o"],
        "w_gate": np.concatenate([x["L0_ffn_sw_gate"], x["L0_ffn_w_gate"]]),
        "w_up": np.concatenate([x["L0_ffn_sw_up"], x["L0_ffn_w_up"]]),
        "w_down": np.concatenate([x["L0_ffn_sw_down"], x["L0_ffn_w_down"]]),
        "w_l1": np.concatenate(last, axis=1),
        "rconst": routing_constants(),
    }
    nc = bacc.Bacc("TRN2", target_bir_lowering=False, num_devices=1)
    feed, args = {}, []
    for name, a in arrays.items():
        a = np.ascontiguousarray(a)
        feed[f"in_{name}"] = a
        args.append(nc.dram_tensor(f"in_{name}", a.shape, mybir.dt.from_np(a.dtype), kind="ExternalInput").ap())
    o = nc.dram_tensor("out_h", (D, N), F32, kind="ExternalOutput").ap()
    vit_tower(nc, *args, o)
    r = run_bass_kernel_spmd(nc, [feed], core_ids=[0])
    return np.ascontiguousarray(r.results[0]["out_h"].reshape(D, B, T).transpose(1, 2, 0))
```

```python
import math
from contextlib import ExitStack

import numpy as np

import concourse.bass as bass
from concourse import mybir

F32 = mybir.dt.float32
F32R = mybir.dt.float32r
ACT = mybir.ActivationFunctionType
ALU = mybir.AluOpType
AX = mybir.AxisListType

P = 128
B = 16
PATCH = 16
GRID = 96 // PATCH
NP = GRID * GRID
T = NP + 1
N = B * T
D = 256
KD = D // P
FP = 3 * PATCH * PATCH
KF = FP // P
HEADS = 16
DH = 64
INNER = HEADS * DH
HP = INNER // P
HID = 1024
KH = HID // P
E = 7
NX = E + 1
C = 2
NC = N // C
BC = B // C
NPC = BC * NP
PAIRS = B // 2
PPC = PAIRS // C
NT = 640
TT = NT // P
T2 = 2 * T
SC = 2 * PPC * T2
MASK = -1e30
SLOTS = 256
ST = SLOTS // P
W1 = KD * HID
BUCKETS = 32
EPS = 1e-5

MC = [(0, 0), (1, 0), (0, 1), (1, 1)]

PB_POS, PB_CLS, PB_BLIN, PB_BD, PB_BV, PB_MUR, PB_MUK, PB_WR = 0, 74, 76, 78, 80, 82, 84, 86
PB = PB_WR + KD * E
CB_ID, CB_TRI, CB_OH = 0, P, P + E * E
CB = CB_OH + 100
RB_IOTA, RB_PART, RB_TRI, RB_ONES = 0, SLOTS, SLOTS + ST, SLOTS + ST + P
RB_REAL = RB_ONES + P
RB = RB_REAL + TT


def pat(a, off, *dims):
    return bass.AP(a.tensor, a.offset + off, [list(a.ap[0])] + [list(d) for d in dims])


def vit_tower(nc, patches, w_lin, par, const, table, w_q, w_k, w_v, w_o, w_gate, w_up, w_down, w_l1, rconst, out):
    ctx = ExitStack()
    with ctx:
        def sb(name, cols, dt=F32):
            return ctx.enter_context(nc.sbuf_tensor(name, [P, cols], dt))

        def sem(name):
            return ctx.enter_context(nc.semaphore(name))

        ws = sb("w_stage", 3 * W1)
        vreg = sb("v_region", PAIRS * INNER)
        hT = sb("hT", KD * N)
        xnf = sb("xn_f32", KD * NT)
        xc = sb("x_centred", KD * N)
        sq = sb("x_squared", KD * N)
        rstd = sb("rstd", N)
        eps = sb("eps", 1)
        qb = sb("q_buf", 2 * NT)
        kb = sb("k_buf", 2 * N)
        sreg = sb("s_region", 3072)
        ptb = sb("probs_T", 2 * 592)
        bias = sb("bias_pair", HEADS * T2)
        stat = sb("softmax_stats", 3 * 3 * 8)
        pb = sb("params", PB)
        cb = sb("consts", CB)
        tb = sb("bias_table", HEADS)
        ones = sb("ones_over_d", P)
        zero = sb("zeros", P)
        small = sb("small", 24)
        wh = sb("w_hi", 3 * W1, F32R)
        wl = sb("w_lo", 3 * W1, F32R)
        cr = sb("c_region", 2 * HP * N, F32R)
        xh = sb("xn_hi", KD * NT, F32R)
        xl = sb("xn_lo", KD * NT, F32R)
        ps = ctx.enter_context(nc.psum_tensor("ps", [P, 8, 512], F32))

        PW = KF * NPC * C
        patch_s = vreg[:, 0:PW]
        wlin_s = vreg[:, PW:PW + KF * D]
        patch_h, patch_l = cr[:, 0:PW], cr[:, PW:2 * PW]
        v_all = vreg[:, :]
        v_tok = [sreg[:, t * INNER:(t + 1) * INNER] for t in range(3)] + [sq[:, 0:INNER], xc[:, 0:INNER]]
        V_RUNS = []
        cuts = sorted({*range(0, N, P), *range(0, N, T2), N})
        for lo_, hi_ in zip(cuts, cuts[1:]):
            V_RUNS.append((lo_ // P, lo_ % P, lo_ // T2, lo_ % T2, hi_ - lo_))
        V_RUNS_C0 = sum(r[2] < PPC for r in V_RUNS)
        ctx_h, ctx_l = cr[:, 0:HP * N], cr[:, HP * N:2 * HP * N]
        HR = 4 * NC
        hid_h, hid_l = cr[:, 0:HR], cr[:, HR:2 * HR]
        xk_h, xk_l = cr[:, 0:KD * N], cr[:, KD * N:2 * KD * N]
        gh_h, gh_l = cr[:, 0:KH * SLOTS], cr[:, KH * SLOTS:2 * KH * SLOTS]
        r0 = 2 * KH * SLOTS
        xt_h, xt_l = cr[:, r0:r0 + TT * D], cr[:, r0 + TT * D:r0 + 2 * TT * D]
        r0 += 2 * TT * D
        pg = cr[:, r0:r0 + TT * SLOTS]
        r0 += TT * SLOTS
        pt = cr[:, r0:r0 + ST * N]
        r0 += ST * N
        tri_r, one_r, sel_r = pt[:, 0:P], pt[:, P:2 * P], pt[:, 2 * P:2 * P + 8 * TT]
        slot_r, cw_r, ident_r = cr[:, r0:r0 + 8], cr[:, r0 + 8:r0 + 24], cr[:, r0 + 24:r0 + 24 + P]
        G = KD * SLOTS
        xg_h, xg_l = xh[:, 0:G], xl[:, 0:G]
        y_h, y_l = xh[:, G:G + ST * D], xl[:, G:G + ST * D]
        silu_g, prod_g = sreg[:, 0:2 * G], sreg[:, 2 * G:4 * G]
        L1W = 5 * KD * D
        XW = B * (T + 1)
        l1_s = vreg[:, 0:L1W]
        l1_h, l1_l = wh[:, 0:L1W], wl[:, 0:L1W]
        cbc = vreg[:, L1W:L1W + E * N]
        rc0 = L1W + 4 * KD * N
        rcb = vreg[:, rc0:rc0 + RB]
        r1 = rc0 + RB
        comb, slot = vreg[:, r1:r1 + 40], vreg[:, r1 + 40:r1 + 80]
        slot_c, comb_c = vreg[:, r1 + 80:r1 + 88], vreg[:, r1 + 88:r1 + 96]
        cw_slot, count = vreg[:, r1 + 96:r1 + 98], vreg[:, r1 + 98:r1 + 99]
        tmp = [vreg[:, o:o + KD * N] for o in [L1W + k * KD * N for k in range(4)] + [0, KD * N]]
        silu_b, prod_b, wprod_b = (sreg[:, k * 2 * NC:(k + 1) * 2 * NC] for k in range(3))
        route = sreg[:, 1800:3072]
        bias_q = ptb[:, 0:HEADS * T]
        cbe = ptb[:, 0:N]
        ident = cb[:, CB_ID:CB_ID + P]

        XT = [(0, 4, 7, 0), (4, 7, 6, P), (7, 10, 7, 0)]
        assert XT[-1][1] == TT * KD
        LG0, POS0, CNT0 = 0, 48, 96

        count_i = ctx.enter_context(nc.sbuf_tensor("count_i", [P, 1], mybir.dt.int32))
        s = {n: sem(n) for n in (
            "d_par d_const d_table d_l1 d_out "
            "const_set pad_set mask_set bias_mm bias_ev d_bias tok_hi tok_lo tok_mm cls_set h_ready "
            "ln_mean ln_xc ln_sq ln_var ln_std ln_rs ln_xn ln_hi ln_lo "
            "d_v0 d_v1 v_mm v_ev_act v_ev_dve q_mm k_mm q_ev k_ev sc_mm sc_ev maxed shifted expd summed recip normed "
            "pt_mm pt_ev ctx_mm ctx_hi ctx_lo wo_mm "
            "d_rc xt_mm xt_hi xt_lo sel_set pos_mm count_set "
            "g_mm g_silu g_mul g_hi g_lo g_row g_pt g_pg g_gath g_xh g_xl g_y g_yh g_yl g_chain "
            "rt_mm rt_shift rt_exp dve_chain comb_set half_hi half_lo half_up back_hi back_lo cb_mm cb_ev "
            "up_lo gu_mm silu_ok gate_mul "
            "weighted cbe_set hid_hi hid_lo dn_mm moe_mm l1_hi l1_lo ra_mm ra_sig "
            "mix_mul mix_ok mix_hi mix_lo mixr_lo rk_mm r_sig k_relu k_sq k_hi k_lo vv_mm gated out_ok out0_ok").split()}
        d_patch = [sem(f"d_patch{i}") for i in range(3)]
        d_w = [sem(f"d_w{i}") for i in range(3)]
        w_hi = [sem(f"w_hi{i}") for i in range(3)]
        w_lo = [sem(f"w_lo{i}") for i in range(3)]
        WBASE = (1, 1, 2)

        def bank(k, cols=512, off=0):
            return ps[:, k, off:off + cols]

        def chunk(a, c, width=N):
            return pat(a, c * NC, [width, KD], [1, NC])

        def half(a, p, k0, k1, j):
            return pat(a[:], p * W1 + k0 * HID + j * (HID // 2), [HID, k1 - k0], [1, HID // 2])

        def qk_bank(n):
            return 4 if n == 1 else 6

        def var_bank(L, c):
            return 6 - 2 * c if L == 1 else 4 + 2 * c

        block = ctx.enter_context(nc.Block())

        @block.sync
        def _(sp):
            for i in range(3):
                for o, x, n in ((wlin_s, w_lin, KF * D // 3), (patch_s, patches, PW // 3)):
                    sp.dma_start(o[:, i * n:(i + 1) * n], x[:, i * n:(i + 1) * n]).then_inc(d_patch[i], 16)
            sp.dma_start(pb[:], par).then_inc(s["d_par"], 16)
            sp.dma_start(cb[:], const).then_inc(s["d_const"], 16)
            sp.dma_start(tb[0:BUCKETS, :], table).then_inc(s["d_table"], 16)

            def part(p):
                return ws[:, p * W1:(p + 1) * W1]

            def rows(w, k):
                return w.rearrange("(k p) n -> p k n", p=P)

            sp.dma_start(part(2).rearrange("p (k n) -> p k n", k=KD), rows(w_v, KD)).then_inc(d_w[2], 16)
            sp.dma_start(part(0).rearrange("p (k n) -> p k n", k=KD), rows(w_q, KD)).then_inc(d_w[0], 16)
            sp.dma_start(part(1).rearrange("p (k n) -> p k n", k=KD), rows(w_k, KD)).then_inc(d_w[1], 16)
            sp.wait_ge(w_lo[2], 1)
            sp.dma_start(part(2).rearrange("p (k n) -> p k n", k=HP), rows(w_o, HP)).then_inc(d_w[2], 16)
            sp.wait_ge(s["bias_ev"], 2)
            sp.wait_ge(s["mask_set"], 1)
            for b2 in range(2):
                sp.dma_start(pat(bias[b2 * T:(b2 + 1) * T, :], b2 * T, [T2, HEADS], [1, T]),
                             bias_q[0:T, :].rearrange("p (h k) -> p h k", h=HEADS)).then_inc(s["d_bias"], 16)
            for t, a, pair, b, n in V_RUNS:
                sp.wait_ge(s["v_ev_act"], t + 1)
                sp.wait_ge(s["v_ev_dve"], t + 1)
                sp.dma_start(v_all[b:b + n, pair * INNER:(pair + 1) * INNER],
                             v_tok[t][a:a + n, :]).then_inc(s[f"d_v{pair // PPC}"], 16)
            with sp.Fori(0, NX) as e:
                for p, w in ((0, w_gate), (1, w_up), (2, w_down)):
                    k = KD if p < 2 else KH
                    sp.wait_ge(w_lo[p], e + WBASE[p])
                    if p == 1:
                        sp.wait_ge(s["up_lo"], e + 1)
                    sp.dma_start(part(p).rearrange("p (k n) -> p k n", k=k),
                                 w[bass.ds(e, 1)].rearrange("o (k p) n -> p (o k) n", p=P)).then_inc(d_w[p], 16)
            for c in range(C):
                if c == 0:
                    sp.wait_ge(s["out0_ok"], 1)
                else:
                    sp.wait_ge(s["out_ok"], KD)
                sp.dma_start(out.rearrange("(m p) n -> p m n", p=P)[:, :, c * NC:(c + 1) * NC],
                             chunk(tmp[5], c)).then_inc(s["d_out"], 16)
            sp.wait_ge(s["d_out"], 16 * C)

        @block.gpsimd
        def _(pool):
            g = nc.gpsimd
            g.memset(ones[:], 1.0 / D).then_inc(s["const_set"], 1)
            g.memset(zero[:], 0.0).then_inc(s["const_set"], 1)
            g.memset(eps[:], EPS).then_inc(s["const_set"], 1)
            for a in (xnf, xh, xl):
                g.memset(pat(a[:], N, [NT, KD], [1, NT - N]).bitcast(F32), 0.0).then_inc(s["pad_set"], 1)
            g.memset(bias[0:T2, :], MASK).then_inc(s["mask_set"], 1)

            def up_low(e):
                r = slice(W1 + W1 // 2, 2 * W1)
                pool.wait_ge(w_hi[1], e + 2)
                g.tensor_tensor(wl[:, r], ws[:, r], wh[:, r].bitcast(F32), ALU.subtract).then_inc(s["up_lo"], 1)

            def down_low(e):
                r = slice(2 * W1, 3 * W1)
                pool.wait_ge(w_hi[2], e + (WBASE[2] + 1))
                g.tensor_tensor(wl[:, r], ws[:, r], wh[:, r].bitcast(F32), ALU.subtract).then_inc(w_lo[2], 1)

            up_low(-1)
            for t in range(2 * HP + 1):
                if t < 2 * HP:
                    pool.wait_ge(s["maxed"], t + 1)
                    sc = pat(sreg[0:T2, :], (t % 3) * SC, [T2, 8], [1, T2])
                    g.tensor_tensor(sc, sc, pat(stat[0:T2, :], (t % 3) * 24, [1, 8], [0, T2]),
                                    ALU.subtract).then_inc(s["shifted"], 1)
                if t >= 1:
                    u = t - 1
                    pool.wait_ge(s["recip"], u + 1)
                    sc = pat(sreg[0:T2, :], (u % 3) * SC, [T2, 8], [1, T2])
                    g.tensor_tensor(sc, sc, pat(stat[0:T2, :], (u % 3) * 24 + 16, [1, 8], [0, T2]),
                                    ALU.mult).then_inc(s["normed"], 1)
            up_low(0)
            down_low(0)
            for j, hi_, lo_ in ((0, s["half_hi"], s["half_up"]), (1, w_hi[1], s["up_lo"])):
                pool.wait_ge(hi_, 2 if j == 0 else 3)
                g.tensor_tensor(half(wl, 1, 1, KD, j), half(ws, 1, 1, KD, j), half(wh, 1, 1, KD, j).bitcast(F32),
                                ALU.subtract).then_inc(lo_, 1)
            pool.wait_ge(s["count_set"], 1)
            with pool.If(pool.value_load(count_i[0:1, 0:1]) <= SLOTS):
                down_low(1)
                with pool.Fori(1, E) as e:
                    up_low(e + 1)
                    down_low(e + 1)
            with pool.Else():
                def dense_expert(e):
                    def weigh(u):
                        pool.wait_ge(s["gate_mul"], e * 16 + (u + 1))
                        pool.wait_ge(s["hid_lo"], e * 16 + (u - 1))
                        g.tensor_tensor(wprod_b[:, (u % 2) * NC:(u % 2 + 1) * NC],
                                        prod_b[:, (u % 2) * NC:(u % 2 + 1) * NC],
                                        cbe[:, (u // 8) * NC:(u // 8 + 1) * NC], ALU.mult).then_inc(s["weighted"], 1)

                    def low(u):
                        pool.wait_ge(s["hid_hi"], e * 16 + (u + 1))
                        g.tensor_tensor(hid_l[:, (u % 4) * NC:(u % 4 + 1) * NC],
                                        wprod_b[:, (u % 2) * NC:(u % 2 + 1) * NC],
                                        hid_h[:, (u % 4) * NC:(u % 4 + 1) * NC].bitcast(F32),
                                        ALU.subtract).then_inc(s["hid_lo"], 1)
                    weigh(0)
                    for u in range(1, 16):
                        weigh(u)
                        low(u - 1)
                    low(15)

                for i in range(2):
                    g.memset(wprod_b[:, i * NC:(i + 1) * NC], 0.0).then_inc(s["weighted"], 1)
                pool.wait_ge(s["cb_ev"], 2 * E)
                pool.wait_ge(s["weighted"], 2)
                def weighted_expert(e):
                    g.tensor_copy(cbe, cbc[:, bass.ds((e - 1) * N, N)]).then_inc(s["cbe_set"], 1)
                    pool.wait_ge(s["cbe_set"], e)
                    dense_expert(e)

                weighted_expert(1)
                with pool.Fori(2, NX) as e:
                    up_low(e)
                    weighted_expert(e)
            for i in range(5):
                r = slice(i * KD * D, (i + 1) * KD * D)
                pool.wait_ge(s["l1_hi"], i + 1)
                g.tensor_tensor(l1_l[:, r], l1_s[:, r], l1_h[:, r].bitcast(F32), ALU.subtract).then_inc(s["l1_lo"], 1)
            for c in range(C):
                pool.wait_ge(s["mix_hi"], 2 * c + 2)
                g.tensor_tensor(chunk(xl[:], c), chunk(tmp[2], c), chunk(xh[:], c).bitcast(F32),
                                ALU.subtract).then_inc(s["mixr_lo"], 1)
            pool.wait_ge(s["gated"], 1)
            g.tensor_tensor(chunk(tmp[5], 0), chunk(hT[:], 0), chunk(tmp[2], 0), ALU.add).then_inc(s["out0_ok"], 1)

        @block.scalar
        def _(act):
            a = nc.scalar

            def w_high(p, n):
                a.activation(wh[:, p * W1:p * W1 + n], ws[:, p * W1:p * W1 + n], ACT.Copy).then_inc(w_hi[p], 1)

            for i in range(3):
                act.wait_ge(d_patch[i], 32)
                for o, x, n in ((wh, wlin_s, KF * D // 3), (patch_h, patch_s, PW // 3)):
                    a.activation(o[:, i * n:(i + 1) * n], x[:, i * n:(i + 1) * n], ACT.Copy).then_inc(s["tok_hi"], 1)
            act.wait_ge(d_w[2], 16)
            w_high(2, W1)

            def preload(func, j):
                a.activation(small[:, 8 + j:9 + j], eps[:, 0:1], func)

            def square(L, c):
                act.wait_ge(s["ln_xc"], 2 * L + c + 1)
                a.activation(chunk(sq[:], c), chunk(xc[:], c), ACT.Square).then_inc(s["ln_sq"], 1)

            def root(L, c):
                act.wait_ge(s["ln_var"], 2 * L + c + 1)
                a.activation(rstd[:, c * NC:(c + 1) * NC], bank(var_bank(L, c), NC), ACT.Sqrt,
                             bias=eps[:, 0:1]).then_inc(s["ln_std"], 1)

            def high(L, c):
                act.wait_ge(s["ln_xn"], 2 * L + c + 1)
                a.activation(chunk(xh[:], c, NT), chunk(xnf[:], c, NT), ACT.Copy).then_inc(s["ln_hi"], 1)

            def norm(L):
                square(L, 0)
                square(L, 1)
                root(L, 0)
                root(L, 1)
                if L == 2:
                    preload(ACT.Sigmoid, 4)
                high(L, 0)
                high(L, 1)

            act.wait_ge(s["const_set"], 3)
            act.wait_ge(s["pad_set"], 3)
            preload(ACT.Sqrt, 0)
            norm(0)
            preload(ACT.Exp, 1)
            for i in range(0, 2 * TT, 2):
                act.wait_ge(s["v_mm"], i + 1)
                a.activation(v_tok[i // 2][:, 0:512], bank(i % 4), ACT.Copy).then_inc(s["v_ev_act"], 1)
                if i in (0, 2):
                    act.wait_ge(d_w[i // 2], 16)
                    act.wait_ge(s["tok_mm"], 4)
                    w_high(i // 2, W1)
            act.wait_ge(d_w[2], 32)

            def q_evac(n):
                hp, c = n // 2, n % 2
                act.wait_ge(s["q_mm"], n + 1)
                if hp >= 2:
                    act.wait_ge(s["sc_mm"], 2 * hp - 2)
                a.activation(qb[:, (hp % 2) * NT + c * NC:(hp % 2) * NT + (c + 1) * NC], bank(qk_bank(n), NC),
                             ACT.Copy).then_inc(s["q_ev"], 1)

            def k_evac(n):
                hp, c = n // 2, n % 2
                act.wait_ge(s["k_mm"], n + 1)
                if hp >= 2:
                    act.wait_ge(s["sc_mm"], 2 * hp - 2)
                a.activation(kb[:, (hp % 2) * N + c * NC:(hp % 2) * N + (c + 1) * NC], bank(qk_bank(n) + 1, NC),
                             ACT.Copy).then_inc(s["k_ev"], 1)

            for n in range(2):
                q_evac(n)
                k_evac(n)
            for t in range(2 * HP + 2):
                if t >= 2:
                    v = t - 2
                    act.wait_ge(s["pt_mm"], v + 1)
                    if v >= 2:
                        act.wait_ge(s["ctx_mm"], v - 1)
                    a.activation(pat(ptb[0:T2, :], (v % 2) * SC, [SC // 2, 2], [1, SC // 2]),
                                 pat(ps[0:T2, 2, :], 0, [512, 2], [1, SC // 2]), ACT.Copy).then_inc(s["pt_ev"], 1)
                if t + 2 < 2 * HP:
                    q_evac(t + 2)
                    k_evac(t + 2)
                if t == 3:
                    w_high(2, W1)
                if t < 2 * HP:
                    act.wait_ge(s["shifted"], t + 1)
                    sc = sreg[0:T2, (t % 3) * SC:(t % 3 + 1) * SC]
                    a.activation(sc, sc, ACT.Exp).then_inc(s["expd"], 1)
                if t >= 2:
                    act.wait_ge(s["ctx_mm"], v + 1)
                    hp, c = v // 2, v % 2
                    a.activation(ctx_h[:, hp * N + c * NC:hp * N + (c + 1) * NC], bank(4 + v % 2, NC),
                                 ACT.Copy).then_inc(s["ctx_hi"], 1)
            act.dma_start(rcb, rconst).then_inc(s["d_rc"], 16)
            act.dma_start(l1_s, w_l1).then_inc(s["d_l1"], 16)

            def expert_high(p, e):
                act.wait_ge(d_w[p], e * 16 + 16 * (WBASE[p] + 1))
                w_high(p, W1)

            preload(ACT.Sqrt, 2)
            expert_high(0, 0)
            square(1, 0)
            expert_high(1, 0)
            root(1, 0)
            act.wait_ge(s["wo_mm"], 4)
            expert_high(2, 0)
            high(1, 0)
            square(1, 1)
            root(1, 1)
            preload(ACT.Silu, 7)
            a.activation(ident_r, ident, ACT.Copy).then_inc(s["xt_hi"], 1)

            def silu(e, u):
                act.wait_ge(s["gu_mm"], e * 16 + (u + 1))
                if not (isinstance(e, int) and e == 0 and u < 2):
                    act.wait_ge(s["gate_mul"], e * 16 + (u - 1))
                a.activation(silu_b[:, (u % 2) * NC:(u % 2 + 1) * NC], bank(2 * (u % 2), NC),
                             ACT.Silu).then_inc(s["silu_ok"], 1)

            def shared_high(u):
                act.wait_ge(s["gate_mul"], u + 1)
                if u >= 4:
                    act.wait_ge(s["dn_mm"], u - 3)
                a.activation(hid_h[:, (u % 4) * NC:(u % 4 + 1) * NC], prod_b[:, (u % 2) * NC:(u % 2 + 1) * NC],
                             ACT.Copy).then_inc(s["hid_hi"], 1)

            def tokens_high(i):
                n0, n1, b, o = XT[i]
                act.wait_ge(s["xt_mm"], i + 1)
                a.activation(xt_h[:, n0 * P:n1 * P], bank(b, (n1 - n0) * P, o), ACT.Copy).then_inc(s["xt_hi"], 1)

            for u in range(16):
                silu(0, u)
                if u == 0:
                    high(1, 1)
                if u >= 1:
                    shared_high(u - 1)
                if u == 2:
                    act.wait_ge(s["rt_shift"], 1)
                    a.activation(route[:, 80:115], route[:, 80:115], ACT.Exp).then_inc(s["rt_exp"], 1)
                if 3 <= u < 6:
                    tokens_high(u - 3)
                if u in (12, 13):
                    p = u - 12
                    act.wait_ge(d_w[p], 16 * (WBASE[p] + 2))
                    a.activation(half(wh, p, 0, KD, 0), half(ws, p, 0, KD, 0), ACT.Copy).then_inc(s["half_hi"], 1)
            shared_high(15)
            act.wait_ge(s["g_gath"], 1)
            a.activation(xg_h, bank(0), ACT.Copy).then_inc(s["g_xh"], 1)
            for p in range(2):
                a.activation(half(wh, p, 0, KD, 1), half(ws, p, 0, KD, 1), ACT.Copy).then_inc(w_hi[p], 1)
            act.wait_ge(s["dn_mm"], 16)
            expert_high(2, 1)

            def last_high():
                act.wait_ge(s["d_l1"], 16)
                for i in range(5):
                    r = slice(i * KD * D, (i + 1) * KD * D)
                    a.activation(l1_h[:, r], l1_s[:, r], ACT.Copy).then_inc(s["l1_hi"], 1)

            def dense_expert(e):
                def high(u):
                    act.wait_ge(s["weighted"], e * 16 + (u - 13))
                    act.wait_ge(s["dn_mm"], e * 16 + (u - 3))
                    a.activation(hid_h[:, (u % 4) * NC:(u % 4 + 1) * NC], wprod_b[:, (u % 2) * NC:(u % 2 + 1) * NC],
                                 ACT.Copy).then_inc(s["hid_hi"], 1)
                silu(e, 0)
                for u in range(1, 16):
                    silu(e, u)
                    high(u - 1)
                high(15)

            act.wait_ge(s["count_set"], 1)
            with act.If(act.value_load(count_i[0:1, 0:1]) <= SLOTS):
                def gathered_expert(e, final):
                    x = e - 1

                    def silu(i):
                        act.wait_ge(s["g_mm"], x * 4 + (i + 1))
                        b = 2 if i == 2 else 0
                        a.activation(pat(silu_g, (i % 2) * G, [SLOTS, 2], [1, SLOTS]),
                                     pat(bank(b), 0, [512, 2], [1, SLOTS]), ACT.Silu).then_inc(s["g_silu"], 1)

                    def high(i):
                        act.wait_ge(s["g_mul"], x * 4 + (i + 1))
                        a.activation(gh_h[:, i * G:(i + 1) * G], prod_g[:, (i % 2) * G:(i % 2 + 1) * G],
                                     ACT.Copy).then_inc(s["g_hi"], 1)

                    for i in range(3):
                        silu(i)
                        high(i)
                    silu(3)
                    if not final:
                        expert_high(0, e + 1)
                    high(3)
                    if final:
                        last_high()
                    else:
                        expert_high(1, e + 1)
                        act.wait_ge(s["g_gath"], x + 2)
                        a.activation(xg_h, bank(0), ACT.Copy).then_inc(s["g_xh"], 1)
                    act.wait_ge(s["g_y"], x + 1)
                    act.wait_ge(s["g_pt"], x + 1)
                    for st in range(ST):
                        a.activation(y_h[:, st * D:(st + 1) * D], bank(2 + st, D), ACT.Copy,
                                     scale=cw_slot[:, st:st + 1]).then_inc(s["g_yh"], 1)
                    if not final:
                        expert_high(2, e + 1)

                gathered_expert(1, False)
                with act.Fori(2, E) as e:
                    gathered_expert(e, False)
                gathered_expert(E, True)
            with act.Else():
                act.wait_ge(s["g_xh"], 1)
                a.activation(xg_h, xnf[:, 0:G], ACT.Copy).then_inc(s["back_hi"], 1)
                dense_expert(1)
                with act.Fori(2, NX) as e:
                    act.wait_ge(s["gate_mul"], e * 16)
                    expert_high(0, e)
                    expert_high(1, e)
                    act.wait_ge(s["dn_mm"], e * 16)
                    expert_high(2, e)
                    dense_expert(e)
                act.wait_ge(s["gu_mm"], NX * 16)
                last_high()
            preload(ACT.Sqrt, 3)
            norm(2)
            for i, (m, c) in enumerate(MC):
                act.wait_ge(s["ra_mm"], 2 * i + 1)
                a.activation(tmp[0][:, m * N + c * NC:m * N + (c + 1) * NC], bank(4 + i, NC), ACT.Sigmoid,
                             bias=pb[:, PB_BD + m:PB_BD + m + 1]).then_inc(s["ra_sig"], 1)

            def previous(c):
                act.wait_ge(s["ln_xn"], 8 + 2 * c)
                for k in (1, 0):
                    for m in range(KD):
                        j = 2 * k + m
                        a.activation(pat(tmp[(4, 1)[k]], m * N + c * NC, [T, BC], [1, T]),
                                     pat(xnf[:], m * XW + c * BC * (T + 1), [T + 1, BC], [1, T]),
                                     ACT.Copy, scale=small[:, 4 + j:5 + j]).then_inc(s["mix_mul"], 1)

            def mix_high(c):
                for k in (1, 0):
                    act.wait_ge(s["mix_ok"], 4 * c + 4 - 2 * k)
                    a.activation(chunk((xh[:, 0:KD * N], xk_h)[k], c), chunk(tmp[2 + k], c),
                                 ACT.Copy).then_inc(s["mix_hi"], 1)

            preload(ACT.Sqrt, 5)
            square(3, 0)
            square(3, 1)
            root(3, 0)
            root(3, 1)
            preload(ACT.Sigmoid, 6)
            act.wait_ge(s["l1_lo"], 5)
            previous(0)
            mix_high(0)
            previous(1)
            mix_high(1)
            for c in range(C):
                act.wait_ge(s["rk_mm"], 4 * c + 2)
                a.activation(chunk(tmp[1], c), pat(bank(2 * c), 0, [512, KD], [1, NC]),
                             ACT.Relu).then_inc(s["k_relu"], 1)
                act.wait_ge(s["k_relu"], c + 1)
                a.activation(chunk(xk_h, c), chunk(tmp[1], c), ACT.Square).then_inc(s["k_hi"], 1)
                for m in range(KD):
                    i = KD * c + m
                    act.wait_ge(s["rk_mm"], 4 * c + 3 + m)
                    a.activation(tmp[0][:, m * N + c * NC:m * N + (c + 1) * NC], bank(4 + i, NC),
                                 ACT.Sigmoid).then_inc(s["r_sig"], 1)

        @block.vector
        def _(dve):
            v = nc.vector
            chain = [0]

            def link(ins):
                chain[0] += 1
                ins.then_inc(s["dve_chain"], 1)
                dve.wait_ge(s["dve_chain"], chain[0])

            def sub(o, x, hi):
                return v.tensor_tensor(o, x, hi.bitcast(F32), ALU.subtract)

            def w_low(p, n):
                return sub(wl[:, p * W1:p * W1 + n], ws[:, p * W1:p * W1 + n],
                           wh[:, p * W1:p * W1 + n]).then_inc(w_lo[p], 1)

            for i in range(3):
                for j, (o, x, h, n) in enumerate(((wl, wlin_s, wh, KF * D // 3), (patch_l, patch_s, patch_h, PW // 3))):
                    r = slice(i * n, (i + 1) * n)
                    dve.wait_ge(s["tok_hi"], 2 * i + j + 1)
                    sub(o[:, r], x[:, r], h[:, r]).then_inc(s["tok_lo"], 1)
            dve.wait_ge(w_hi[2], 1)
            w_low(2, W1)
            dve.wait_ge(s["d_par"], 16)
            link(v.tensor_tensor(small[:, 0:KD], pb[:, PB_CLS:PB_CLS + KD],
                                 pat(pb[:], PB_POS, [T, KD]), ALU.add))
            v.tensor_copy(pat(hT[:], 0, [N, KD], [T, B]),
                          pat(small[:], 0, [1, KD], [0, B])).then_inc(s["cls_set"], 1)
            for i, (m, c) in enumerate(MC):
                dve.wait_ge(s["tok_mm"], i + 1)
                v.scalar_tensor_tensor(out=pat(hT[:], m * N + c * NC + 1, [T, BC], [1, NP]),
                                       in0=bank(4 + i, NPC).rearrange("p (b n) -> p b n", b=BC),
                                       scalar=pb[:, PB_BLIN + m:PB_BLIN + m + 1],
                                       in1=pat(pb[:], PB_POS + m * T + 1, [0, BC], [1, NP]),
                                       op0=ALU.add, op1=ALU.add).then_inc(s["h_ready"], 1)

            def centre(L, c):
                dve.wait_ge(s["ln_mean"], 2 * L + c + 1)
                v.tensor_tensor(chunk(xc[:], c), chunk(hT[:], c), pat(bank(2 * c), 0, [0, KD], [1, NC]),
                                ALU.subtract).then_inc(s["ln_xc"], 1)

            def invert(L, c):
                r = rstd[:, c * NC:(c + 1) * NC]
                dve.wait_ge(s["ln_std"], 2 * L + c + 1)
                v.reciprocal(r, r).then_inc(s["ln_rs"], 1)
                dve.wait_ge(s["ln_rs"], 2 * L + c + 1)

            def normal(L, c):
                v.tensor_tensor(chunk(xnf[:], c, NT), chunk(xc[:], c), pat(rstd[:], c * NC, [0, KD], [1, NC]),
                                ALU.mult).then_inc(s["ln_xn"], 1)

            def low(L, c):
                dve.wait_ge(s["ln_hi"], 2 * L + c + 1)
                sub(chunk(xl[:], c, NT), chunk(xnf[:], c, NT), chunk(xh[:], c, NT)).then_inc(s["ln_lo"], 1)

            def norm(L):
                centre(L, 0)
                centre(L, 1)
                for c in range(C):
                    invert(L, c)
                    normal(L, c)
                    low(L, c)
                    if L == 0 and c == 0:
                        dve.wait_ge(s["bias_mm"], 1)
                        v.tensor_copy(pat(bias_q[0:T, :], 0, [T, HEADS], [1, 32]),
                                      pat(ps[0:T, 1, :], 0, [1, HEADS], [HEADS, 32])).then_inc(s["bias_ev"], 1)
                        v.tensor_copy(pat(bias_q[0:T, :], 32, [T, HEADS], [1, T - 32]),
                                      pat(ps[0:T, 3, :], 0, [1, HEADS], [HEADS, T - 32])).then_inc(s["bias_ev"], 1)

            norm(0)
            for i in range(1, 2 * TT, 2):
                dve.wait_ge(s["v_mm"], i + 1)
                v.tensor_copy(v_tok[i // 2][:, 512:1024], bank(i % 4)).then_inc(s["v_ev_dve"], 1)
                if i in (3, 5):
                    p = (i - 3) // 2
                    dve.wait_ge(w_hi[p], 1)
                    w_low(p, W1 // (p + 1))

            dve.wait_ge(s["d_bias"], 32)
            dve.wait_ge(s["d_v0"], 16 * V_RUNS_C0)
            dve.wait_ge(s["d_v1"], 16 * (len(V_RUNS) - V_RUNS_C0))
            for t in range(2 * HP + 3):
                if t < 2 * HP:
                    hp = t // 2
                    sc = sreg[0:T2, (t % 3) * SC:(t % 3 + 1) * SC]
                    dve.wait_ge(s["sc_mm"], t + 1)
                    if t >= 3:
                        dve.wait_ge(s["pt_mm"], t - 2)
                    v.tensor_tensor(pat(sc, 0, [PPC * T2, 2], [T2, PPC], [1, T2]),
                                    pat(ps[0:T2, 0, :], 0, [512, 2], [T2, PPC], [1, T2]),
                                    pat(bias[0:T2, :], 2 * hp * T2, [T2, 2], [0, PPC], [1, T2]),
                                    ALU.add).then_inc(s["sc_ev"], 1)
                    dve.wait_ge(s["sc_ev"], t + 1)
                    v.tensor_reduce(stat[0:T2, (t % 3) * 24:(t % 3) * 24 + 8], sc.rearrange("p (g k) -> p g k", g=8),
                                    AX.X, ALU.max).then_inc(s["maxed"], 1)
                if 1 <= t <= 2 * HP:
                    u = t - 1
                    sm, rc = (stat[0:T2, (u % 3) * 24 + 8 * k:(u % 3) * 24 + 8 * k + 8] for k in (1, 2))
                    dve.wait_ge(s["expd"], u + 1)
                    v.tensor_reduce(sm, pat(sreg[0:T2, :], (u % 3) * SC, [T2, 8], [1, T2]),
                                    AX.X, ALU.add).then_inc(s["summed"], 1)
                    dve.wait_ge(s["summed"], u + 1)
                    v.reciprocal(rc, sm).then_inc(s["recip"], 1)
                if t == 4:
                    dve.wait_ge(w_hi[2], 2)
                    w_low(2, W1)
                if t >= 3:
                    u = t - 3
                    hp, c = u // 2, u % 2
                    r = slice(hp * N + c * NC, hp * N + (c + 1) * NC)
                    dve.wait_ge(s["ctx_hi"], u + 1)
                    sub(ctx_l[:, r], bank(4 + u % 2, NC), ctx_h[:, r]).then_inc(s["ctx_lo"], 1)

            def expert_low(p, e):
                dve.wait_ge(w_hi[p], e + (WBASE[p] + 1))
                w_low(p, W1 // 2 if p == 1 else W1)

            def add_attention(i):
                m, c = MC[i]
                r = slice(m * N + c * NC, m * N + (c + 1) * NC)
                dve.wait_ge(s["wo_mm"], i + 1)
                v.tensor_tensor(hT[:, r], hT[:, r], bank(6 - 2 * c + m, NC), ALU.add).then_inc(s["h_ready"], 1)

            add_attention(0)
            add_attention(1)
            centre(1, 0)
            expert_low(0, 0)
            expert_low(1, 0)
            add_attention(2)
            invert(1, 0)
            add_attention(3)
            normal(1, 0)
            centre(1, 1)
            low(1, 0)
            dve.wait_ge(s["d_rc"], 16)
            v.tensor_copy(tri_r, rcb[:, RB_TRI:RB_TRI + P])
            v.tensor_copy(one_r, rcb[:, RB_ONES:RB_ONES + P])
            v.memset(sel_r.bitcast(F32), 0.0).then_inc(s["sel_set"], 1)
            dve.wait_ge(s["sel_set"], 1)
            invert(1, 1)
            normal(1, 1)
            lg, gt, eq = route[:, 0:40], route[:, 120:365], route[:, 365:610]
            rank, selm, mx5, sm5 = route[:, 610:645], route[:, 645:680], route[:, 680:685], route[:, 685:690]
            ex, selr = route[:, 80:115], route[:, 690:725]

            def shared_low(u):
                dve.wait_ge(s["hid_hi"], u + 1)
                if u >= 4:
                    dve.wait_ge(s["dn_mm"], u - 3)
                r = slice((u % 4) * NC, (u % 4 + 1) * NC)
                sub(hid_l[:, r], prod_b[:, (u % 2) * NC:(u % 2 + 1) * NC], hid_h[:, r]).then_inc(s["hid_lo"], 1)
            jj = ([8, TT], [0, E], [1, E])
            ee = ([8, TT], [1, E], [0, E])
            three = ([49, TT], [E, E], [1, E])

            def rank_experts():
                dve.wait_ge(s["rt_mm"], 1)
                link(v.tensor_copy(lg, bank(6, 40, LG0)))
                link(v.tensor_tensor(pat(gt, 0, *three), pat(lg, 0, *jj), pat(lg, 0, *ee), ALU.is_gt))
                link(v.tensor_tensor(pat(eq, 0, *three), pat(lg, 0, *jj), pat(lg, 0, *ee), ALU.is_equal))
                link(v.tensor_tensor(pat(eq, 0, *three), pat(eq, 0, *three),
                                     pat(cb[:], CB_TRI, [0, TT], [E, E], [1, E]), ALU.mult))
                link(v.tensor_tensor(gt, gt, eq, ALU.add))
                link(v.tensor_reduce(rank, pat(gt, 0, [E, TT * E], [1, E]), AX.X, ALU.add))
                link(v.tensor_scalar(selm, rank, 1.5, None, ALU.is_lt))
                v.tensor_tensor(pat(selr, 0, [E, TT], [1, E]), pat(selm, 0, [E, TT], [1, E]),
                                pat(rcb, RB_REAL, [1, TT], [0, E]), ALU.mult)
                v.tensor_tensor(pat(sel_r, 0, [8, TT], [1, E]), pat(selm, 0, [E, TT], [1, E]),
                                pat(rcb, RB_REAL, [1, TT], [0, E]), ALU.mult).then_inc(s["sel_set"], 1)

            def shift_logits():
                link(v.tensor_reduce(mx5, pat(lg, 0, [8, TT], [1, E]), AX.X, ALU.max))
                v.tensor_tensor(pat(ex, 0, [E, TT], [1, E]), pat(lg, 0, [8, TT], [1, E]),
                                pat(mx5, 0, [1, TT], [0, E]), ALU.subtract).then_inc(s["rt_shift"], 1)

            def token_weights():
                dve.wait_ge(s["rt_exp"], 1)
                link(v.tensor_tensor(ex, ex, selm, ALU.mult))
                link(v.tensor_reduce(sm5, pat(ex, 0, [E, TT], [1, E]), AX.X, ALU.add))
                link(v.reciprocal(sm5, sm5))
                v.memset(pat(comb, E, [8, TT]), 1.0).then_inc(s["comb_set"], 1)
                v.tensor_tensor(pat(comb, 0, [8, TT], [1, E]), pat(ex, 0, [E, TT], [1, E]),
                                pat(sm5, 0, [1, TT], [0, E]), ALU.mult).then_inc(s["comb_set"], 1)

            def slots():
                dve.wait_ge(s["pos_mm"], 1)
                link(v.memset(slot, -1.0))
                link(v.scalar_tensor_tensor(out=pat(slot, 0, [8, TT], [1, E]),
                                            in0=pat(bank(6), POS0, [8, TT], [1, E]), scalar=1.0,
                                            in1=pat(selr, 0, [E, TT], [1, E]), op0=ALU.add, op1=ALU.mult))
                link(v.tensor_scalar(pat(slot, 0, [8, TT], [1, E]), pat(slot, 0, [8, TT], [1, E]),
                                     -1.0, None, ALU.add))
                link(v.tensor_reduce(count, bank(6, E, CNT0), AX.X, ALU.max))
                v.tensor_copy(count_i[:], count).then_inc(s["count_set"], 1)

            def tokens_low(i):
                n0, n1, b, o = XT[i]
                dve.wait_ge(s["xt_hi"], i + 2)
                r = slice(n0 * P, n1 * P)
                sub(xt_l[:, r], bank(b, (n1 - n0) * P, o), xt_h[:, r]).then_inc(s["xt_lo"], 1)

            LINKS = 3

            def columns(x, n):
                def glink(ins, j):
                    ins.then_inc(s["g_chain"], 1)
                    dve.wait_ge(s["g_chain"], n + j)
                v.tensor_copy(slot_c[:, 0:TT].unsqueeze(2), slot_at(x))
                glink(v.tensor_copy(comb_c[:, 0:TT].unsqueeze(2), comb_at(x)), 1)
                v.tensor_copy(slot_r[:, 0:TT], slot_c[:, 0:TT])
                glink(v.tensor_copy(pat(cw_r, 0, [2, TT]), comb_c[:, 0:TT]), 2)
                glink(v.tensor_tensor(pat(cw_r, 1, [2, TT]), comb_c[:, 0:TT],
                                      pat(cw_r, 0, [2, TT]).bitcast(F32), ALU.subtract), 3)
                for t in range(TT):
                    w = v.tensor_scalar(pg[:, t * SLOTS:(t + 1) * SLOTS], rcb[:, RB_IOTA:RB_IOTA + SLOTS],
                                        slot_c[:, t:t + 1], None, ALU.is_equal)
                w.then_inc(s["g_pg"], 1)

            def slot_at(x):
                return slot.rearrange("p (t e) -> p t e", e=8)[:, :, bass.ds(x, 1)]

            def comb_at(x):
                return comb.rearrange("p (t e) -> p t e", e=8)[:, :, bass.ds(x, 1)]

            dve.wait_ge(s["d_const"], 16)
            for u in range(16):
                r = slice((u % 2) * NC, (u % 2 + 1) * NC)
                dve.wait_ge(s["silu_ok"], u + 1)
                if u >= 2:
                    dve.wait_ge(s["hid_hi"], u - 1)
                    dve.wait_ge(s["hid_lo"], u - 1)
                v.tensor_tensor(prod_b[:, r], silu_b[:, r], bank(2 * (u % 2) + 1, NC),
                                ALU.mult).then_inc(s["gate_mul"], 1)
                if u == 0:
                    low(1, 1)
                if u >= 1:
                    shared_low(u - 1)
                if u == 1:
                    rank_experts()
                    shift_logits()
                if u == 3:
                    token_weights()
                if 3 <= u < 6:
                    tokens_low(u - 3)
                if u == 7:
                    slots()
                if u in (13, 14):
                    p = u - 13
                    dve.wait_ge(s["half_hi"], p + 1)
                    sub(half(wl, p, 0, KD - p, 0), half(ws, p, 0, KD - p, 0),
                        half(wh, p, 0, KD - p, 0)).then_inc(s["half_lo"], 1)
                if u == 10:
                    dve.wait_ge(s["comb_set"], 2)
                    dve.wait_ge(s["count_set"], 1)
                    columns(0, 0)
            shared_low(15)
            dve.wait_ge(s["g_gath"], 1)
            v.tensor_copy(xg_l, bank(1)).then_inc(s["g_xl"], 1)
            for p in range(2):
                dve.wait_ge(w_hi[p], WBASE[p] + 2)
                sub(half(wl, p, 0, KD - p, 1), half(ws, p, 0, KD - p, 1),
                    half(wh, p, 0, KD - p, 1)).then_inc(w_lo[p], 1)

            def dense_expert(e):
                for u in range(16):
                    dve.wait_ge(s["silu_ok"], e * 16 + (u + 1))
                    dve.wait_ge(s["weighted"], e * 16 + (u - 15))
                    r = slice((u % 2) * NC, (u % 2 + 1) * NC)
                    v.tensor_tensor(prod_b[:, r], silu_b[:, r], bank(2 * (u % 2) + 1, NC),
                                    ALU.mult).then_inc(s["gate_mul"], 1)

            with dve.If(dve.value_load(count_i[0:1, 0:1]) <= SLOTS):
                def gathered_expert(e, final):
                    x = e - 1

                    def gate(i):
                        dve.wait_ge(s["g_silu"], x * 4 + (i + 1))
                        b = 2 if i == 2 else 0
                        v.tensor_tensor(pat(prod_g, (i % 2) * G, [SLOTS, 2], [1, SLOTS]),
                                        pat(silu_g, (i % 2) * G, [SLOTS, 2], [1, SLOTS]),
                                        pat(bank(b), SLOTS, [512, 2], [1, SLOTS]), ALU.mult).then_inc(s["g_mul"], 1)

                    def low(i):
                        dve.wait_ge(s["g_hi"], x * 4 + (i + 1))
                        sub(gh_l[:, i * G:(i + 1) * G], prod_g[:, (i % 2) * G:(i % 2 + 1) * G],
                            gh_h[:, i * G:(i + 1) * G]).then_inc(s["g_lo"], 1)

                    gate(0)
                    low(0)
                    dve.wait_ge(s["g_row"], x + 1)
                    v.tensor_reduce(cw_slot, pat(bank(3), 256, [2, ST], [1, 2]), AX.X, ALU.add)
                    for st in range(ST):
                        w = v.tensor_scalar(pt[:, st * N:(st + 1) * N], pat(bank(2), 0, [1, N]),
                                            rcb[:, RB_PART + st:RB_PART + st + 1], None, ALU.is_equal)
                    w.then_inc(s["g_pt"], 1)
                    gate(1)
                    if not final:
                        columns(e, LINKS * e)
                    low(1)
                    gate(2)
                    low(2)
                    gate(3)
                    if not final:
                        expert_low(0, e + 1)
                    low(3)
                    if not final:
                        expert_low(1, e + 1)
                        dve.wait_ge(s["g_gath"], x + 2)
                        v.tensor_copy(xg_l, bank(1)).then_inc(s["g_xl"], 1)
                    dve.wait_ge(s["g_pt"], x + 1)
                    for st in range(ST):
                        r = slice(st * D, (st + 1) * D)
                        dve.wait_ge(s["g_yh"], x * ST + (st + 1))
                        v.scalar_tensor_tensor(out=y_l[:, r], in0=bank(2 + st, D), scalar=cw_slot[:, st:st + 1],
                                               in1=y_h[:, r].bitcast(F32), op0=ALU.mult,
                                               op1=ALU.subtract).then_inc(s["g_yl"], 1)

                gathered_expert(1, False)
                with dve.Fori(2, E) as e:
                    gathered_expert(e, False)
                gathered_expert(E, True)
            with dve.Else():
                dve.wait_ge(s["g_xl"], 1)
                dve.wait_ge(s["back_hi"], 1)
                sub(xg_l, xnf[:, 0:G], xg_h).then_inc(s["back_lo"], 1)
                expert_low(2, 1)
                for e in range(E):
                    dve.wait_ge(s["cb_mm"], e + 1)
                    b = 2 * (e % 2)
                    v.tensor_copy(cbc[:, e * N:e * N + 512], bank(b)).then_inc(s["cb_ev"], 1)
                    v.tensor_copy(cbc[:, e * N + 512:(e + 1) * N], bank(b + 1, N - 512)).then_inc(s["cb_ev"], 1)
                dense_expert(1)
                with dve.Fori(2, NX) as e:
                    for p in range(3):
                        expert_low(p, e)
                    dense_expert(e)
            for i, (m, c) in enumerate(MC):
                dve.wait_ge(s["moe_mm"], i + 1)
                r = slice(m * N + c * NC, m * N + (c + 1) * NC)
                v.tensor_tensor(hT[:, r], hT[:, r], bank(4 + i, NC), ALU.add).then_inc(s["h_ready"], 1)
            link(v.tensor_scalar(small[:, 4:8], pb[:, PB_MUR:PB_MUR + 4], -1.0, 1.0, ALU.mult, ALU.add))
            norm(2)
            for c in range(C):
                for m in range(KD):
                    i = KD * c + m
                    r = slice(m * N + c * NC, m * N + (c + 1) * NC)
                    dve.wait_ge(s["ra_sig"], i + 1)
                    v.tensor_scalar(tmp[2][:, r], tmp[0][:, r], -1.0, 1.0, ALU.mult, ALU.add)
                    dve.wait_ge(s["ra_mm"], 2 * i + 2)
                    w = v.scalar_tensor_tensor(out=tmp[1][:, r], in0=bank(i, NC),
                                               scalar=pb[:, PB_BV + m:PB_BV + m + 1],
                                               in1=tmp[0][:, r], op0=ALU.add, op1=ALU.mult)
                link(w)
                link(v.memset(pat(tmp[2], c * NC, [N, KD], [T, BC]), 0.0))
                for m in range(KD):
                    r = slice(m * N + c * NC, m * N + (c + 1) * NC)
                    w = v.tensor_tensor_scan(tmp[3][:, r], tmp[2][:, r], tmp[1][:, r], 0.0, ALU.mult, ALU.add)
                link(w)
                for m in range(KD):
                    r = slice(m * N + c * NC, m * N + (c + 1) * NC)
                    v.tensor_tensor(hT[:, r], hT[:, r], tmp[3][:, r], ALU.add).then_inc(s["h_ready"], 1)

            v.memset(pat(xnf[:], 0, [T + 1, KD * B]), 0.0)
            centre(3, 0)
            centre(3, 1)

            def normal_spread(c):
                for m in range(KD):
                    v.tensor_tensor(pat(xnf[:], m * XW + c * BC * (T + 1) + 1, [T + 1, BC], [1, T]),
                                    pat(xc[:], m * N + c * NC, [T, BC], [1, T]),
                                    pat(rstd[:], c * NC, [T, BC], [1, T]), ALU.mult).then_inc(s["ln_xn"], 1)

            def mix(c):
                dve.wait_ge(s["ln_xn"], 8 + 2 * c)
                for k in (1, 0):
                    for m in range(KD):
                        j = 2 * k + m
                        dve.wait_ge(s["mix_mul"], 4 * c + 2 * (1 - k) + m + 1)
                        v.scalar_tensor_tensor(out=pat(tmp[2 + k], m * N + c * NC, [T, BC], [1, T]),
                                               in0=pat(xnf[:], m * XW + c * BC * (T + 1) + 1, [T + 1, BC], [1, T]),
                                               scalar=pb[:, PB_MUR + j:PB_MUR + j + 1],
                                               in1=pat(tmp[(4, 1)[k]], m * N + c * NC, [T, BC], [1, T]),
                                               op0=ALU.mult, op1=ALU.add).then_inc(s["mix_ok"], 1)

            def mix_low(c):
                dve.wait_ge(s["mix_hi"], 2 * c + 1)
                dve.wait_ge(s["mix_ok"], 4 * c + 2)
                sub(chunk(xk_l, c), chunk(tmp[3], c), chunk(xk_h, c)).then_inc(s["mix_lo"], 1)

            invert(3, 0)
            normal_spread(0)
            invert(3, 1)
            mix(0)
            normal_spread(1)
            mix_low(0)
            mix(1)
            mix_low(1)
            for c in range(C):
                dve.wait_ge(s["k_relu"], c + 1)
                v.tensor_tensor(chunk(tmp[4], c), chunk(tmp[1], c), chunk(tmp[1], c), ALU.mult).then_inc(s["k_sq"], 1)
                dve.wait_ge(s["k_sq"], c + 1)
                dve.wait_ge(s["k_hi"], c + 1)
                sub(chunk(xk_l, c), chunk(tmp[4], c), chunk(xk_h, c)).then_inc(s["k_lo"], 1)
            dve.wait_ge(s["r_sig"], KD)
            dve.wait_ge(s["vv_mm"], KD)
            v.tensor_tensor(chunk(tmp[2], 0), chunk(tmp[0], 0), pat(bank(4), 0, [512, KD], [1, NC]),
                            ALU.mult).then_inc(s["gated"], 1)
            for m in range(KD):
                i = KD + m
                r = slice(m * N + NC, m * N + 2 * NC)
                dve.wait_ge(s["r_sig"], i + 1)
                dve.wait_ge(s["vv_mm"], i + 1)
                link(v.tensor_tensor(tmp[2][:, r], tmp[0][:, r], bank(4 + i, NC), ALU.mult))
                v.tensor_tensor(tmp[5][:, r], hT[:, r], tmp[2][:, r], ALU.add).then_inc(s["out_ok"], 1)

        @block.tensor
        def _(pe):
            mm = nc.tensor.matmul

            def three(o, a_h, a_l, b_h, b_l, start, stop):
                mm(o, a_h, b_h, start=start, stop=False)
                mm(o, a_h, b_l, start=False, stop=False)
                return mm(o, a_l, b_h, start=False, stop=stop)

            for k in range(KF):
                pe.wait_ge(s["tok_lo"], 2 * (k // 2) + 2)
                for i, (m, c) in enumerate(MC):
                    w_ = slice(k * D + m * P, k * D + (m + 1) * P)
                    x_ = slice(k * NP * B + c * NPC, k * NP * B + (c + 1) * NPC)
                    w = three(bank(4 + i, NPC), wh[:, w_], wl[:, w_], patch_h[:, x_], patch_l[:, x_],
                              k == 0, k == KF - 1)
                    if k == KF - 1:
                        w.then_inc(s["tok_mm"], 1)

            def mean(L, c):
                pe.wait_ge(s["h_ready"], 4 * L + 2 * c + 2)
                for k in range(KD):
                    w = mm(bank(2 * c, NC), ones[:], hT[:, k * N + c * NC:k * N + (c + 1) * NC],
                           start=(k == 0), stop=(k == KD - 1))
                w.then_inc(s["ln_mean"], 1)

            def variance(L, c):
                pe.wait_ge(s["ln_sq"], 2 * L + c + 1)
                for k in range(KD):
                    w = mm(bank(var_bank(L, c), NC), ones[:], sq[:, k * N + c * NC:k * N + (c + 1) * NC],
                           start=(k == 0), stop=(k == KD - 1))
                w.then_inc(s["ln_var"], 1)

            def keep_clock(n):
                for _ in range(n):
                    mm(bank(3, P), zero[:], ident, start=True, stop=True)

            def norm(L):
                mean(L, 0)
                mean(L, 1)
                variance(L, 0)
                variance(L, 1)

            pe.wait_ge(s["const_set"], 3)
            pe.wait_ge(s["cls_set"], 1)
            norm(0)
            pe.wait_ge(s["d_const"], 16)
            pe.wait_ge(s["d_table"], 16)
            for k in range(T):
                lhs = cb[0:BUCKETS, CB_OH + T - 1 - k:CB_OH + 2 * T - 1 - k]
                w = mm(ps[0:T, 1 + 2 * (k // 32), (k % 32) * HEADS:(k % 32 + 1) * HEADS], lhs, tb[0:BUCKETS, :],
                       start=True, stop=True)
            w.then_inc(s["bias_mm"], 1)
            pe.wait_ge(w_lo[2], 1)
            for i in range(2 * TT):
                t, n = i // 2, i % 2
                pe.wait_ge(s["ln_lo"], 1 if (t + 1) * P <= NC else 2)
                if i == 1:
                    pe.wait_ge(s["bias_ev"], 2)
                if i >= 4:
                    pe.wait_ge(s["v_ev_act"] if i % 2 == 0 else s["v_ev_dve"], (i - 4) // 2 + 1)
                for k in range(KD):
                    x_h, x_l = (x[:, k * NT + t * P:k * NT + (t + 1) * P] for x in (xh, xl))
                    w_ = slice(2 * W1 + k * INNER + n * 512, 2 * W1 + k * INNER + (n + 1) * 512)
                    w = three(bank(i % 4), x_h, x_l, wh[:, w_], wl[:, w_], k == 0, k == KD - 1)
                w.then_inc(s["v_mm"], 1)

            def project(hp, c, j):
                n = 2 * hp + c
                if n >= 2:
                    pe.wait_ge(s["q_ev"] if j == 0 else s["k_ev"], n)
                for k in range(KD):
                    w_ = slice(j * W1 + k * INNER + hp * P, j * W1 + k * INNER + (hp + 1) * P)
                    x_ = slice(k * NT + c * NC, k * NT + (c + 1) * NC)
                    w = three(bank(qk_bank(n) + j, NC), wh[:, w_], wl[:, w_], xh[:, x_], xl[:, x_], k == 0, k == KD - 1)
                w.then_inc(s["q_mm"] if j == 0 else s["k_mm"], 1)

            pe.wait_ge(w_lo[0], 1)
            pe.wait_ge(w_lo[1], 1)
            pe.wait_ge(s["up_lo"], 1)
            for c in range(C):
                for j in range(2):
                    project(0, c, j)

            def output(m, c, k0, k1):
                for k in range(k0, k1):
                    w_ = slice(2 * W1 + k * D + m * P, 2 * W1 + k * D + (m + 1) * P)
                    x_ = slice(k * N + c * NC, k * N + (c + 1) * NC)
                    w = three(bank(6 - 2 * c + m, NC), wh[:, w_], wl[:, w_], ctx_h[:, x_], ctx_l[:, x_],
                              k == 0, k == HP - 1)
                if k1 == HP:
                    w.then_inc(s["wo_mm"], 1)

            pe.wait_ge(s["v_ev_act"], TT)
            pe.wait_ge(s["v_ev_dve"], TT)
            for t in range(2 * HP + 2):
                if t < 2 * HP:
                    hp, half = t // 2, t % 2
                    pe.wait_ge(s["q_ev"], 2 * hp + 2)
                    pe.wait_ge(s["k_ev"], 2 * hp + 2)
                    if t >= 1:
                        pe.wait_ge(s["sc_ev"], t)
                    for g in range(8):
                        pair, hd = PPC * half + g // 2, g % 2
                        r = slice(64 * hd, 64 * hd + 64)
                        w = mm(ps[0:T2, hd, (g // 2) * T2:(g // 2 + 1) * T2],
                               qb[r, (hp % 2) * NT + pair * T2:(hp % 2) * NT + (pair + 1) * T2],
                               kb[r, (hp % 2) * N + pair * T2:(hp % 2) * N + (pair + 1) * T2],
                               start=True, stop=True)
                    w.then_inc(s["sc_mm"], 1)
                if t >= 2:
                    u = t - 2
                    pe.wait_ge(s["normed"], u + 1)
                    if u >= 1:
                        pe.wait_ge(s["pt_ev"], u)
                    for g in range(8):
                        o = (u % 3) * SC + g * T2
                        w = nc.tensor.transpose(ps[0:T2, 2 + g // 4, (g % 4) * T2:(g % 4 + 1) * T2],
                                                sreg[0:T2, o:o + T2], ident[0:T2, 0:T2])
                    w.then_inc(s["pt_mm"], 1)
                if t + 2 < 2 * HP:
                    project(t // 2 + 1, t % 2, 0)
                    project(t // 2 + 1, t % 2, 1)
                else:
                    m, late = t % 2, t >= 2 * HP
                    pe.wait_ge(s["q_ev"] if m == 0 else s["k_ev"], 2 * HP)
                    pe.wait_ge(w_lo[2], 2)
                    pe.wait_ge(s["ctx_lo"], 2 * HP - 3 if late else 2 * HP - 7)
                    output(m, 0, *((4, HP - 1) if late else (0, 4)))
                if t >= 2:
                    hp, half = u // 2, u % 2
                    pe.wait_ge(s["pt_ev"], u + 1)
                    if u < 2:
                        pe.wait_ge(s[f"d_v{u}"], 16 * (V_RUNS_C0 if u == 0 else len(V_RUNS) - V_RUNS_C0))
                    if u >= 2:
                        pe.wait_ge(s["ctx_lo"], u - 1)
                    for g in range(8):
                        pair, hd = PPC * half + g % 4, g // 4
                        vo = pair * INNER + hp * P + hd * DH
                        po = (u % 2) * SC + g * T2
                        w = mm(ps[64 * hd:64 * hd + 64, 4 + u % 2, (g % 4) * T2:(g % 4 + 1) * T2],
                               v_all[0:T2, vo:vo + DH], ptb[0:T2, po:po + T2], start=True, stop=True)
                    w.then_inc(s["ctx_mm"], 1)
            pe.wait_ge(s["ctx_lo"], 2 * HP - 1)
            output(0, 0, HP - 1, HP)
            output(1, 0, HP - 1, HP)
            pe.wait_ge(s["ctx_lo"], 2 * HP)
            output(0, 1, 0, HP // 2)
            mean(1, 0)
            output(0, 1, HP // 2, HP)
            output(1, 1, 0, HP // 2)
            variance(1, 0)
            output(1, 1, HP // 2, HP)
            mean(1, 1)
            variance(1, 1)

            def gate_up(e, u):
                c, j = u // KH, u % KH
                if not (isinstance(e, int) and e == 0 and u < 2):
                    pe.wait_ge(s["gate_mul"], e * 16 + (u - 1))
                for q in range(2):
                    for k in range(KD):
                        w_ = slice(q * W1 + k * HID + j * P, q * W1 + k * HID + (j + 1) * P)
                        x_ = slice(k * NT + c * NC, k * NT + (c + 1) * NC)
                        w = three(bank(2 * (u % 2) + q, NC), wh[:, w_], wl[:, w_], xh[:, x_], xl[:, x_],
                                  k == 0, k == KD - 1)
                w.then_inc(s["gu_mm"], 1)

            def down(e, u, first=False):
                c, j = u // KH, u % KH
                pe.wait_ge(s["hid_lo"], e * 16 + (u + 1))
                x_ = slice((u % 4) * NC, (u % 4 + 1) * NC)
                for m in range(KD):
                    w_ = slice(2 * W1 + j * D + m * P, 2 * W1 + j * D + (m + 1) * P)
                    w = three(bank(4 + 2 * c + m, NC), wh[:, w_], wl[:, w_], hid_h[:, x_], hid_l[:, x_],
                              first, False)
                w.then_inc(s["dn_mm"], 1)

            def logits():
                pe.wait_ge(s["ln_lo"], 4)
                for t in range(TT):
                    for k in range(KD):
                        w = mm(bank(6, E, LG0 + t * 8), xnf[:, k * NT + t * P:k * NT + (t + 1) * P],
                               pb[:, PB_WR + k * E:PB_WR + (k + 1) * E], start=(k == 0), stop=(k == KD - 1))
                w.then_inc(s["rt_mm"], 1)

            def turn_tokens(i):
                n0, n1, b, o = XT[i]
                if i == 1:
                    pe.wait_ge(s["sel_set"], 2)
                if i == 2:
                    pe.wait_ge(s["xt_lo"], 1)
                for n in range(n0, n1):
                    t, k = n // KD, n % KD
                    w = nc.tensor.transpose(bank(b, P, o + (n - n0) * P),
                                            xnf[:, k * NT + t * P:k * NT + (t + 1) * P], ident)
                w.then_inc(s["xt_mm"], 1)

            def positions():
                pe.wait_ge(s["sel_set"], 2)
                pe.wait_ge(s["xt_lo"], 2)
                for t in range(TT + 1):
                    o = bank(6, 8, POS0 + t * 8) if t < TT else bank(6, 8, CNT0)
                    for j in range(min(t + 1, TT)):
                        w = mm(o, tri_r if j == t else one_r, sel_r[:, j * 8:(j + 1) * 8],
                               start=(j == 0), stop=(j == min(t, TT - 1)))
                w.then_inc(s["pos_mm"], 1)

            def gather(n):
                pe.wait_ge(s["g_pg"], n)
                for part, src in ((0, xt_h), (1, xt_l)):
                    for m in range(KD):
                        for t in range(TT):
                            w = mm(ps[:, part, m * SLOTS:(m + 1) * SLOTS],
                                   src[:, t * D + m * P:t * D + (m + 1) * P],
                                   pg[:, t * SLOTS:(t + 1) * SLOTS], start=(t == 0), stop=(t == TT - 1))
                w.then_inc(s["g_gath"], 1)

            pe.wait_ge(w_lo[0], WBASE[0] + 1)
            pe.wait_ge(w_lo[1], WBASE[1] + 1)
            pe.wait_ge(s["up_lo"], 2)
            pe.wait_ge(s["ln_lo"], 3)
            gate_up(0, 0)
            gate_up(0, 1)
            for u in range(2, 16):
                gate_up(0, u)
                if u == 2:
                    logits()
                    pe.wait_ge(w_lo[2], WBASE[2] + 1)
                if u == 10:
                    pe.wait_ge(s["xt_lo"], 3)
                    pe.wait_ge(s["count_set"], 1)
                if u == 15:
                    pe.wait_ge(s["gate_mul"], 15)
                    gather(1)
                down(0, u - 2, first=u - 2 in (0, KH))
                if u in (2, 3):
                    turn_tokens(u - 2)
                if u == 4:
                    turn_tokens(2)
                if u == 5:
                    positions()
            down(0, 14)
            down(0, 15)

            def dense_expert(e):
                pe.wait_ge(w_lo[0], e + (WBASE[0] + 1))
                pe.wait_ge(w_lo[1], e + (WBASE[1] + 1))
                pe.wait_ge(s["up_lo"], e + 2)
                gate_up(e, 0)
                gate_up(e, 1)
                for u in range(2, 16):
                    gate_up(e, u)
                    if u == 2:
                        pe.wait_ge(w_lo[2], e + (WBASE[2] + 1))
                    down(e, u - 2)
                down(e, 14)
                down(e, 15)

            pe.wait_ge(s["count_set"], 1)
            with pe.If(pe.value_load(count_i[0:1, 0:1]) <= SLOTS):
                def scatter(x, final=False):
                    pe.wait_ge(s["g_yl"], x * ST)
                    pe.wait_ge(s["g_yh"], x * ST)
                    pe.wait_ge(s["g_pt"], x)
                    for i, (m, c) in enumerate(MC):
                        for st in range(ST):
                            for y in (y_h, y_l):
                                w = mm(bank(4 + i, NC), y[:, st * D + m * P:st * D + (m + 1) * P],
                                       pt[:, st * N + c * NC:st * N + (c + 1) * NC], start=False,
                                       stop=final and st == ST - 1 and y is y_l)
                        if final:
                            w.then_inc(s["moe_mm"], 1)

                def gathered_expert(e, final=False, first=False):
                    x = e - 1

                    def gate_up(i):
                        b = 2 if i == 2 else 0
                        for jj in range(2):
                            j = 2 * i + jj
                            for q in range(2):
                                for k in range(KD):
                                    w_ = slice(q * W1 + k * HID + j * P, q * W1 + k * HID + (j + 1) * P)
                                    x_ = slice(k * SLOTS, (k + 1) * SLOTS)
                                    w = three(ps[:, b + jj, q * SLOTS:(q + 1) * SLOTS], wh[:, w_], wl[:, w_],
                                              xg_h[:, x_], xg_l[:, x_], k == 0, k == KD - 1)
                        w.then_inc(s["g_mm"], 1)

                    def down(i):
                        pe.wait_ge(s["g_lo"], x * 4 + (i + 1))
                        for j in (2 * i, 2 * i + 1):
                            w_ = slice(2 * W1 + j * D, 2 * W1 + (j + 1) * D)
                            for st in range(ST):
                                h_ = slice(j * SLOTS + st * P, j * SLOTS + (st + 1) * P)
                                w = three(bank(2 + st, D), gh_h[:, h_], gh_l[:, h_], wh[:, w_], wl[:, w_],
                                          j == 0, j == KH - 1)
                        return w

                    def matrices_ready():
                        pe.wait_ge(w_lo[0], e + (WBASE[0] + 1))
                        pe.wait_ge(w_lo[1], e + (WBASE[1] + 1))
                        pe.wait_ge(s["up_lo"], e + 2)

                    if first:
                        pe.wait_ge(s["half_lo"], 2)
                        pe.wait_ge(s["half_up"], 1)
                    else:
                        matrices_ready()
                    pe.wait_ge(s["g_xh"], x + 1)
                    pe.wait_ge(s["g_xl"], x + 1)
                    gate_up(0)
                    if not first:
                        scatter(x)
                    for t in range(TT):
                        mm(ps[:, 2 + t // 4, (t % 4) * P:(t % 4 + 1) * P], pat(slot_r, t, [0, P]), ident_r,
                           start=True, stop=True)
                    for st in range(ST):
                        for t in range(TT):
                            w = mm(bank(3, 2, 256 + 2 * st), pg[:, t * SLOTS + st * P:t * SLOTS + (st + 1) * P],
                                   cw_r[:, 2 * t:2 * t + 2], start=(t == 0), stop=(t == TT - 1))
                    w.then_inc(s["g_row"], 1)
                    pe.wait_ge(s["g_mul"], x * 4 + 1)
                    gate_up(1)
                    pe.wait_ge(s["g_pt"], x + 1)
                    if first:
                        matrices_ready()
                    gate_up(2)
                    pe.wait_ge(s["g_mul"], x * 4 + 2)
                    gate_up(3)
                    pe.wait_ge(s["g_mul"], x * 4 + 3)
                    pe.wait_ge(w_lo[2], e + (WBASE[2] + 1))
                    for i in range(3):
                        down(i)
                    if not final:
                        pe.wait_ge(s["g_mul"], x * 4 + 4)
                        gather(x + 2)
                    down(3).then_inc(s["g_y"], 1)

                gathered_expert(1, first=True)
                with pe.Fori(2, E) as e:
                    gathered_expert(e)
                gathered_expert(E, final=True)
                scatter(E, final=True)
            with pe.Else():
                pe.wait_ge(s["gate_mul"], 16)
                pe.wait_ge(s["back_lo"], 1)
                pe.wait_ge(s["comb_set"], 2)
                for e in range(E):
                    if e >= 2:
                        pe.wait_ge(s["cb_ev"], 2 * (e - 1))
                    for t in range(TT):
                        w = mm(ps[:, 2 * (e % 2) + t // 4, (t % 4) * P:(t % 4 + 1) * P],
                               pat(comb, t * 8 + e, [0, P]), ident, start=True, stop=True)
                    w.then_inc(s["cb_mm"], 1)
                pe.wait_ge(s["cb_ev"], 2 * E)
                with pe.Fori(1, NX) as e:
                    dense_expert(e)
                for i in range(4):
                    mm(bank(4 + i, P), zero[:], ident, start=False, stop=True).then_inc(s["moe_mm"], 1)
            norm(2)
            keep_clock(8)

            def last(w, k, m):
                return slice((w * KD + k) * D + m * P, (w * KD + k) * D + (m + 1) * P)

            pe.wait_ge(s["l1_lo"], 5)
            for i, (m, c) in enumerate(MC):
                pe.wait_ge(s["ln_lo"], 5 + c)
                for w_i, b in ((0, 4 + i), (1, i)):
                    for k in range(KD):
                        x_ = slice(k * NT + c * NC, k * NT + (c + 1) * NC)
                        w = three(bank(b, NC), l1_h[:, last(w_i, k, m)], l1_l[:, last(w_i, k, m)],
                                  xh[:, x_], xl[:, x_], k == 0, k == KD - 1)
                    w.then_inc(s["ra_mm"], 1)
            norm(3)
            keep_clock(26)
            for c in range(C):
                for w_i, a_h, a_l in ((3, xk_h, xk_l), (2, xh, xl)):
                    pe.wait_ge(s["mix_lo"] if w_i == 3 else s["mixr_lo"], c + 1)
                    for m in range(KD):
                        b = KD * c + m + (4 if w_i == 2 else 0)
                        for k in range(KD):
                            x_ = slice(k * N + c * NC, k * N + (c + 1) * NC)
                            w = three(bank(b, NC), l1_h[:, last(w_i, k, m)], l1_l[:, last(w_i, k, m)],
                                      a_h[:, x_], a_l[:, x_], k == 0, k == KD - 1)
                        w.then_inc(s["rk_mm"], 1)
            for i, (m, c) in enumerate(MC):
                pe.wait_ge(s["r_sig"], i + 1)
                pe.wait_ge(s["k_lo"], c + 1)
                for k in range(KD):
                    x_ = slice(k * N + c * NC, k * N + (c + 1) * NC)
                    w = three(bank(4 + i, NC), l1_h[:, last(4, k, m)], l1_l[:, last(4, k, m)],
                              xk_h[:, x_], xk_l[:, x_], k == 0, k == KD - 1)
                w.then_inc(s["vv_mm"], 1)


def bucket_onehot():
    rp = 36 - np.arange(100)
    half, exact = BUCKETS // 2, BUCKETS // 4
    a = np.abs(rp)
    far = exact + (np.log(np.maximum(a, 1).astype(np.float32) / np.float32(exact))
                   / np.float32(math.log(128 / exact)) * np.float32(half - exact)).astype(np.int32)
    bucket = (rp > 0) * half + np.where(a < exact, a, np.minimum(far, half - 1))
    oh = np.zeros((P, 100), np.float32)
    for j in range(73):
        oh[bucket[j], j] = 1.0
    return oh


def routing_constants():
    p, f = np.arange(P), np.float32
    return np.concatenate([
        np.tile(np.arange(SLOTS), (P, 1)).astype(f),
        (p[:, None] + P * np.arange(ST)[None, :]).astype(f),
        (p[:, None] < p[None, :]).astype(f),
        np.ones((P, P), f),
        (p[:, None] + P * np.arange(TT)[None, :] < N).astype(f)], axis=1)


def kernel(**inputs):
    import concourse.bacc as bacc
    from concourse.bass_utils import run_bass_kernel_spmd

    x = {k: np.asarray(v) for k, v in inputs.items()}

    def tiles(a):
        return np.ascontiguousarray(a.reshape(-1, P, a.shape[-1]).transpose(1, 0, 2).reshape(P, -1))

    im = x["x"].reshape(B, 3, GRID, PATCH, GRID, PATCH).transpose(1, 3, 5, 0, 2, 4).reshape(FP, B * NP)
    cols = np.concatenate([x["L0_tok_position_embeddings"][0].T, x["L0_tok_class_token"][0].T], axis=1)
    per = [tiles(cols[:, :T]), tiles(cols[:, T:])]
    for n in ("L0_tok_b_lin", "L1_attn_b_delta", "L1_attn_b_value", "L1_ffn_mu_r", "L1_ffn_mu_k"):
        per.append(tiles(x[n][:, None]))
    per.append(tiles(x["L0_ffn_router_w"].T))
    tri = np.tile((np.arange(E)[None, :] < np.arange(E)[:, None]).astype(np.float32).reshape(1, -1), (P, 1))
    last = [tiles(x[n].T) for n in ("L1_attn_W_delta", "L1_attn_W_value", "L1_ffn_W_r", "L1_ffn_W_k", "L1_ffn_W_v")]
    arrays = {
        "patches": tiles(im),
        "w_lin": tiles(x["L0_tok_W_lin"].T),
        "par": np.concatenate(per, axis=1),
        "const": np.concatenate([np.eye(P, dtype=np.float32), tri, bucket_onehot()], axis=1),
        "table": x["L0_attn_rel_bias_table"],
        "w_q": x["L0_attn_w_q"], "w_k": x["L0_attn_w_k"], "w_v": x["L0_attn_w_v"], "w_o": x["L0_attn_w_o"],
        "w_gate": np.concatenate([x["L0_ffn_sw_gate"], x["L0_ffn_w_gate"]]),
        "w_up": np.concatenate([x["L0_ffn_sw_up"], x["L0_ffn_w_up"]]),
        "w_down": np.concatenate([x["L0_ffn_sw_down"], x["L0_ffn_w_down"]]),
        "w_l1": np.concatenate(last, axis=1),
        "rconst": routing_constants(),
    }
    nc = bacc.Bacc("TRN2", target_bir_lowering=False, num_devices=1)
    feed, args = {}, []
    for name, a in arrays.items():
        a = np.ascontiguousarray(a)
        feed[f"in_{name}"] = a
        args.append(nc.dram_tensor(f"in_{name}", a.shape, mybir.dt.from_np(a.dtype), kind="ExternalInput").ap())
    o = nc.dram_tensor("out_h", (D, N), F32, kind="ExternalOutput").ap()
    vit_tower(nc, *args, o)
    r = run_bass_kernel_spmd(nc, [feed], core_ids=[0])
    return np.ascontiguousarray(r.results[0]["out_h"].reshape(D, B, T).transpose(1, 2, 0))
```
